# Optimizing a Trainium2 kernel written in Bass

```python
import numpy as np
import jax
import jax.numpy as jnp

def _softmax(x, axis=-1):
    return jax.nn.softmax(x, axis=axis)

def _gelu(x):
    return jax.nn.gelu(x, approximate=True)

def _silu(x):
    return jax.nn.silu(x)

def _sigmoid(x):
    return jax.nn.sigmoid(x)

def _layernorm(x, axis=-1, eps=1e-05):
    m = jnp.mean(x, axis=axis, keepdims=True)
    v = jnp.var(x, axis=axis, keepdims=True)
    return (x - m) / jnp.sqrt(v + eps)

def _scatter_add(tgt, idx, src, axis=0):
    return tgt.at[idx].add(src)

def _segment_sum(src, seg, n):
    return jax.ops.segment_sum(src, seg, n)
kernel_name = 'mk_xattn_ffn_d2_seqx_r4_f7cc3b'

def setup_inputs(seed: int=0):
    np.random.seed(seed)
    _w = jnp.asarray

    def _rec_inputs():
        import jax
        import jax.numpy as jnp
        _rk = jax.random.key(seed)
        x = 7.22e-05 + 1 * jax.random.normal(jax.random.fold_in(_rk, 1), (4, 512, 256), jnp.float32)
        _lenS = 512 - jax.random.randint(jax.random.fold_in(_rk, 7), (4,), 0, max(1, 512 // 4) + 1, jnp.int32)
        _lenS2 = 512 - jax.random.randint(jax.random.fold_in(_rk, 8), (4,), 0, max(1, 512 // 4) + 1, jnp.int32)
        _ctx_1024P = jax.random.normal(jax.random.fold_in(_rk, 11), (4, 16, 256), jnp.float32)
        _ctx_1024c = jax.random.dirichlet(jax.random.fold_in(_rk, 511), 0.3 * jnp.ones((16,), jnp.float32), (4, 512))
        _ctx_1024t = jnp.einsum('bsk,bkd->bsd', _ctx_1024c, _ctx_1024P)
        _ctx_1024t = _ctx_1024t * jax.lax.rsqrt(jnp.mean(jnp.square(_ctx_1024t)) + 1e-12) * 0.953939
        ctx_1024 = 4.13588e-05 + 0.999923 * (_ctx_1024t + 0.3 * jax.random.normal(jax.random.fold_in(_rk, 611), (4, 512, 256), jnp.float32))
        _validS = jnp.arange(512)[None, :] < _lenS[:, None]
        _validS2 = jnp.arange(512)[None, :] < _lenS2[:, None]
        _causal = jnp.tril(jnp.ones((512, 512), dtype=bool))
        mask_1x1xSxS_fk0 = jnp.where(jnp.broadcast_to(_validS[0:1, None, None, :], (1, 1, 512, 512)), 0.0, 1.0).astype(jnp.float32)
        mask_Bx1x1xS_ff1 = jnp.where(jnp.ones((4, 1, 1, 512), dtype=bool), 1.0, 0.0).astype(jnp.float32)
        return (x, ctx_1024, mask_1x1xSxS_fk0, mask_Bx1x1xS_ff1)
    x, ctx_1024, mask_1x1xSxS_fk0, mask_Bx1x1xS_ff1 = _rec_inputs()

    def _L0_xattn_setup():
        import jax, jax.numpy as jnp
        import numpy as np
        B, S, D, H, DFF = (4, 512, 256, 16, 1024)
        DEPTH = D // H
        EPS = 1e-06

        def _ln(x, g, b):
            m = jnp.mean(x, axis=-1, keepdims=True)
            v = jnp.mean(jnp.square(x - m), axis=-1, keepdims=True)
            return (x - m) * jax.lax.rsqrt(v + EPS) * g + b

        def _mha(q_in, k_in, v_in, wq, bq, wk, bk, wv, bv, wo, bo, mask=None):
            b = q_in.shape[0]

            def heads(t):
                return t.reshape(b, -1, H, DEPTH).transpose(0, 2, 1, 3)
            q = heads(q_in @ wq + bq)
            k = heads(k_in @ wk + bk)
            v = heads(v_in @ wv + bv)
            scores = jnp.einsum('bhqd,bhkd->bhqk', q, k) / jnp.sqrt(jnp.float32(DEPTH))
            if mask is not None:
                scores = scores + mask * -1000000000.0
            attn = jax.nn.softmax(scores, axis=-1)
            out = jnp.einsum('bhqk,bhkd->bhqd', attn, v)
            out = out.transpose(0, 2, 1, 3).reshape(b, -1, D)
            return out @ wo + bo
        key = jax.random.key(seed)
        ks = jax.random.split(key, 32)

        def dense(i, fan_in, fan_out):
            w = jax.random.normal(ks[i], (fan_in, fan_out), jnp.float32) / np.sqrt(fan_in)
            return (w, jnp.zeros((fan_out,), jnp.float32))
        inp = {}
        inp['x'] = jax.random.normal(ks[0], (B, S, D), jnp.float32)
        inp['enc_output'] = jax.random.normal(ks[1], (B, S, D), jnp.float32)
        inp['attention_mask'] = jnp.tril(jnp.ones((S, S), jnp.float32))[None, None]
        inp['padding_mask'] = jnp.ones((B, 1, 1, S), jnp.float32)
        names = ['wq1', 'wk1', 'wv1', 'wo1', 'wq2', 'wk2', 'wv2', 'wo2']
        for j, n in enumerate(names):
            w, bb = dense(2 + j, D, D)
            inp[n] = w
            inp['b' + n[1:]] = bb
        inp['w_ff1'], inp['b_ff1'] = dense(10, D, DFF)
        inp['w_ff2'], inp['b_ff2'] = dense(11, DFF, D)
        for i in (1, 2, 3):
            inp[f'g{i}'] = jnp.ones((D,), jnp.float32)
            inp[f'be{i}'] = jnp.zeros((D,), jnp.float32)
        return inp
    _L0_xattn_all = _L0_xattn_setup()
    _L0_xattn_in = {k: v for k, v in _L0_xattn_all.items() if k in ('wq1', 'bq1', 'wk1', 'bk1', 'wv1', 'bv1', 'wo1', 'bo1', 'wq2', 'bq2', 'wk2', 'bk2', 'wv2', 'bv2', 'wo2', 'bo2', 'w_ff1', 'b_ff1', 'w_ff2', 'b_ff2', 'g1', 'be1', 'g2', 'be2', 'g3', 'be3')}
    del _L0_xattn_all

    def _L0_ffn_setup():
        import jax, jax.numpy as jnp
        import numpy as np
        B, S, IN, OUT = (4, 2048, 256, 256)
        EPS = 1e-06

        def _xla_quantized_matmul(x2d, weight_q, weight_scale):
            amax = jnp.max(jnp.abs(x2d), axis=-1, keepdims=True)
            x_scale = jnp.maximum(amax, EPS) / 127.0
            x_q = jnp.clip(jnp.round(x2d / x_scale), -128, 127).astype(jnp.int8)
            acc = jax.lax.dot_general(x_q, weight_q, (((1,), (1,)), ((), ())), preferred_element_type=jnp.int32)
            return acc.astype(jnp.float32) * x_scale * weight_scale[None, :]
        key = jax.random.key(seed)
        k1, k2, k3, k4 = jax.random.split(key, 4)
        x = jax.random.normal(k1, (B, S, IN), dtype=jnp.float32)
        weight_q = jax.random.randint(k2, (OUT, IN), -128, 128, dtype=jnp.int32).astype(jnp.int8)
        weight_scale = jax.random.uniform(k3, (OUT,), dtype=jnp.float32, minval=0.001, maxval=0.01)
        bias = jax.random.normal(k4, (OUT,), dtype=jnp.float32) * 0.01
        return {'x': x, 'weight_q': weight_q, 'weight_scale': weight_scale, 'bias': bias}
    _L0_ffn_all = _L0_ffn_setup()
    _L0_ffn_in = {k: v for k, v in _L0_ffn_all.items() if k in ('weight_q', 'weight_scale', 'bias')}
    del _L0_ffn_all

    def _L1_xattn_setup():
        import jax, jax.numpy as jnp
        import numpy as np
        D_MODEL = 256
        NUM_HEADS = 16
        DEPTH = D_MODEL // NUM_HEADS

        def _split_heads(x, B):
            return x.reshape(B, -1, NUM_HEADS, DEPTH).transpose(0, 2, 1, 3)
        key = jax.random.key(seed)
        ks = jax.random.split(key, 11)
        B, S = (4, 512)
        scale = 1.0 / np.sqrt(D_MODEL)
        inp = {'query': jax.random.normal(ks[0], (B, S, D_MODEL), jnp.float32), 'key': jax.random.normal(ks[1], (B, S, D_MODEL), jnp.float32), 'value': jax.random.normal(ks[2], (B, S, D_MODEL), jnp.float32), 'wq_w': jax.random.normal(ks[3], (D_MODEL, D_MODEL), jnp.float32) * scale, 'wq_b': jnp.zeros((D_MODEL,), jnp.float32), 'wk_w': jax.random.normal(ks[4], (D_MODEL, D_MODEL), jnp.float32) * scale, 'wk_b': jnp.zeros((D_MODEL,), jnp.float32), 'wv_w': jax.random.normal(ks[5], (D_MODEL, D_MODEL), jnp.float32) * scale, 'wv_b': jnp.zeros((D_MODEL,), jnp.float32), 'dense_w': jax.random.normal(ks[6], (D_MODEL, D_MODEL), jnp.float32) * scale, 'dense_b': jnp.zeros((D_MODEL,), jnp.float32)}
        return inp
    _L1_xattn_all = _L1_xattn_setup()
    _L1_xattn_in = {k: v for k, v in _L1_xattn_all.items() if k in ('wq_w', 'wq_b', 'wk_w', 'wk_b', 'wv_w', 'wv_b', 'dense_w', 'dense_b')}
    del _L1_xattn_all

    def _L1_ffn_setup():
        import jax, jax.numpy as jnp
        import numpy as np
        D_MODEL = 256
        N_EXPERTS = 16
        TOP_K = 2
        EXPERT_DIM = 256
        SHARED_DIM = 512
        B, T = (2, 256)
        key = jax.random.key(seed)
        ks = jax.random.split(key, 7)
        std = 0.02
        return {'x': jax.random.normal(ks[0], (B, T, D_MODEL), dtype=jnp.float32), 'router_w': jax.random.normal(ks[1], (N_EXPERTS, D_MODEL), dtype=jnp.float32) * std, 'gate_up_w': jax.random.normal(ks[2], (N_EXPERTS, D_MODEL, 2 * EXPERT_DIM), dtype=jnp.float32) * std, 'down_w': jax.random.normal(ks[3], (N_EXPERTS, EXPERT_DIM, D_MODEL), dtype=jnp.float32) * std, 'shared_gate_w': jax.random.normal(ks[4], (SHARED_DIM, D_MODEL), dtype=jnp.float32) * std, 'shared_up_w': jax.random.normal(ks[5], (SHARED_DIM, D_MODEL), dtype=jnp.float32) * std, 'shared_down_w': jax.random.normal(ks[6], (D_MODEL, SHARED_DIM), dtype=jnp.float32) * std}
    _L1_ffn_all = _L1_ffn_setup()
    _L1_ffn_in = {k: v for k, v in _L1_ffn_all.items() if k in ('router_w', 'gate_up_w', 'down_w', 'shared_gate_w', 'shared_up_w', 'shared_down_w')}
    del _L1_ffn_all
    return {'x': x, 'ctx_1024': ctx_1024, 'mask_1x1xSxS_fk0': mask_1x1xSxS_fk0, 'mask_Bx1x1xS_ff1': mask_Bx1x1xS_ff1, 'L0_xattn_wq1': _L0_xattn_in['wq1'], 'L0_xattn_bq1': _L0_xattn_in['bq1'], 'L0_xattn_wk1': _L0_xattn_in['wk1'], 'L0_xattn_bk1': _L0_xattn_in['bk1'], 'L0_xattn_wv1': _L0_xattn_in['wv1'], 'L0_xattn_bv1': _L0_xattn_in['bv1'], 'L0_xattn_wo1': _L0_xattn_in['wo1'], 'L0_xattn_bo1': _L0_xattn_in['bo1'], 'L0_xattn_wq2': _L0_xattn_in['wq2'], 'L0_xattn_bq2': _L0_xattn_in['bq2'], 'L0_xattn_wk2': _L0_xattn_in['wk2'], 'L0_xattn_bk2': _L0_xattn_in['bk2'], 'L0_xattn_wv2': _L0_xattn_in['wv2'], 'L0_xattn_bv2': _L0_xattn_in['bv2'], 'L0_xattn_wo2': _L0_xattn_in['wo2'], 'L0_xattn_bo2': _L0_xattn_in['bo2'], 'L0_xattn_w_ff1': _L0_xattn_in['w_ff1'], 'L0_xattn_b_ff1': _L0_xattn_in['b_ff1'], 'L0_xattn_w_ff2': _L0_xattn_in['w_ff2'], 'L0_xattn_b_ff2': _L0_xattn_in['b_ff2'], 'L0_xattn_g1': _L0_xattn_in['g1'], 'L0_xattn_be1': _L0_xattn_in['be1'], 'L0_xattn_g2': _L0_xattn_in['g2'], 'L0_xattn_be2': _L0_xattn_in['be2'], 'L0_xattn_g3': _L0_xattn_in['g3'], 'L0_xattn_be3': _L0_xattn_in['be3'], 'L0_ffn_weight_q': _L0_ffn_in['weight_q'], 'L0_ffn_weight_scale': _L0_ffn_in['weight_scale'], 'L0_ffn_bias': _L0_ffn_in['bias'], 'L1_xattn_wq_w': _L1_xattn_in['wq_w'], 'L1_xattn_wq_b': _L1_xattn_in['wq_b'], 'L1_xattn_wk_w': _L1_xattn_in['wk_w'], 'L1_xattn_wk_b': _L1_xattn_in['wk_b'], 'L1_xattn_wv_w': _L1_xattn_in['wv_w'], 'L1_xattn_wv_b': _L1_xattn_in['wv_b'], 'L1_xattn_dense_w': _L1_xattn_in['dense_w'], 'L1_xattn_dense_b': _L1_xattn_in['dense_b'], 'L1_ffn_router_w': _L1_ffn_in['router_w'], 'L1_ffn_gate_up_w': _L1_ffn_in['gate_up_w'], 'L1_ffn_down_w': _L1_ffn_in['down_w'], 'L1_ffn_shared_gate_w': _L1_ffn_in['shared_gate_w'], 'L1_ffn_shared_up_w': _L1_ffn_in['shared_up_w'], 'L1_ffn_shared_down_w': _L1_ffn_in['shared_down_w']}

def reference(x, ctx_1024, mask_1x1xSxS_fk0, mask_Bx1x1xS_ff1, L0_xattn_wq1, L0_xattn_bq1, L0_xattn_wk1, L0_xattn_bk1, L0_xattn_wv1, L0_xattn_bv1, L0_xattn_wo1, L0_xattn_bo1, L0_xattn_wq2, L0_xattn_bq2, L0_xattn_wk2, L0_xattn_bk2, L0_xattn_wv2, L0_xattn_bv2, L0_xattn_wo2, L0_xattn_bo2, L0_xattn_w_ff1, L0_xattn_b_ff1, L0_xattn_w_ff2, L0_xattn_b_ff2, L0_xattn_g1, L0_xattn_be1, L0_xattn_g2, L0_xattn_be2, L0_xattn_g3, L0_xattn_be3, L0_ffn_weight_q, L0_ffn_weight_scale, L0_ffn_bias, L1_xattn_wq_w, L1_xattn_wq_b, L1_xattn_wk_w, L1_xattn_wk_b, L1_xattn_wv_w, L1_xattn_wv_b, L1_xattn_dense_w, L1_xattn_dense_b, L1_ffn_router_w, L1_ffn_gate_up_w, L1_ffn_down_w, L1_ffn_shared_gate_w, L1_ffn_shared_up_w, L1_ffn_shared_down_w):
    import jax
    import jax.numpy as jnp

    def _L0_xattn_ref(x, enc_output, attention_mask, padding_mask, wq1, bq1, wk1, bk1, wv1, bv1, wo1, bo1, wq2, bq2, wk2, bk2, wv2, bv2, wo2, bo2, w_ff1, b_ff1, w_ff2, b_ff2, g1, be1, g2, be2, g3, be3):
        import jax, jax.numpy as jnp
        import numpy as np
        B, S, D, H, DFF = (4, 512, 256, 16, 1024)
        DEPTH = D // H
        EPS = 1e-06

        def _ln(x, g, b):
            m = jnp.mean(x, axis=-1, keepdims=True)
            v = jnp.mean(jnp.square(x - m), axis=-1, keepdims=True)
            return (x - m) * jax.lax.rsqrt(v + EPS) * g + b

        def _mha(q_in, k_in, v_in, wq, bq, wk, bk, wv, bv, wo, bo, mask=None):
            b = q_in.shape[0]

            def heads(t):
                return t.reshape(b, -1, H, DEPTH).transpose(0, 2, 1, 3)
            q = heads(q_in @ wq + bq)
            k = heads(k_in @ wk + bk)
            v = heads(v_in @ wv + bv)
            scores = jnp.einsum('bhqd,bhkd->bhqk', q, k) / jnp.sqrt(jnp.float32(DEPTH))
            if mask is not None:
                scores = scores + mask * -1000000000.0
            attn = jax.nn.softmax(scores, axis=-1)
            out = jnp.einsum('bhqk,bhkd->bhqd', attn, v)
            out = out.transpose(0, 2, 1, 3).reshape(b, -1, D)
            return out @ wo + bo
        inv_mask = 1.0 - attention_mask * padding_mask
        attn_out = _mha(x, x, x, wq1, bq1, wk1, bk1, wv1, bv1, wo1, bo1, inv_mask)
        h1 = _ln(x + attn_out, g1, be1)
        cross = _mha(h1, enc_output, enc_output, wq2, bq2, wk2, bk2, wv2, bv2, wo2, bo2, None)
        h2 = _ln(h1 + cross, g2, be2)
        ff = jax.nn.relu(h2 @ w_ff1 + b_ff1) @ w_ff2 + b_ff2
        return _ln(h2 + ff, g3, be3)

    def _L0_ffn_ref(x, weight_q, weight_scale, bias):
        import jax, jax.numpy as jnp
        import numpy as np
        B, S, IN, OUT = (4, 2048, 256, 256)
        EPS = 1e-06

        def _xla_quantized_matmul(x2d, weight_q, weight_scale):
            amax = jnp.max(jnp.abs(x2d), axis=-1, keepdims=True)
            x_scale = jnp.maximum(amax, EPS) / 127.0
            x_q = jnp.clip(jnp.round(x2d / x_scale), -128, 127).astype(jnp.int8)
            acc = jax.lax.dot_general(x_q, weight_q, (((1,), (1,)), ((), ())), preferred_element_type=jnp.int32)
            return acc.astype(jnp.float32) * x_scale * weight_scale[None, :]
        orig_shape = x.shape
        x2d = x.reshape(-1, orig_shape[-1])
        out = _xla_quantized_matmul(x2d, weight_q, weight_scale)
        out = out.reshape(*orig_shape[:-1], out.shape[-1])
        out = out + bias
        return out

    def _L1_xattn_ref(query, key, value, wq_w, wq_b, wk_w, wk_b, wv_w, wv_b, dense_w, dense_b):
        import jax, jax.numpy as jnp
        import numpy as np
        D_MODEL = 256
        NUM_HEADS = 16
        DEPTH = D_MODEL // NUM_HEADS

        def _split_heads(x, B):
            return x.reshape(B, -1, NUM_HEADS, DEPTH).transpose(0, 2, 1, 3)
        B = query.shape[0]
        q = _split_heads(query @ wq_w.T + wq_b, B)
        k = _split_heads(key @ wk_w.T + wk_b, B)
        v = _split_heads(value @ wv_w.T + wv_b, B)
        scores = jnp.einsum('bhqd,bhkd->bhqk', q, k) / jnp.sqrt(jnp.float32(DEPTH)).astype(q.dtype)
        attn = jax.nn.softmax(scores, axis=-1)
        out = jnp.einsum('bhqk,bhkd->bhqd', attn, v)
        out = out.transpose(0, 2, 1, 3).reshape(B, -1, D_MODEL)
        return out @ dense_w.T + dense_b

    def _L1_ffn_ref(x, router_w, gate_up_w, down_w, shared_gate_w, shared_up_w, shared_down_w):
        import jax, jax.numpy as jnp
        import numpy as np
        D_MODEL = 256
        N_EXPERTS = 16
        TOP_K = 2
        EXPERT_DIM = 256
        SHARED_DIM = 512
        B, T = (2, 256)
        Bb, Tt, C = x.shape
        N = Bb * Tt
        E = gate_up_w.shape[0]
        logits = jnp.einsum('btc,ec->bte', x, router_w)
        top_vals, top_idx = jax.lax.top_k(logits, TOP_K)
        gates = jax.nn.sigmoid(top_vals)
        xf = x.reshape(N, C)
        sel = top_idx.reshape(N, TOP_K)
        gw = gates.reshape(N, TOP_K)
        w_full = jnp.zeros((N, E), dtype=x.dtype).at[jnp.arange(N)[:, None], sel].add(gw)
        gu = jnp.einsum('nc,ech->neh', xf, gate_up_w)
        gate, up = jnp.split(gu, 2, axis=-1)
        h = jax.nn.silu(gate) * up
        out_all = jnp.einsum('neh,ehc->nec', h, down_w)
        moe = jnp.einsum('ne,nec->nc', w_full, out_all).reshape(Bb, Tt, C)
        sg = jnp.einsum('btc,sc->bts', x, shared_gate_w)
        su = jnp.einsum('btc,sc->bts', x, shared_up_w)
        shared = jnp.einsum('bts,cs->btc', jax.nn.silu(sg) * su, shared_down_w)
        return moe + shared
    x = x + _L0_xattn_ref(_layernorm(x, axis=-1), ctx_1024, mask_1x1xSxS_fk0, mask_Bx1x1xS_ff1, L0_xattn_wq1, L0_xattn_bq1, L0_xattn_wk1, L0_xattn_bk1, L0_xattn_wv1, L0_xattn_bv1, L0_xattn_wo1, L0_xattn_bo1, L0_xattn_wq2, L0_xattn_bq2, L0_xattn_wk2, L0_xattn_bk2, L0_xattn_wv2, L0_xattn_bv2, L0_xattn_wo2, L0_xattn_bo2, L0_xattn_w_ff1, L0_xattn_b_ff1, L0_xattn_w_ff2, L0_xattn_b_ff2, L0_xattn_g1, L0_xattn_be1, L0_xattn_g2, L0_xattn_be2, L0_xattn_g3, L0_xattn_be3)
    x = x + _L0_ffn_ref(_layernorm(x, axis=-1), L0_ffn_weight_q, L0_ffn_weight_scale, L0_ffn_bias)
    x = x + _L1_xattn_ref(_layernorm(x, axis=-1), ctx_1024, ctx_1024, L1_xattn_wq_w, L1_xattn_wq_b, L1_xattn_wk_w, L1_xattn_wk_b, L1_xattn_wv_w, L1_xattn_wv_b, L1_xattn_dense_w, L1_xattn_dense_b)
    x = x + _L1_ffn_ref(_layernorm(x, axis=-1), L1_ffn_router_w, L1_ffn_gate_up_w, L1_ffn_down_w, L1_ffn_shared_gate_w, L1_ffn_shared_up_w, L1_ffn_shared_down_w)
    return x

_drawn_inputs = setup_inputs


def setup_inputs(seed=0):
    import zlib

    import numpy as np

    out = dict(_drawn_inputs(seed))
    spreads = {'L0_xattn_bq1': (0.0, 0.653),
     'L0_xattn_bk1': (0.0, 0.8),
     'L0_xattn_bv1': (0.0, 0.1),
     'L0_xattn_bo1': (0.0, 0.1),
     'L0_xattn_bq2': (0.0, 0.54),
     'L0_xattn_bk2': (0.0, 0.8),
     'L0_xattn_bv2': (0.0, 0.1),
     'L0_xattn_bo2': (0.0, 0.1),
     'L0_xattn_b_ff1': (0.0, 0.1),
     'L0_xattn_b_ff2': (0.0, 0.1),
     'L0_xattn_g1': (1.0, 0.2),
     'L0_xattn_be1': (0.0, 0.1),
     'L0_xattn_g2': (1.0, 0.2),
     'L0_xattn_be2': (0.0, 0.1),
     'L0_xattn_g3': (1.0, 0.2),
     'L0_xattn_be3': (0.0, 0.1),
     'L1_xattn_wq_b': (0.0, 0.8),
     'L1_xattn_wk_b': (0.0, 0.8),
     'L1_xattn_wv_b': (0.0, 0.683),
     'L1_xattn_dense_b': (0.0, 0.612)}
    factors = {'L0_ffn_bias': 8.0,
     'L1_ffn_router_w': 8.0,
     'L1_ffn_gate_up_w': 8.0,
     'L1_ffn_down_w': 8.0,
     'L1_ffn_shared_gate_w': 8.0,
     'L1_ffn_shared_up_w': 8.0,
     'L1_ffn_shared_down_w': 8.0}
    for name, (base, spread) in spreads.items():
        noise = np.random.default_rng([zlib.crc32(name.encode()), seed]).standard_normal(out[name].shape)
        drawn = base * np.exp(spread * noise) if base else spread * noise
        out[name] = jnp.asarray(drawn.astype(out[name].dtype))
    for name, factor in factors.items():
        out[name] = (out[name] * factor).astype(out[name].dtype)
    return out
```

```python
from contextlib import ExitStack

import concourse.bass as bass
from concourse import mybir

ALU = mybir.AluOpType
ACT = mybir.ActivationFunctionType
AX = mybir.AxisListType
F32 = mybir.dt.float32
BF16 = mybir.dt.bfloat16
I8 = mybir.dt.int8
I32 = mybir.dt.int32
U32 = mybir.dt.uint32

B, S, D, H = 4, 512, 256, 16
DEPTH = D // H
P = 128
QT = S // P
KD = D // P
DFF = 1024
FT = DFF // P
NE, EH = 16, 256
SH = 512
HG = 4
NG = H // HG
PAIRS_Q = (0, 0, 1, 1, 0, 2)
PAIRS_K = (0, 1, 0, 1, 2, 0)
STACK = DEPTH * len(PAIRS_Q)
ROWS = STACK + 3
ATT = 3
LEAD = 6
UNITS = NG * QT
MAGIC = 1.5 * 2.0 ** 23
NEG = -1.0e9
CAST = 1.0 / DEPTH ** 0.5


def misc_jobs():
    jobs = []

    def job(*name, by):
        jobs.append((name, by))

    def turned(n):
        for kd in range(KD):
            job("turn", n, kd, by="act")

    def project(a, what):
        if what == "v":
            for half in range(2):
                job("v", a, half, by="dve")
        else:
            for m in range(KD):
                job(what, a, m, by="act")

    def attention(a):
        for u in range(-LEAD, UNITS + 2):
            g = max_group(u)
            if g is not None:
                job("max", a, g, by="dve")
            g = out_group(u)
            if g is not None:
                job("oT", a, g, by="dve")
        for kd in range(KD):
            job("attT", a, kd, by="act")
        for half in range(2):
            job("out", a, half, by="dve")

    turned(0)
    for what in "qkv":
        project(0, what)
    attention(0)
    for a in (1, 2):
        for what in "kv":
            project(a, what)
        if a == 2:
            break
        turned(1)
        project(1, "q")
        attention(1)
        turned(2)
        for f in range(FT):
            job("ff1", f, by="act")
        for half in range(2):
            job("ff2", half, by="dve")
        job("i8T", by="dve")
        for half in range(2):
            job("i8", half, by="dve")
    turned(5)
    project(2, "q")
    attention(2)
    turned(6)
    job("logits", by="dve")
    return jobs


def max_group(u):
    v = u + LEAD - 1
    return v // QT if v >= 0 and v % QT == QT - 1 and v < UNITS else None


def out_group(u):
    v = u - 2
    return v // QT if v >= 0 and v % QT == QT - 1 and v < UNITS else None


def build(nc, x, ctxT, am, amT, pmrow, pmcol, wqkv, wo, bqk, brow, bff1, wff1, wff2, wi8,
          routerT, gate_up, down, sgT, suT, sdT, out):
    JOBS = misc_jobs()
    JOB = {name: n for n, (name, _) in enumerate(JOBS)}
    nth, counts = [], {"act": 0, "dve": 0}
    for _, by in JOBS:
        counts[by] += 1
        nth.append(counts[by])

    x_scr = nc.dram_tensor("x_scr", [B, S, D], F32, kind="Internal").ap()
    tT_scr = nc.dram_tensor("tT_scr", [B, D, S], F32, kind="Internal").ap()
    w_scr = nc.dram_tensor("w_scr", [B, P, QT * NE], F32, kind="Internal").ap()
    parts_scr = nc.dram_tensor("parts_scr", [ATT, 2, 3, D, S], BF16, kind="Internal").ap()

    with ExitStack() as phase:
        def sb(name, shape, dt):
            return phase.enter_context(nc.sbuf_tensor(name, shape, dt))

        def sem(name):
            s = phase.enter_context(nc.semaphore(name))
            every.append(s)
            return s

        every = []
        identf = sb("identf", [P, P], F32)
        identb = sb("identb", [P, P], BF16)
        w_qkv = sb("w_qkv", [P, ATT, 3, KD, D], F32)
        w_o = sb("w_o", [P, ATT, KD, D], F32)
        w_ff1 = sb("w_ff1", [P, KD, DFF], F32)
        w_ff2 = sb("w_ff2", [P, FT, D], F32)
        w_i8 = sb("w_i8", [P, KD, D // 4], I32)
        w_i8b = sb("w_i8b", [P, KD, D], BF16)
        w_router = sb("w_router", [P, KD, NE], F32)
        b_qk = sb("b_qk", [P, ATT, 2, KD], F32)
        b_q4 = sb("b_q4", [P, ATT, KD], F32)
        b_ff1 = sb("b_ff1", [P, FT], F32)
        NROW = 15
        b_row = sb("b_row", [P, NROW, D], F32)
        BV, BO, BFF2, GAIN, BETA, I8S, I8B = 0, 3, 6, 7, 10, 13, 14
        minus_half = sb("minus_half", [P, QT], F32)
        iota_e = sb("iota_e", [P, NE], F32)
        am_n = sb("am_n", [P, QT, S], F32)
        am_t = sb("am_t", [P, QT, S], F32)
        X = sb("X", [P, QT, D], F32)
        Hn = sb("Hn", [P, QT, D], F32)
        HB = sb("HB", [P, QT, D], F32)
        T1 = sb("T1", [P, QT, D], F32)
        hT = sb("hT", [P, KD, S], F32)
        cT = sb("cT", [P, KD, S], F32)
        pm_row = sb("pm_row", [P, S], F32)
        pm_col = sb("pm_col", [P, QT], F32)
        mb_n = sb("mb_n", [P, QT, S], F32)
        mb_t = sb("mb_t", [P, QT, S], F32)
        QS = sb("QS", [P, H, S], BF16)
        KS = sb("KS", [P, H, S], BF16)
        V = sb("V", [P, QT, H, 32], F32)
        NP_ = 2
        prob = sb("prob", [P, NP_, HG, S], F32)
        ff_h = prob[:, :, :, :].rearrange("p a b c -> p (a b) c")
        qf = sb("qf", [P, 2, S], F32)
        rest = sb("rest", [P, S], F32)
        parts = sb("parts", [P, 2, 3, S], BF16)
        Mx = sb("Mx", [P, 2, HG, QT], F32)
        neg = sb("neg", [HG * QT, P], F32)
        MR = sb("MR", [HG * QT, 2, 3, P], BF16)
        oT = sb("oT", [P, 2, S], F32)
        rsum = sb("rsum", [P, 2, QT, HG], F32)
        stats = sb("stats", [P, QT, 6], F32)
        mv = sb("mv", [P, QT, 2], F32)
        ve = sb("ve", [P, QT], F32)
        rstd = sb("rstd", [P, QT], F32)
        amax = sb("amax", [P, QT], F32)
        xscale = sb("xscale", [P, QT], F32)
        xrec = sb("xrec", [P, QT], F32)
        xq = sb("xq", [P, QT, D], BF16)
        xqT = sb("xqT", [P, KD, S], BF16)
        lg = sb("lg", [P, QT, NE], F32)
        top = sb("top", [P, QT, 8], F32)
        topi = sb("topi", [P, QT, 8], U32)
        topf = sb("topf", [P, QT, 2], F32)
        gate_e = sb("gate_e", [P, QT, 2], F32)
        gate = sb("gate", [P, QT, 2], F32)
        wsel = sb("wsel", [P, QT, 2, NE], F32)
        wfull = sb("wfull", [P, QT, NE], F32)

        bank = [phase.enter_context(nc.psum_tensor(f"bank{i}", [P, 512], F32)) for i in range(8)]
        bankS, bankT, bankO, bankM = bank[0:2], bank[2:5], bank[5], bank[6:8]

        weights_in = sem("weights_in")
        consts_ready = sem("consts_ready")

        with nc.Block() as block:
            @block.sync
            def _(sp):
                n = 0
                for dst, src in ((w_qkv[:, :, :, :, :].rearrange("p a w k n -> p (a w k) n"), wqkv),
                                 (w_o[:, :, :, :].rearrange("p a k n -> p (a k) n"), wo),
                                 (b_qk[:, :, :, :].rearrange("p a w k -> p (a w k)"), bqk),
                                 (b_ff1[:, :], bff1),
                                 (w_ff1[:, :, :], wff1.rearrange("(k p) n -> p k n", p=P)),
                                 (w_ff2[:, :, :], wff2.rearrange("(k p) n -> p k n", p=P)),
                                 (w_i8[:, :, :], wi8.rearrange("(k p) n -> p k n", p=P)),
                                 (w_router[:, :, :], routerT.rearrange("(k p) n -> p k n", p=P)),
                                 (am_n[:, :, :], am.rearrange("(t p) k -> p t k", p=P)),
                                 (am_t[:, :, :], amT.rearrange("(t p) k -> p t k", p=P)),
                                 (b_row[:, :, :].rearrange("p r n -> p (r n)"),
                                  brow.rearrange("r n -> (r n)").partition_broadcast(P))):
                    sp.dma_start(dst, src).then_inc(weights_in, 16)
                    n += 16
                sp.wait_ge(weights_in, n)

            @block.gpsimd
            def _(pool):
                pool.memset(identf[:, :], 0.0).then_inc(consts_ready, 1)
                pool.memset(identb[:, :], 0.0).then_inc(consts_ready, 1)
                pool.wait_ge(consts_ready, 2)
                for n, m in enumerate((identf, identb)):
                    pool.affine_select(out=m[:, :], in_=m[:, :], compare_op=ALU.not_equal, fill=1.0, base=0,
                                       pattern=[[-1, P]], channel_multiplier=1)
                pool.iota(iota_e[:, :], [[1, NE]], base=0, channel_multiplier=0,
                          allow_small_or_imprecise_dtypes=True)
                pool.memset(minus_half[:, :], -0.5)

            @block.vector
            def _(dve):
                dve.memset(V[:, :, :, :], 1.0)
                dve.memset(KS[STACK:ROWS, :, :], 1.0)
                dve.wait_ge(weights_in, 176)
                dve.tensor_copy(w_i8b[:, :, :], w_i8[:, :, :].bitcast(I8))
                dve.tensor_scalar(b_q4[:, :, :], b_qk[:, :, 0, :], CAST, None, ALU.mult)

        row_in = sem("row_in")
        ctx_in = sem("ctx_in")
        mask_ready = sem("mask_ready")
        m_full = sem("m_full")
        m_act = sem("m_act")
        m_dve = sem("m_dve")
        s_full = sem("s_full")
        s_read = sem("s_read")
        t_full = sem("t_full")
        t_masked = sem("t_masked")
        exp_done = sem("exp_done")
        av_done = sem("av_done")
        o_read = sem("o_read")
        hn_ready = sem("hn_ready")
        hb_ready = sem("hb_ready")
        ve_ready = sem("ve_ready")
        rstd_ready = sem("rstd_ready")
        part_ready = sem("part_ready")
        part_out = [sem(f"part_out{i}") for i in range(2)]
        stack_in = [sem(f"stack_in{i}") for i in range(2)]
        mr_ready = sem("mr_ready")
        rows_in = [sem(f"rows_in{i}") for i in range(2)]
        t1_ready = sem("t1_ready")
        chain = sem("chain")
        pchain = sem("pchain")
        gate_sem = sem("gate_sem")
        row_out = sem("row_out")

        PARTS = [(0, 0, 0), (0, 0, 1), (0, 1, 0), (0, 1, 1)]
        for a in (1, 2):
            PARTS += [(a, 1, 0), (a, 1, 1), (a, 0, 0), (a, 0, 1)]
        PART = {p: n for n, p in enumerate(PARTS)}
        LN_HB = {0: BO + 0, 1: BO + 1, 2: BFF2}

        def read_done(eng, name):
            n = JOB[name]
            eng.wait_ge(m_act if JOBS[n][1] == "act" else m_dve, nth[n])

        with nc.Fori(0, B) as row:
            with nc.Block() as block:
                @block.sync
                def _(sp):
                    sp.dma_start(X[:, :, :], x[row].rearrange("(t p) n -> p t n", p=P)).then_inc(row_in, 16)
                    sp.dma_start(pm_row[:, :], pmrow[row].partition_broadcast(P)).then_inc(ctx_in, 16)
                    sp.dma_start(pm_col[:, :], pmcol[row]).then_inc(ctx_in, 16)
                    sp.dma_start(cT[:, :, :], ctxT[row].rearrange("(k p) n -> p k n", p=P)).then_inc(ctx_in, 16)

                    def stack(a, t):
                        for m in range(KD):
                            n = PART[(a, t, m)]
                            sp.wait_ge(part_ready, n + 1)
                            sp.dma_start(parts_scr[a, t].rearrange("j (m p) s -> m p j s", p=P)[m],
                                         parts[:, n % 2, :, :]).then_inc(part_out[n % 2], 16)
                        if a:
                            sp.wait_ge(av_done, a * UNITS)
                        for m in range(KD):
                            n = PART[(a, t, m)]
                            sp.wait_ge(part_out[n % 2], 16 * (n // 2 + 1))
                            dst = (QS, KS)[t]
                            for r, j in enumerate((PAIRS_Q, PAIRS_K)[t]):
                                src = parts_scr[a, t, j].rearrange("(h d) s -> d h s", d=DEPTH)
                                sp.dma_start(dst[DEPTH * r:DEPTH * (r + 1), m * 8:m * 8 + 8, :],
                                             src[:, m * 8:m * 8 + 8, :]).then_inc(stack_in[t], 16)

                    for a in range(ATT):
                        for t in ((0, 1) if a == 0 else (1, 0)):
                            stack(a, t)
                        for g in range(NG):
                            n = a * NG + g
                            sp.wait_ge(mr_ready, n + 1)
                            for j in range(3):
                                dst = QS[STACK + j:STACK + j + 1, g * HG:(g + 1) * HG, :]
                                sp.dma_start(dst.rearrange("o h (t q) -> o (h t) q", q=P),
                                             MR[:, n % 2, j, :]).then_inc(rows_in[n % 2], 16)
                    sp.wait_ge(hn_ready, 7)
                    sp.dma_start(x_scr[row].rearrange("(t p) n -> p t n", p=P), X[:, :, :]).then_inc(row_out, 16)
                    read_done(sp, ("turn", 6, 1))
                    read_done(sp, ("turn", 6, 0))
                    sp.dma_start(tT_scr[row].rearrange("(k p) n -> p k n", p=P), hT[:, :, :]).then_inc(row_out, 16)
                    sp.wait_ge(t1_ready, 4)
                    sp.dma_start(w_scr[row], wfull[:, :, :].rearrange("p t e -> p (t e)")).then_inc(row_out, 16)
                    sp.wait_ge(row_out, 48)

                @block.gpsimd
                def _(pool):
                    links = [0]

                    def link(ins):
                        links[0] += 1
                        ins.then_inc(pchain, 1)
                        pool.wait_ge(pchain, links[0])

                    def root(n):
                        pool.wait_ge(ve_ready, n + 1)
                        pool.tensor_tensor(rstd[:, :], ve[:, :], minus_half[:, :], ALU.pow).then_inc(rstd_ready, 1)

                    def residual(n, src, row_of):
                        pool.wait_ge(hn_ready, n + 1)
                        pool.tensor_tensor(HB[:, :, :], src[:, :, :],
                                           b_row[:, row_of, :].unsqueeze(1).broadcast_to([P, QT, D]),
                                           ALU.add).then_inc(hb_ready, 1)

                    root(0)
                    pool.wait_ge(ctx_in, 48)
                    link(pool.tensor_tensor(mb_n[:, :, :], am_n[:, :, :],
                                            pm_row[:, :].unsqueeze(1).broadcast_to([P, QT, S]), ALU.mult))
                    link(pool.tensor_scalar(mb_n[:, :, :], mb_n[:, :, :], -1.0, 1.0, ALU.mult, ALU.add))
                    pool.tensor_scalar(mb_n[:, :, :], mb_n[:, :, :], NEG, None, ALU.mult).then_inc(mask_ready, 1)
                    for kt in range(QT):
                        link(pool.tensor_scalar(mb_t[:, kt, :], am_t[:, kt, :], pm_col[:, kt:kt + 1], None, ALU.mult))
                    link(pool.tensor_scalar(mb_t[:, :, :], mb_t[:, :, :], -1.0, 1.0, ALU.mult, ALU.add))
                    pool.tensor_scalar(mb_t[:, :, :], mb_t[:, :, :], NEG, None, ALU.mult).then_inc(mask_ready, 1)
                    residual(0, Hn, BO)
                    root(1)
                    residual(1, Hn, BO + 1)
                    root(2)
                    residual(2, Hn, BFF2)
                    root(3)
                    residual(3, X, I8B)
                    root(4)
                    root(5)
                    residual(5, X, BO + 2)
                    root(6)

                @block.scalar
                def _(act):
                    def read(name, dst, func=ACT.Identity, **kw):
                        n = JOB[name]
                        act.wait_ge(m_full, n + 1)
                        act.activation(dst, bankM[n % 2][:, :], func, **kw).then_inc(m_act, 1)

                    def turn(n):
                        for kd in range(KD):
                            read(("turn", n, kd), hT[:, kd, :])

                    def project(a, t):
                        for m in range(KD):
                            n = PART[(a, t, m)]
                            if n >= 2:
                                act.wait_ge(part_ready, n - 1)
                            if t == 0:
                                read(("q", a, m), qf[:, n % 2, :], bias=b_q4[:, a, m:m + 1], scale=CAST)
                            else:
                                read(("k", a, m), qf[:, n % 2, :], bias=b_qk[:, a, 1, m:m + 1])

                    def attention(a):
                        for u in range(UNITS + 1):
                            if u < UNITS:
                                U = a * UNITS + u
                                if a and U >= NP_:
                                    act.wait_ge(av_done, U - NP_ + 1)
                                for j in range(HG):
                                    e = U * HG + j
                                    if a == 0:
                                        act.wait_ge(t_masked, e + 1)
                                        src = prob[:, U % NP_, j, :]
                                    else:
                                        act.wait_ge(t_full, e + 1)
                                        src = bankT[e % 3][:, :]
                                    act.activation(prob[:, U % NP_, j, :], src, ACT.Exp).then_inc(exp_done, 1)
                            if u % QT == 0 and u:
                                g = a * NG + u // QT - 1
                                act.wait_ge(av_done, a * UNITS + u)
                                if g >= 2:
                                    act.wait_ge(m_full, JOB[("oT", (g - 2) // NG, (g - 2) % NG)] + 1)
                                act.activation(oT[:, g % 2, :], bankO[:, :], ACT.Copy).then_inc(o_read, 1)
                        for kd in range(KD):
                            read(("attT", a, kd), hT[:, kd, :])

                    turn(0)
                    project(0, 0)
                    project(0, 1)
                    attention(0)
                    project(1, 1)
                    turn(1)
                    project(1, 0)
                    attention(1)
                    turn(2)
                    for f in range(FT):
                        read(("ff1", f), ff_h[:, f, :], ACT.Relu, bias=b_ff1[:, f:f + 1])
                    project(2, 1)
                    turn(5)
                    project(2, 0)
                    attention(2)
                    turn(6)
                    act.wait_ge(t1_ready, 3)
                    act.activation(gate_e[:, :, :], top[:, :, 0:2], ACT.Exp, scale=-1.0).then_inc(gate_sem, 1)

                @block.tensor
                def _(pe):
                    def bank_free(n):
                        if n >= 2:
                            read_done(pe, JOBS[n - 2][0])
                        return bankM[n % 2]

                    def turn(n):
                        pe.wait_ge(hn_ready, n + 1)
                        for kd in range(KD):
                            j = JOB[("turn", n, kd)]
                            m = bank_free(j)
                            for t in range(QT):
                                ins = pe.transpose(m[:, t * P:(t + 1) * P], Hn[:, t, kd * P:(kd + 1) * P], identf[:, :])
                            ins.then_inc(m_full, 1)
                        read_done(pe, ("turn", n, KD - 1))

                    def columns(name, w, src, n):
                        j = JOB[name]
                        m = bank_free(j)
                        for kd in range(KD):
                            ins = pe.matmul(m[:, :], w[:, kd, n * P:(n + 1) * P], src[:, kd, :],
                                            start=(kd == 0), stop=(kd == KD - 1))
                        ins.then_inc(m_full, 1)

                    def tokens(name, half, src, w, nk):
                        j = JOB[name]
                        m = bank_free(j)
                        for i in range(2):
                            t = 2 * half + i
                            for k in range(nk):
                                ins = pe.matmul(m[:, i * D:(i + 1) * D], src[:, k, t * P:(t + 1) * P], w[:, k, :],
                                                start=(k == 0), stop=(k == nk - 1))
                        ins.then_inc(m_full, 1)

                    def project(a, what):
                        src = hT if what == "q" or a == 0 else cT
                        w = w_qkv[:, a, "qkv".index(what), :, :]
                        if what == "v":
                            for half in range(2):
                                tokens(("v", a, half), half, src, w, KD)
                        else:
                            for m in range(KD):
                                columns((what, a, m), w, src, m)

                    def score(a, v, qt):
                        n = (a * UNITS + v) * QT + qt
                        if n >= 2:
                            pe.wait_ge(s_read, n - 1)
                        pe.matmul(bankS[n % 2][:, :], QS[0:STACK, v, qt * P:(qt + 1) * P], KS[0:STACK, v, :],
                                  start=True, stop=True).then_inc(s_full, 1)

                    def score_t(a, u, j):
                        g, kt = u // QT, u % QT
                        e = (a * UNITS + u) * HG + j
                        if e >= 3:
                            p = e - 3
                            pe.wait_ge(t_masked if p < UNITS * HG else exp_done, p + 1)
                        h = g * HG + j
                        pe.matmul(bankT[e % 3][:, :], KS[0:ROWS, h, kt * P:(kt + 1) * P], QS[0:ROWS, h, :],
                                  start=True, stop=True).then_inc(t_full, 1)

                    def values(a, u):
                        U = a * UNITS + u
                        g, kt = u // QT, u % QT
                        pe.wait_ge(exp_done, (U + 1) * HG)
                        if kt == 0 and a * NG + g:
                            pe.wait_ge(o_read, a * NG + g)
                        for j in range(HG):
                            ins = pe.matmul(bankO[32 * j:32 * j + 32, :], V[:, kt, g * HG + j, :],
                                            prob[:, U % NP_, j, :], start=(kt == 0), stop=(kt == QT - 1))
                        ins.then_inc(av_done, 1)

                    def attention(a):
                        pe.wait_ge(stack_in[0], 192 * (a + 1))
                        pe.wait_ge(stack_in[1], 192 * (a + 1))
                        read_done(pe, ("v", a, 1))
                        for u in range(-LEAD, UNITS + 2):
                            if u >= 0 and u % QT == 0 and u < UNITS:
                                g = a * NG + u // QT
                                pe.wait_ge(rows_in[g % 2], 48 * (g // 2 + 1))
                            for j in range(HG):
                                if 0 <= u < UNITS:
                                    score_t(a, u, j)
                                if u + LEAD < UNITS:
                                    score(a, u + LEAD, j)
                            if 0 <= u - 1 < UNITS:
                                values(a, u - 1)
                            g = max_group(u)
                            if g is not None:
                                n = JOB[("max", a, g)]
                                m = bank_free(n)
                                pe.wait_ge(s_read, (a * UNITS + (g + 1) * HG) * QT)
                                pe.transpose(m[0:HG * QT, 0:P],
                                             Mx[:, (a * NG + g) % 2, :, :].rearrange("p h t -> p (h t)"),
                                             identf[:, :]).then_inc(m_full, 1)
                            g = out_group(u)
                            if g is not None:
                                n = JOB[("oT", a, g)]
                                m = bank_free(n)
                                pe.wait_ge(o_read, a * NG + g + 1)
                                for t in range(QT):
                                    ins = pe.transpose(m[:, t * P:(t + 1) * P],
                                                       oT[:, (a * NG + g) % 2, t * P:(t + 1) * P], identf[:, :])
                                ins.then_inc(m_full, 1)
                        read_done(pe, ("oT", a, NG - 1))
                        for kd in range(KD):
                            m = bank_free(JOB[("attT", a, kd)])
                            for t in range(QT):
                                ins = pe.transpose(m[:, t * P:(t + 1) * P], T1[:, t, kd * P:(kd + 1) * P], identf[:, :])
                            ins.then_inc(m_full, 1)
                        read_done(pe, ("attT", a, KD - 1))
                        for half in range(2):
                            tokens(("out", a, half), half, hT, w_o[:, a, :, :], KD)

                    turn(0)
                    for what in "qkv":
                        project(0, what)
                    attention(0)
                    pe.wait_ge(ctx_in, 48)
                    project(1, "k")
                    project(1, "v")
                    turn(1)
                    project(1, "q")
                    attention(1)
                    turn(2)
                    for f in range(FT):
                        columns(("ff1", f), w_ff1, hT, f)
                    read_done(pe, ("ff1", FT - 1))
                    for half in range(2):
                        tokens(("ff2", half), half, ff_h, w_ff2, FT)
                    pe.wait_ge(hn_ready, 5)
                    m = bank_free(JOB[("i8T",)])[:, :].bitcast(BF16).rearrange("p (k s) -> p k s", k=KD)
                    for kd in range(KD):
                        for t in range(QT):
                            ins = pe.transpose(m[:, kd, t * P:(t + 1) * P], xq[:, t, kd * P:(kd + 1) * P], identb[:, :])
                    ins.then_inc(m_full, 1)
                    read_done(pe, ("i8T",))
                    for half in range(2):
                        tokens(("i8", half), half, xqT, w_i8b, KD)
                    project(2, "k")
                    project(2, "v")
                    turn(5)
                    project(2, "q")
                    attention(2)
                    turn(6)
                    m = bank_free(JOB[("logits",)])
                    for t in range(QT):
                        for kd in range(KD):
                            ins = pe.matmul(m[:, t * NE:(t + 1) * NE], hT[:, kd, t * P:(t + 1) * P], w_router[:, kd, :],
                                            start=(kd == 0), stop=(kd == KD - 1))
                    ins.then_inc(m_full, 1)

                @block.vector
                def _(dve):
                    links = [0]

                    def link(ins):
                        links[0] += 1
                        ins.then_inc(chain, 1)
                        dve.wait_ge(chain, links[0])

                    def bank_of(name):
                        n = JOB[name]
                        dve.wait_ge(m_full, n + 1)
                        return bankM[n % 2]

                    def wide(r):
                        return b_row[:, r, :].unsqueeze(1).broadcast_to([P, QT, D])

                    def norm(n, src, eps, gain=None, dst=Hn):
                        for t in range(QT):
                            ins = dve.bn_stats(stats[:, t, :], src[:, t, :])
                        link(ins)
                        for t in range(QT):
                            ins = dve.bn_aggr(mv[:, t, :], stats[:, t, :])
                        link(ins)
                        dve.tensor_scalar(ve[:, :], mv[:, :, 1], eps, None, ALU.add).then_inc(ve_ready, 1)
                        dve.wait_ge(rstd_ready, n + 1)
                        for t in range(QT):
                            ins = dve.tensor_scalar(dst[:, t, :], src[:, t, :], mv[:, t, 0:1], rstd[:, t:t + 1],
                                                    ALU.subtract, ALU.mult)
                        if gain is None:
                            if n == 4:
                                link(ins)
                            else:
                                ins.then_inc(hn_ready, 1)
                            return
                        link(ins)
                        link(dve.tensor_tensor(dst[:, :, :], dst[:, :, :], wide(GAIN + gain), ALU.mult))
                        ins = dve.tensor_tensor(dst[:, :, :], dst[:, :, :], wide(BETA + gain), ALU.add)
                        if n == 3:
                            link(ins)
                        else:
                            ins.then_inc(hn_ready, 1)

                    def cut(a, t):
                        for m in range(KD):
                            n = PART[(a, t, m)]
                            j = JOB[("qk"[t], a, m)]
                            dve.wait_ge(m_act, nth[j])
                            if n >= 2:
                                dve.wait_ge(part_out[n % 2], 16 * (n // 2))
                            s = parts[:, n % 2, :, :]
                            link(dve.tensor_copy(s[:, 0, :], qf[:, n % 2, :]))
                            link(dve.tensor_tensor(rest[:, :], qf[:, n % 2, :], s[:, 0, :], ALU.subtract))
                            link(dve.tensor_copy(s[:, 1, :], rest[:, :]))
                            dve.tensor_tensor(s[:, 2, :], rest[:, :], s[:, 1, :], ALU.subtract).then_inc(part_ready, 1)

                    def values(a):
                        for half in range(2):
                            m = bank_of(("v", a, half))
                            for i in range(2):
                                ins = dve.tensor_tensor(V[:, 2 * half + i, :, 0:DEPTH],
                                                        m[:, i * D:(i + 1) * D].rearrange("p (h d) -> p h d", h=H),
                                                        b_row[:, BV + a, :].rearrange("p (h d) -> p h d", h=H), ALU.add)
                            ins.then_inc(m_dve, 1)

                    def maximum(a, v, qt):
                        n = (a * UNITS + v) * QT + qt
                        g = a * NG + v // HG
                        dve.wait_ge(s_full, n + 1)
                        if v % HG == 0 and qt == 0 and g >= 2:
                            dve.wait_ge(m_full, JOB[("max", (g - 2) // NG, (g - 2) % NG)] + 1)
                        dst = Mx[:, g % 2, v % HG, qt:qt + 1]
                        if a == 0:
                            dve.tensor_tensor_reduce(bankS[n % 2][:, :], bankS[n % 2][:, :], mb_n[:, qt, :], 1.0, -3.0e38,
                                                     ALU.add, ALU.max, dst).then_inc(s_read, 1)
                        else:
                            dve.tensor_reduce(dst, bankS[n % 2][:, :], AX.X, ALU.max).then_inc(s_read, 1)

                    def masked(u, j):
                        e = u * HG + j
                        if u >= NP_ and j == 0:
                            dve.wait_ge(av_done, u - NP_ + 1)
                        dve.wait_ge(t_full, e + 1)
                        dve.tensor_tensor(prob[:, u % NP_, j, :], bankT[e % 3][:, :], mb_t[:, u % QT, :],
                                          ALU.add).then_inc(t_masked, 1)

                    def attention(a):
                        if a == 0:
                            dve.wait_ge(mask_ready, 2)
                        for u in range(-LEAD, UNITS + 2):
                            for j in range(HG):
                                if a == 0 and 0 <= u < UNITS:
                                    masked(u, j)
                                if u + LEAD < UNITS:
                                    maximum(a, u + LEAD, j)
                            g = max_group(u)
                            if g is not None:
                                n = a * NG + g
                                m = bank_of(("max", a, g))
                                dve.tensor_scalar(neg[:, :], m[0:HG * QT, 0:P], -1.0, None,
                                                  ALU.mult).then_inc(m_dve, 1)
                                dve.wait_ge(m_dve, nth[JOB[("max", a, g)]])
                                if n >= 2:
                                    dve.wait_ge(rows_in[n % 2], 48 * (n // 2))
                                link(dve.tensor_copy(MR[:, n % 2, 0, :], neg[:, :]))
                                link(dve.tensor_tensor(neg[:, :], neg[:, :], MR[:, n % 2, 0, :], ALU.subtract))
                                link(dve.tensor_copy(MR[:, n % 2, 1, :], neg[:, :]))
                                dve.tensor_tensor(MR[:, n % 2, 2, :], neg[:, :], MR[:, n % 2, 1, :],
                                                  ALU.subtract).then_inc(mr_ready, 1)
                            g = out_group(u)
                            if g is not None:
                                m = bank_of(("oT", a, g))[:, :].rearrange("p (t h c) -> p t h c", t=QT, h=HG)
                                link(dve.reciprocal(rsum[:, g % 2, :, :], m[:, :, :, DEPTH]))
                                o = T1[:, :, g * HG * DEPTH:(g + 1) * HG * DEPTH].rearrange("p t (h c) -> p t h c", h=HG)
                                dve.tensor_tensor(o, m[:, :, :, 0:DEPTH],
                                                  rsum[:, g % 2, :, :].unsqueeze(3).broadcast_to([P, QT, HG, DEPTH]),
                                                  ALU.mult).then_inc(m_dve, 1)

                    def add_out(name, dst, hb):
                        dve.wait_ge(hb_ready, hb)
                        for half in range(2):
                            m = bank_of((*name, half))
                            dve.tensor_tensor(dst[:, 2 * half:2 * half + 2, :],
                                              m[:, :].rearrange("p (t n) -> p t n", t=2),
                                              HB[:, 2 * half:2 * half + 2, :], ALU.add).then_inc(m_dve, 1)
                        dve.wait_ge(m_dve, nth[JOB[(*name, 1)]])

                    dve.wait_ge(row_in, 16)
                    norm(0, X, 1e-5)
                    cut(0, 0)
                    cut(0, 1)
                    values(0)
                    attention(0)
                    add_out(("out", 0), T1, 1)
                    norm(1, T1, 1e-6, 0)
                    cut(1, 1)
                    values(1)
                    cut(1, 0)
                    attention(1)
                    add_out(("out", 1), T1, 2)
                    norm(2, T1, 1e-6, 1)
                    add_out(("ff2",), T1, 3)
                    norm(3, T1, 1e-6, 2, T1)
                    dve.tensor_tensor(X[:, :, :], X[:, :, :], T1[:, :, :], ALU.add).then_inc(hn_ready, 1)
                    dve.wait_ge(hn_ready, 4)
                    norm(4, X, 1e-5)
                    link(dve.tensor_reduce(amax[:, :], Hn[:, :, :], AX.X, ALU.max, apply_absolute_value=True))
                    link(dve.tensor_scalar(xscale[:, :], amax[:, :], 1e-6, 1.0 / 127.0, ALU.max, ALU.mult))
                    link(dve.reciprocal(xrec[:, :], xscale[:, :]))
                    for t in range(QT):
                        ins = dve.tensor_scalar(T1[:, t, :], Hn[:, t, :], xrec[:, t:t + 1], MAGIC, ALU.mult, ALU.add)
                    link(ins)
                    link(dve.tensor_scalar(T1[:, :, :], T1[:, :, :], -MAGIC, 127.0, ALU.add, ALU.min))
                    dve.tensor_scalar(xq[:, :, :], T1[:, :, :], -128.0, None, ALU.max).then_inc(hn_ready, 1)
                    m = bank_of(("i8T",))
                    dve.tensor_copy(xqT[:, :, :].rearrange("p k s -> p (k s)"), m[:, :].bitcast(BF16)).then_inc(m_dve, 1)
                    for half in range(2):
                        m = bank_of(("i8", half))
                        for i in range(2):
                            t = 2 * half + i
                            ins = dve.scalar_tensor_tensor(out=T1[:, t, :], in0=m[:, i * D:(i + 1) * D],
                                                           scalar=xscale[:, t:t + 1], in1=b_row[:, I8S, :],
                                                           op0=ALU.mult, op1=ALU.mult)
                        ins.then_inc(m_dve, 1)
                    dve.wait_ge(m_dve, nth[JOB[("i8", 1)]])
                    dve.wait_ge(hb_ready, 4)
                    link(dve.tensor_tensor(X[:, :, :], T1[:, :, :], HB[:, :, :], ALU.add))
                    norm(5, X, 1e-5)
                    cut(2, 1)
                    values(2)
                    cut(2, 0)
                    attention(2)
                    add_out(("out", 2), X, 5)
                    norm(6, X, 1e-5)
                    m = bank_of(("logits",))
                    dve.tensor_copy(lg[:, :, :].rearrange("p t e -> p (t e)"), m[:, 0:QT * NE]).then_inc(m_dve, 1)
                    dve.wait_ge(m_dve, nth[JOB[("logits",)]])
                    for t in range(QT):
                        ins = dve.max(top[:, t, :], lg[:, t, :])
                    ins.then_inc(t1_ready, 3)
                    dve.wait_ge(t1_ready, 3)
                    for t in range(QT):
                        ins = dve.max_index(topi[:, t, :], top[:, t, :], lg[:, t, :])
                    link(ins)
                    link(dve.tensor_copy(topf[:, :, :], topi[:, :, 0:2]))
                    dve.wait_ge(gate_sem, 1)
                    link(dve.tensor_scalar(gate_e[:, :, :], gate_e[:, :, :], 1.0, None, ALU.add))
                    link(dve.reciprocal(gate[:, :, :], gate_e[:, :, :]))
                    for t in range(QT):
                        for k in range(2):
                            ins = dve.tensor_scalar(wsel[:, t, k, :], iota_e[:, :], topf[:, t, k:k + 1],
                                                    gate[:, t, k:k + 1], ALU.is_equal, ALU.mult)
                    link(ins)
                    dve.tensor_tensor(wfull[:, :, :], wsel[:, :, 0, :], wsel[:, :, 1, :], ALU.add).then_inc(t1_ready, 1)

            nc.all_engine_barrier()
            for s in every:
                nc.gpsimd.sem_clear(s)
            nc.all_engine_barrier()

    experts(nc, x_scr, tT_scr, w_scr, gate_up, down, sgT, suT, sdT, out)


def experts(nc, x_scr, tT_scr, w_scr, gate_up, down, sgT, suT, sdT, out):
    acc_scr_tiles = B * QT
    with ExitStack() as phase:
        def sb(name, shape, dt):
            return phase.enter_context(nc.sbuf_tensor(name, shape, dt))

        def sem(name):
            s = phase.enter_context(nc.semaphore(name))
            every.append(s)
            return s

        every = []
        tT = sb("tT", [P, KD, B * S], F32)
        acc = sb("acc", [P, acc_scr_tiles, D], F32)
        wf = sb("wf", [P, B, QT, NE], F32)
        wcol = sb("wcol", [P, acc_scr_tiles], F32)
        wgu = sb("wgu", [P, KD, 2 * EH], F32)
        wdn = sb("wdn", [P, EH // P, D], F32)
        sg = sb("sg", [P, 2, S], F32)
        hid = sb("hid", [P, 2, 2, S], F32)
        bank = [phase.enter_context(nc.psum_tensor(f"ebank{i}", [P, 512], F32)) for i in range(8)]
        loaded = sem("loaded")
        up_full = sem("up_full")
        sg_done = sem("sg_done")
        hid_done = sem("hid_done")
        y_full = sem("y_full")
        y_read = sem("y_read")
        wcol_ready = sem("wcol_ready")
        stored = sem("stored")

        with nc.Block() as block:
            @block.sync
            def _(sp):
                for b in range(B):
                    sp.dma_start(tT[:, :, b * S:(b + 1) * S],
                                 tT_scr[b].rearrange("(k p) n -> p k n", p=P)).then_inc(loaded, 16)
                sp.dma_start(acc[:, :, :], x_scr.rearrange("b (t p) n -> p (b t) n", p=P)).then_inc(loaded, 16)
                sp.dma_start(wf[:, :, :, :].rearrange("p b t e -> p b (t e)"),
                             w_scr.rearrange("b p n -> p b n")).then_inc(loaded, 16)
                sp.wait_ge(loaded, 96)
        nc.all_engine_barrier()
        nc.gpsimd.sem_clear(loaded)
        nc.all_engine_barrier()

        def one(src_gu, src_dn, weight):
            with nc.Block() as block:
                @block.sync
                def _(sp):
                    for dst, src in zip((wgu[:, :, 0:EH], wgu[:, :, EH:2 * EH]), src_gu):
                        sp.dma_start(dst, src).then_inc(loaded, 16)
                    sp.dma_start(wdn[:, :, :], src_dn).then_inc(loaded, 16)

                @block.tensor
                def _(pe):
                    pe.wait_ge(loaded, 48)
                    for c in range(B):
                        for m in range(2):
                            n = c * 2 + m
                            if n >= 2:
                                pe.wait_ge(hid_done, n - 1)
                            for i in range(2):
                                bk = bank[(n % 2) * 2 + i]
                                for k in range(KD):
                                    ins = pe.matmul(bk[:, :], wgu[:, k, i * EH + m * P:i * EH + (m + 1) * P],
                                                    tT[:, k, c * S:(c + 1) * S], start=(k == 0), stop=(k == KD - 1))
                            ins.then_inc(up_full, 1)
                        pe.wait_ge(hid_done, 2 * (c + 1))
                        for t in range(QT):
                            n = c * QT + t
                            if n >= 4:
                                pe.wait_ge(y_read, n - 3)
                            for k in range(2):
                                ins = pe.matmul(bank[4 + n % 4][:, 0:D], hid[:, c % 2, k, t * P:(t + 1) * P],
                                                wdn[:, k, :], start=(k == 0), stop=(k == 1))
                            ins.then_inc(y_full, 1)

                @block.scalar
                def _(act):
                    for n in range(2 * B):
                        act.wait_ge(up_full, n + 1)
                        if n >= 2:
                            act.wait_ge(hid_done, n - 1)
                        act.activation(sg[:, n % 2, :], bank[(n % 2) * 2][:, :], ACT.Silu).then_inc(sg_done, 1)

                @block.vector
                def _(dve):
                    if weight is not None:
                        dve.tensor_copy(wcol[:, :], wf[:, :, :, :].rearrange("p b t e -> p (b t) e")[:, :, weight])\
                           .then_inc(wcol_ready, 1)
                    else:
                        dve.memset(wcol[:, :], 1.0).then_inc(wcol_ready, 1)
                    dve.wait_ge(wcol_ready, 1)
                    for c in range(B):
                        for m in range(2):
                            n = c * 2 + m
                            dve.wait_ge(sg_done, n + 1)
                            dve.tensor_tensor(hid[:, c % 2, m, :], bank[(n % 2) * 2 + 1][:, :], sg[:, n % 2, :],
                                              ALU.mult).then_inc(hid_done, 1)
                        for t in range(QT):
                            n = c * QT + t
                            dve.wait_ge(y_full, n + 1)
                            dve.scalar_tensor_tensor(out=acc[:, n, :], in0=bank[4 + n % 4][:, 0:D],
                                                     scalar=wcol[:, n:n + 1], in1=acc[:, n, :],
                                                     op0=ALU.mult, op1=ALU.add).then_inc(y_read, 1)
            nc.all_engine_barrier()
            for s in every:
                nc.gpsimd.sem_clear(s)
            nc.all_engine_barrier()

        with nc.Fori(0, NE) as e:
            gu = gate_up[e].rearrange("(k p) n -> p k n", p=P)
            one((gu[:, :, 0:EH], gu[:, :, EH:2 * EH]), down[e].rearrange("(k p) n -> p k n", p=P), e)
        for half in range(2):
            lo = half * EH
            one_gu = [s.rearrange("(k p) n -> p k n", p=P)[:, :, lo:lo + EH] for s in (sgT, suT)]
            one(one_gu, sdT[lo:lo + EH, :].rearrange("(k p) n -> p k n", p=P), None)
        with nc.Block() as block:
            @block.sync
            def _(sp):
                sp.dma_start(out.rearrange("b (t p) n -> p (b t) n", p=P), acc[:, :, :]).then_inc(stored, 16)
                sp.wait_ge(stored, 16)


def kernel(**inputs):
    import numpy as np
    import concourse.bacc as bacc
    from concourse.bass_utils import run_bass_kernel_spmd as run

    t = {k: np.asarray(v) for k, v in inputs.items()}
    L0, L1 = "L0_xattn_", "L1_xattn_"

    def chunks(w):
        return w.reshape(-1, P, w.shape[1]).transpose(1, 0, 2)

    qkv = [[t[L0 + f"w{c}{n}"] for c in "qkv"] for n in (1, 2)] + [[t[L1 + f"w{c}_w"].T for c in "qkv"]]
    wqkv = np.concatenate([chunks(w) for ws in qkv for w in ws], axis=1)
    wo = np.concatenate([chunks(w) for w in (t[L0 + "wo1"], t[L0 + "wo2"], t[L1 + "dense_w"].T)], axis=1)
    bqk = np.concatenate([t[n].reshape(KD, P).T for n in (
        L0 + "bq1", L0 + "bk1", L0 + "bq2", L0 + "bk2", L1 + "wq_b", L1 + "wk_b")], axis=1)
    brow = np.stack([t[n] for n in (
        L0 + "bv1", L0 + "bv2", L1 + "wv_b", L0 + "bo1", L0 + "bo2", L1 + "dense_b", L0 + "b_ff2",
        L0 + "g1", L0 + "g2", L0 + "g3", L0 + "be1", L0 + "be2", L0 + "be3",
        "L0_ffn_weight_scale", "L0_ffn_bias")])
    pm = t["mask_Bx1x1xS_ff1"].reshape(B, S)
    arrays = {
        "x": t["x"], "ctxT": t["ctx_1024"].transpose(0, 2, 1),
        "am": t["mask_1x1xSxS_fk0"].reshape(S, S), "amT": t["mask_1x1xSxS_fk0"].reshape(S, S).T,
        "pmrow": pm, "pmcol": pm.reshape(B, QT, P).transpose(0, 2, 1),
        "wqkv": wqkv, "wo": wo, "bqk": bqk, "brow": brow, "bff1": t[L0 + "b_ff1"].reshape(FT, P).T,
        "wff1": t[L0 + "w_ff1"], "wff2": t[L0 + "w_ff2"], "wi8": np.ascontiguousarray(t["L0_ffn_weight_q"].T).view(np.int32),
        "routerT": t["L1_ffn_router_w"].T, "gate_up": t["L1_ffn_gate_up_w"], "down": t["L1_ffn_down_w"],
        "sgT": t["L1_ffn_shared_gate_w"].T, "suT": t["L1_ffn_shared_up_w"].T, "sdT": t["L1_ffn_shared_down_w"].T,
    }
    arrays = {f"in_{k}": np.ascontiguousarray(v) for k, v in arrays.items()}
    nc = bacc.Bacc("TRN2", target_bir_lowering=False, num_devices=1)
    args = [nc.dram_tensor(k, a.shape, mybir.dt.from_np(a.dtype), kind="ExternalInput").ap()
            for k, a in arrays.items()]
    args.append(nc.dram_tensor("out_0", (B, S, D), F32, kind="ExternalOutput").ap())
    build(nc, *args)
    return run(nc, [arrays], core_ids=[0]).results[0]["out_0"]
```

```python
from contextlib import ExitStack

import concourse.bass as bass
from concourse import mybir

ALU = mybir.AluOpType
ACT = mybir.ActivationFunctionType
AX = mybir.AxisListType
F32 = mybir.dt.float32
BF16 = mybir.dt.bfloat16
I8 = mybir.dt.int8
I32 = mybir.dt.int32
U32 = mybir.dt.uint32

B, S, D, H = 4, 512, 256, 16
DEPTH = D // H
P = 128
QT = S // P
KD = D // P
DFF = 1024
FT = DFF // P
NE, EH = 16, 256
SH = 512
HG = 4
NG = H // HG
PAIRS_Q = (0, 0, 1, 1, 0, 2)
PAIRS_K = (0, 1, 0, 1, 2, 0)
STACK = DEPTH * len(PAIRS_Q)
ROWS = STACK + 3
ATT = 3
LEAD = 6
UNITS = NG * QT
MAGIC = 1.5 * 2.0 ** 23
NEG = -1.0e9
CAST = 1.0 / DEPTH ** 0.5
TT = B * QT
HT = SH // P
TOPK = 2
TILES = 48
TSTEP = 16


def misc_jobs():
    jobs = []

    def job(*name, by):
        jobs.append((name, by))

    def turned(n):
        for kd in range(KD):
            job("turn", n, kd, by="act")

    def project(a, what):
        if what == "v":
            for half in range(2):
                job("v", a, half, by="dve")
        else:
            for m in range(KD):
                job(what, a, m, by="act")

    def attention(a):
        for u in range(-LEAD, UNITS + 2):
            g = max_group(u)
            if g is not None:
                job("max", a, g, by="dve")
            g = out_group(u)
            if g is not None:
                job("oT", a, g, by="dve")
        for kd in range(KD):
            job("attT", a, kd, by="act")
        for half in range(2):
            job("out", a, half, by="dve")

    turned(0)
    for what in "qkv":
        project(0, what)
    attention(0)
    for a in (1, 2):
        for what in "kv":
            project(a, what)
        if a == 2:
            break
        turned(1)
        project(1, "q")
        attention(1)
        turned(2)
        for f in range(FT):
            job("ff1", f, by="act")
        for half in range(2):
            job("ff2", half, by="dve")
        job("i8T", by="dve")
        for half in range(2):
            job("i8", half, by="dve")
    turned(5)
    project(2, "q")
    attention(2)
    turned(6)
    job("logits", by="dve")
    job("rank", by="dve")
    return jobs


def max_group(u):
    v = u + LEAD - 1
    return v // QT if v >= 0 and v % QT == QT - 1 and v < UNITS else None


def out_group(u):
    v = u - 2
    return v // QT if v >= 0 and v % QT == QT - 1 and v < UNITS else None


def build(nc, x, ctxT, am, amT, pmrow, pmcol, wqkv, wo, bqk, brow, bff1, wff1, wff2, wi8,
          routerT, gate_up, down, sgT, suT, sdT, out):
    JOBS = misc_jobs()
    JOB = {name: n for n, (name, _) in enumerate(JOBS)}
    nth, counts = [], {"act": 0, "dve": 0}
    for _, by in JOBS:
        counts[by] += 1
        nth.append(counts[by])

    x_scr = nc.dram_tensor("x_scr", [B, S, D], F32, kind="Internal").ap()
    tT_scr = nc.dram_tensor("tT_scr", [B, D, S], F32, kind="Internal").ap()
    t_scr = nc.dram_tensor("t_scr", [B, S, D], F32, kind="Internal").ap()
    route_scr = nc.dram_tensor("route_scr", [B, P, QT * 6], F32, kind="Internal").ap()
    disp = nc.dram_tensor("disp", [TILES * P, D], F32, kind="Internal").ap()
    y_disp = nc.dram_tensor("y_disp", [TILES * P, D], F32, kind="Internal").ap()
    parts_scr = nc.dram_tensor("parts_scr", [ATT, 2, 3, D, S], BF16, kind="Internal").ap()

    lasting = ExitStack()
    cnt = lasting.enter_context(nc.sbuf_tensor("cnt", [P, NE], F32))
    zero = lasting.enter_context(nc.sbuf_tensor("zero", [P, D], F32))
    zero_ready = lasting.enter_context(nc.semaphore("zero_ready"))
    zeroed = lasting.enter_context(nc.semaphore("zeroed"))

    with ExitStack() as phase:
        def sb(name, shape, dt):
            return phase.enter_context(nc.sbuf_tensor(name, shape, dt))

        def sem(name):
            s = phase.enter_context(nc.semaphore(name))
            every.append(s)
            return s

        every = []
        identf = sb("identf", [P, P], F32)
        identb = sb("identb", [P, P], BF16)
        w_qkv = sb("w_qkv", [P, ATT, 3, KD, D], F32)
        w_o = sb("w_o", [P, ATT, KD, D], F32)
        w_ff1 = sb("w_ff1", [P, KD, DFF], F32)
        w_ff2 = sb("w_ff2", [P, FT, D], F32)
        w_i8 = sb("w_i8", [P, KD, D // 4], I32)
        w_i8b = sb("w_i8b", [P, KD, D], BF16)
        w_router = sb("w_router", [P, KD, NE], F32)
        b_qk = sb("b_qk", [P, ATT, 2, KD], F32)
        b_q4 = sb("b_q4", [P, ATT, KD], F32)
        b_ff1 = sb("b_ff1", [P, FT], F32)
        NROW = 15
        b_row = sb("b_row", [P, NROW, D], F32)
        BV, BO, BFF2, GAIN, BETA, I8S, I8B = 0, 3, 6, 7, 10, 13, 14
        minus_half = sb("minus_half", [P, QT], F32)
        iota_e = sb("iota_e", [P, NE], F32)
        ones_b = sb("ones_b", [P, P], BF16)
        before = sb("before", [P, P], BF16)
        am_n = sb("am_n", [P, QT, S], F32)
        am_t = sb("am_t", [P, QT, S], F32)
        X = sb("X", [P, QT, D], F32)
        Hn = sb("Hn", [P, QT, D], F32)
        HB = sb("HB", [P, QT, D], F32)
        T1 = sb("T1", [P, QT, D], F32)
        hT = sb("hT", [P, KD, S], F32)
        cT = sb("cT", [P, KD, S], F32)
        pm_row = sb("pm_row", [P, S], F32)
        pm_col = sb("pm_col", [P, QT], F32)
        mb_n = sb("mb_n", [P, QT, S], F32)
        mb_t = sb("mb_t", [P, QT, S], F32)
        QS = sb("QS", [P, H, S], BF16)
        KS = sb("KS", [P, H, S], BF16)
        V = sb("V", [P, QT, H, 32], F32)
        NP_ = 2
        prob = sb("prob", [P, NP_, HG, S], F32)
        ff_h = prob[:, :, :, :].rearrange("p a b c -> p (a b) c")
        qf = sb("qf", [P, 2, S], F32)
        rest = sb("rest", [P, S], F32)
        parts = sb("parts", [P, 2, 3, S], BF16)
        Mx = sb("Mx", [P, 2, HG, QT], F32)
        neg = sb("neg", [HG * QT, P], F32)
        MR = sb("MR", [HG * QT, 2, 3, P], BF16)
        oT = sb("oT", [P, 2, S], F32)
        rsum = sb("rsum", [P, 2, QT, HG], F32)
        stats = sb("stats", [P, QT, 6], F32)
        mv = sb("mv", [P, QT, 2], F32)
        ve = sb("ve", [P, QT], F32)
        rstd = sb("rstd", [P, QT], F32)
        amax = sb("amax", [P, QT], F32)
        xscale = sb("xscale", [P, QT], F32)
        xrec = sb("xrec", [P, QT], F32)
        xq = sb("xq", [P, QT, D], BF16)
        xqT = sb("xqT", [P, KD, S], BF16)
        lg = sb("lg", [P, QT, NE], F32)
        top = sb("top", [P, QT, 8], F32)
        topi = sb("topi", [P, QT, 8], U32)
        gate_e = sb("gate_e", [P, QT, 2], F32)
        sel = sb("sel", [P, 2, QT, NE], F32)
        both = sb("both", [P, QT, NE], BF16)
        ranks = sb("ranks", [P, QT, NE], F32)
        route = sb("route1", [P, QT, 6], F32)

        bank = [phase.enter_context(nc.psum_tensor(f"bank{i}", [P, 512], F32)) for i in range(8)]
        bankS, bankT, bankO, bankM = bank[0:2], bank[2:5], bank[5], bank[6:8]

        weights_in = sem("weights_in")
        consts_ready = sem("consts_ready")

        with nc.Block() as block:
            @block.sync
            def _(sp):
                n = 0
                for dst, src in ((w_qkv[:, :, :, :, :].rearrange("p a w k n -> p (a w k) n"), wqkv),
                                 (w_o[:, :, :, :].rearrange("p a k n -> p (a k) n"), wo),
                                 (b_qk[:, :, :, :].rearrange("p a w k -> p (a w k)"), bqk),
                                 (b_ff1[:, :], bff1),
                                 (w_ff1[:, :, :], wff1.rearrange("(k p) n -> p k n", p=P)),
                                 (w_ff2[:, :, :], wff2.rearrange("(k p) n -> p k n", p=P)),
                                 (w_i8[:, :, :], wi8.rearrange("(k p) n -> p k n", p=P)),
                                 (w_router[:, :, :], routerT.rearrange("(k p) n -> p k n", p=P)),
                                 (am_n[:, :, :], am.rearrange("(t p) k -> p t k", p=P)),
                                 (am_t[:, :, :], amT.rearrange("(t p) k -> p t k", p=P)),
                                 (b_row[:, :, :].rearrange("p r n -> p (r n)"),
                                  brow.rearrange("r n -> (r n)").partition_broadcast(P))):
                    sp.dma_start(dst, src).then_inc(weights_in, 16)
                    n += 16
                sp.wait_ge(zero_ready, 1)
                sp.dma_start(disp.rearrange("(t p) n -> p t n", p=P),
                             zero[:, :].unsqueeze(1).broadcast_to([P, TILES, D])).then_inc(zeroed, 16)
                sp.wait_ge(weights_in, n)

            @block.gpsimd
            def _(pool):
                pool.memset(identf[:, :], 0.0).then_inc(consts_ready, 1)
                pool.memset(identb[:, :], 0.0).then_inc(consts_ready, 1)
                pool.wait_ge(consts_ready, 2)
                for n, m in enumerate((identf, identb)):
                    pool.affine_select(out=m[:, :], in_=m[:, :], compare_op=ALU.not_equal, fill=1.0, base=0,
                                       pattern=[[-1, P]], channel_multiplier=1)
                pool.iota(iota_e[:, :], [[1, NE]], base=0, channel_multiplier=0,
                          allow_small_or_imprecise_dtypes=True)
                pool.memset(minus_half[:, :], -0.5)
                pool.memset(ones_b[:, :], 1.0).then_inc(consts_ready, 1)
                pool.wait_ge(consts_ready, 3)
                pool.affine_select(out=before[:, :], in_=ones_b[:, :], compare_op=ALU.is_gt, fill=0.0, base=0,
                                   pattern=[[1, P]], channel_multiplier=-1)

            @block.vector
            def _(dve):
                dve.memset(zero[:, :], 0.0).then_inc(zero_ready, 1)
                dve.memset(cnt[:, :], 0.0)
                dve.memset(V[:, :, :, :], 1.0)
                dve.memset(KS[STACK:ROWS, :, :], 1.0)
                dve.wait_ge(weights_in, 176)
                dve.tensor_copy(w_i8b[:, :, :], w_i8[:, :, :].bitcast(I8))
                dve.tensor_scalar(b_q4[:, :, :], b_qk[:, :, 0, :], CAST, None, ALU.mult)

        row_in = sem("row_in")
        ctx_in = sem("ctx_in")
        mask_ready = sem("mask_ready")
        m_full = sem("m_full")
        m_act = sem("m_act")
        m_dve = sem("m_dve")
        s_full = sem("s_full")
        s_read = sem("s_read")
        t_full = sem("t_full")
        t_masked = sem("t_masked")
        exp_done = sem("exp_done")
        av_done = sem("av_done")
        o_read = sem("o_read")
        hn_ready = sem("hn_ready")
        hb_ready = sem("hb_ready")
        ve_ready = sem("ve_ready")
        rstd_ready = sem("rstd_ready")
        part_ready = sem("part_ready")
        part_out = [sem(f"part_out{i}") for i in range(2)]
        stack_in = [sem(f"stack_in{i}") for i in range(2)]
        mr_ready = sem("mr_ready")
        rows_in = [sem(f"rows_in{i}") for i in range(2)]
        top_ready = sem("top_ready")
        both_ready = sem("both_ready")
        route_ready = sem("route_ready")
        chain = sem("chain")
        pchain = sem("pchain")
        gate_sem = sem("gate_sem")
        row_out = sem("row_out")

        PARTS = [(0, 0, 0), (0, 0, 1), (0, 1, 0), (0, 1, 1)]
        for a in (1, 2):
            PARTS += [(a, 1, 0), (a, 1, 1), (a, 0, 0), (a, 0, 1)]
        PART = {p: n for n, p in enumerate(PARTS)}
        LN_HB = {0: BO + 0, 1: BO + 1, 2: BFF2}

        def read_done(eng, name):
            n = JOB[name]
            eng.wait_ge(m_act if JOBS[n][1] == "act" else m_dve, nth[n])

        with nc.Fori(0, B) as row:
            with nc.Block() as block:
                @block.sync
                def _(sp):
                    sp.dma_start(X[:, :, :], x[row].rearrange("(t p) n -> p t n", p=P)).then_inc(row_in, 16)
                    sp.dma_start(pm_row[:, :], pmrow[row].partition_broadcast(P)).then_inc(ctx_in, 16)
                    sp.dma_start(pm_col[:, :], pmcol[row]).then_inc(ctx_in, 16)
                    sp.dma_start(cT[:, :, :], ctxT[row].rearrange("(k p) n -> p k n", p=P)).then_inc(ctx_in, 16)

                    def stack(a, t):
                        for m in range(KD):
                            n = PART[(a, t, m)]
                            sp.wait_ge(part_ready, n + 1)
                            sp.dma_start(parts_scr[a, t].rearrange("j (m p) s -> m p j s", p=P)[m],
                                         parts[:, n % 2, :, :]).then_inc(part_out[n % 2], 16)
                        if a:
                            sp.wait_ge(av_done, a * UNITS)
                        for m in range(KD):
                            n = PART[(a, t, m)]
                            sp.wait_ge(part_out[n % 2], 16 * (n // 2 + 1))
                            dst = (QS, KS)[t]
                            for r, j in enumerate((PAIRS_Q, PAIRS_K)[t]):
                                src = parts_scr[a, t, j].rearrange("(h d) s -> d h s", d=DEPTH)
                                sp.dma_start(dst[DEPTH * r:DEPTH * (r + 1), m * 8:m * 8 + 8, :],
                                             src[:, m * 8:m * 8 + 8, :]).then_inc(stack_in[t], 16)

                    for a in range(ATT):
                        for t in ((0, 1) if a == 0 else (1, 0)):
                            stack(a, t)
                        for g in range(NG):
                            n = a * NG + g
                            sp.wait_ge(mr_ready, n + 1)
                            for j in range(3):
                                dst = QS[STACK + j:STACK + j + 1, g * HG:(g + 1) * HG, :]
                                sp.dma_start(dst.rearrange("o h (t q) -> o (h t) q", q=P),
                                             MR[:, n % 2, j, :]).then_inc(rows_in[n % 2], 16)
                    sp.wait_ge(hn_ready, 7)
                    sp.dma_start(x_scr[row].rearrange("(t p) n -> p t n", p=P), X[:, :, :]).then_inc(row_out, 16)
                    read_done(sp, ("turn", 6, 1))
                    read_done(sp, ("turn", 6, 0))
                    sp.dma_start(tT_scr[row].rearrange("(k p) n -> p k n", p=P), hT[:, :, :]).then_inc(row_out, 16)
                    sp.dma_start(t_scr[row].rearrange("(t p) n -> p t n", p=P), Hn[:, :, :]).then_inc(row_out, 16)
                    sp.wait_ge(route_ready, 1)
                    sp.dma_start(route_scr[row], route[:, :, :].rearrange("p t c -> p (t c)")).then_inc(row_out, 16)
                    sp.wait_ge(row_out, 64)

                @block.gpsimd
                def _(pool):
                    links = [0]

                    def link(ins):
                        links[0] += 1
                        ins.then_inc(pchain, 1)
                        pool.wait_ge(pchain, links[0])

                    def root(n):
                        pool.wait_ge(ve_ready, n + 1)
                        pool.tensor_tensor(rstd[:, :], ve[:, :], minus_half[:, :], ALU.pow).then_inc(rstd_ready, 1)

                    def residual(n, src, row_of):
                        pool.wait_ge(hn_ready, n + 1)
                        pool.tensor_tensor(HB[:, :, :], src[:, :, :],
                                           b_row[:, row_of, :].unsqueeze(1).broadcast_to([P, QT, D]),
                                           ALU.add).then_inc(hb_ready, 1)

                    root(0)
                    pool.wait_ge(ctx_in, 48)
                    link(pool.tensor_tensor(mb_n[:, :, :], am_n[:, :, :],
                                            pm_row[:, :].unsqueeze(1).broadcast_to([P, QT, S]), ALU.mult))
                    link(pool.tensor_scalar(mb_n[:, :, :], mb_n[:, :, :], -1.0, 1.0, ALU.mult, ALU.add))
                    pool.tensor_scalar(mb_n[:, :, :], mb_n[:, :, :], NEG, None, ALU.mult).then_inc(mask_ready, 1)
                    for kt in range(QT):
                        link(pool.tensor_scalar(mb_t[:, kt, :], am_t[:, kt, :], pm_col[:, kt:kt + 1], None, ALU.mult))
                    link(pool.tensor_scalar(mb_t[:, :, :], mb_t[:, :, :], -1.0, 1.0, ALU.mult, ALU.add))
                    pool.tensor_scalar(mb_t[:, :, :], mb_t[:, :, :], NEG, None, ALU.mult).then_inc(mask_ready, 1)
                    residual(0, Hn, BO)
                    root(1)
                    residual(1, Hn, BO + 1)
                    root(2)
                    residual(2, Hn, BFF2)
                    root(3)
                    residual(3, X, I8B)
                    root(4)
                    root(5)
                    residual(5, X, BO + 2)
                    root(6)

                @block.scalar
                def _(act):
                    def read(name, dst, func=ACT.Identity, **kw):
                        n = JOB[name]
                        act.wait_ge(m_full, n + 1)
                        act.activation(dst, bankM[n % 2][:, :], func, **kw).then_inc(m_act, 1)

                    def turn(n):
                        for kd in range(KD):
                            read(("turn", n, kd), hT[:, kd, :])

                    def project(a, t):
                        for m in range(KD):
                            n = PART[(a, t, m)]
                            if n >= 2:
                                act.wait_ge(part_ready, n - 1)
                            if t == 0:
                                read(("q", a, m), qf[:, n % 2, :], bias=b_q4[:, a, m:m + 1], scale=CAST)
                            else:
                                read(("k", a, m), qf[:, n % 2, :], bias=b_qk[:, a, 1, m:m + 1])

                    def attention(a):
                        for u in range(UNITS + 1):
                            if u < UNITS:
                                U = a * UNITS + u
                                if a and U >= NP_:
                                    act.wait_ge(av_done, U - NP_ + 1)
                                for j in range(HG):
                                    e = U * HG + j
                                    if a == 0:
                                        act.wait_ge(t_masked, e + 1)
                                        src = prob[:, U % NP_, j, :]
                                    else:
                                        act.wait_ge(t_full, e + 1)
                                        src = bankT[e % 3][:, :]
                                    act.activation(prob[:, U % NP_, j, :], src, ACT.Exp).then_inc(exp_done, 1)
                            if u % QT == 0 and u:
                                g = a * NG + u // QT - 1
                                act.wait_ge(av_done, a * UNITS + u)
                                if g >= 2:
                                    act.wait_ge(m_full, JOB[("oT", (g - 2) // NG, (g - 2) % NG)] + 1)
                                act.activation(oT[:, g % 2, :], bankO[:, :], ACT.Copy).then_inc(o_read, 1)
                        for kd in range(KD):
                            read(("attT", a, kd), hT[:, kd, :])

                    turn(0)
                    project(0, 0)
                    project(0, 1)
                    attention(0)
                    project(1, 1)
                    turn(1)
                    project(1, 0)
                    attention(1)
                    turn(2)
                    for f in range(FT):
                        read(("ff1", f), ff_h[:, f, :], ACT.Relu, bias=b_ff1[:, f:f + 1])
                    project(2, 1)
                    turn(5)
                    project(2, 0)
                    attention(2)
                    turn(6)
                    act.wait_ge(top_ready, 1)
                    act.activation(gate_e[:, :, :], top[:, :, 0:2], ACT.Exp, scale=-1.0).then_inc(gate_sem, 1)

                @block.tensor
                def _(pe):
                    def bank_free(n):
                        if n >= 2:
                            read_done(pe, JOBS[n - 2][0])
                        return bankM[n % 2]

                    def turn(n):
                        pe.wait_ge(hn_ready, n + 1)
                        for kd in range(KD):
                            j = JOB[("turn", n, kd)]
                            m = bank_free(j)
                            for t in range(QT):
                                ins = pe.transpose(m[:, t * P:(t + 1) * P], Hn[:, t, kd * P:(kd + 1) * P], identf[:, :])
                            ins.then_inc(m_full, 1)
                        read_done(pe, ("turn", n, KD - 1))

                    def columns(name, w, src, n):
                        j = JOB[name]
                        m = bank_free(j)
                        for kd in range(KD):
                            ins = pe.matmul(m[:, :], w[:, kd, n * P:(n + 1) * P], src[:, kd, :],
                                            start=(kd == 0), stop=(kd == KD - 1))
                        ins.then_inc(m_full, 1)

                    def tokens(name, half, src, w, nk):
                        j = JOB[name]
                        m = bank_free(j)
                        for i in range(2):
                            t = 2 * half + i
                            for k in range(nk):
                                ins = pe.matmul(m[:, i * D:(i + 1) * D], src[:, k, t * P:(t + 1) * P], w[:, k, :],
                                                start=(k == 0), stop=(k == nk - 1))
                        ins.then_inc(m_full, 1)

                    def project(a, what):
                        src = hT if what == "q" or a == 0 else cT
                        w = w_qkv[:, a, "qkv".index(what), :, :]
                        if what == "v":
                            for half in range(2):
                                tokens(("v", a, half), half, src, w, KD)
                        else:
                            for m in range(KD):
                                columns((what, a, m), w, src, m)

                    def score(a, v, qt):
                        n = (a * UNITS + v) * QT + qt
                        if n >= 2:
                            pe.wait_ge(s_read, n - 1)
                        pe.matmul(bankS[n % 2][:, :], QS[0:STACK, v, qt * P:(qt + 1) * P], KS[0:STACK, v, :],
                                  start=True, stop=True).then_inc(s_full, 1)

                    def score_t(a, u, j):
                        g, kt = u // QT, u % QT
                        e = (a * UNITS + u) * HG + j
                        if e >= 3:
                            p = e - 3
                            pe.wait_ge(t_masked if p < UNITS * HG else exp_done, p + 1)
                        h = g * HG + j
                        pe.matmul(bankT[e % 3][:, :], KS[0:ROWS, h, kt * P:(kt + 1) * P], QS[0:ROWS, h, :],
                                  start=True, stop=True).then_inc(t_full, 1)

                    def values(a, u):
                        U = a * UNITS + u
                        g, kt = u // QT, u % QT
                        pe.wait_ge(exp_done, (U + 1) * HG)
                        if kt == 0 and a * NG + g:
                            pe.wait_ge(o_read, a * NG + g)
                        for j in range(HG):
                            ins = pe.matmul(bankO[32 * j:32 * j + 32, :], V[:, kt, g * HG + j, :],
                                            prob[:, U % NP_, j, :], start=(kt == 0), stop=(kt == QT - 1))
                        ins.then_inc(av_done, 1)

                    def attention(a):
                        pe.wait_ge(stack_in[0], 192 * (a + 1))
                        pe.wait_ge(stack_in[1], 192 * (a + 1))
                        read_done(pe, ("v", a, 1))
                        for u in range(-LEAD, UNITS + 2):
                            if u >= 0 and u % QT == 0 and u < UNITS:
                                g = a * NG + u // QT
                                pe.wait_ge(rows_in[g % 2], 48 * (g // 2 + 1))
                            for j in range(HG):
                                if 0 <= u < UNITS:
                                    score_t(a, u, j)
                                if u + LEAD < UNITS:
                                    score(a, u + LEAD, j)
                            if 0 <= u - 1 < UNITS:
                                values(a, u - 1)
                            g = max_group(u)
                            if g is not None:
                                n = JOB[("max", a, g)]
                                m = bank_free(n)
                                pe.wait_ge(s_read, (a * UNITS + (g + 1) * HG) * QT)
                                pe.transpose(m[0:HG * QT, 0:P],
                                             Mx[:, (a * NG + g) % 2, :, :].rearrange("p h t -> p (h t)"),
                                             identf[:, :]).then_inc(m_full, 1)
                            g = out_group(u)
                            if g is not None:
                                n = JOB[("oT", a, g)]
                                m = bank_free(n)
                                pe.wait_ge(o_read, a * NG + g + 1)
                                for t in range(QT):
                                    ins = pe.transpose(m[:, t * P:(t + 1) * P],
                                                       oT[:, (a * NG + g) % 2, t * P:(t + 1) * P], identf[:, :])
                                ins.then_inc(m_full, 1)
                        read_done(pe, ("oT", a, NG - 1))
                        for kd in range(KD):
                            m = bank_free(JOB[("attT", a, kd)])
                            for t in range(QT):
                                ins = pe.transpose(m[:, t * P:(t + 1) * P], T1[:, t, kd * P:(kd + 1) * P], identf[:, :])
                            ins.then_inc(m_full, 1)
                        read_done(pe, ("attT", a, KD - 1))
                        for half in range(2):
                            tokens(("out", a, half), half, hT, w_o[:, a, :, :], KD)

                    turn(0)
                    for what in "qkv":
                        project(0, what)
                    attention(0)
                    pe.wait_ge(ctx_in, 48)
                    project(1, "k")
                    project(1, "v")
                    turn(1)
                    project(1, "q")
                    attention(1)
                    turn(2)
                    for f in range(FT):
                        columns(("ff1", f), w_ff1, hT, f)
                    read_done(pe, ("ff1", FT - 1))
                    for half in range(2):
                        tokens(("ff2", half), half, ff_h, w_ff2, FT)
                    pe.wait_ge(hn_ready, 5)
                    m = bank_free(JOB[("i8T",)])[:, :].bitcast(BF16).rearrange("p (k s) -> p k s", k=KD)
                    for kd in range(KD):
                        for t in range(QT):
                            ins = pe.transpose(m[:, kd, t * P:(t + 1) * P], xq[:, t, kd * P:(kd + 1) * P], identb[:, :])
                    ins.then_inc(m_full, 1)
                    read_done(pe, ("i8T",))
                    for half in range(2):
                        tokens(("i8", half), half, xqT, w_i8b, KD)
                    project(2, "k")
                    project(2, "v")
                    turn(5)
                    project(2, "q")
                    attention(2)
                    turn(6)
                    m = bank_free(JOB[("logits",)])
                    for t in range(QT):
                        for kd in range(KD):
                            ins = pe.matmul(m[:, t * NE:(t + 1) * NE], hT[:, kd, t * P:(t + 1) * P], w_router[:, kd, :],
                                            start=(kd == 0), stop=(kd == KD - 1))
                    ins.then_inc(m_full, 1)
                    m = bank_free(JOB[("rank",)])
                    pe.wait_ge(both_ready, 1)
                    for t in range(QT + 1):
                        for e in range(min(t + 1, QT)):
                            ins = pe.matmul(m[:, t * NE:(t + 1) * NE], (before if e == t else ones_b)[:, :],
                                            both[:, e, :], start=(e == 0), stop=(e == min(t, QT - 1)))
                    ins.then_inc(m_full, 1)

                @block.vector
                def _(dve):
                    links = [0]

                    def link(ins):
                        links[0] += 1
                        ins.then_inc(chain, 1)
                        dve.wait_ge(chain, links[0])

                    def bank_of(name):
                        n = JOB[name]
                        dve.wait_ge(m_full, n + 1)
                        return bankM[n % 2]

                    def wide(r):
                        return b_row[:, r, :].unsqueeze(1).broadcast_to([P, QT, D])

                    def norm(n, src, eps, gain=None, dst=Hn):
                        for t in range(QT):
                            ins = dve.bn_stats(stats[:, t, :], src[:, t, :])
                        link(ins)
                        for t in range(QT):
                            ins = dve.bn_aggr(mv[:, t, :], stats[:, t, :])
                        link(ins)
                        dve.tensor_scalar(ve[:, :], mv[:, :, 1], eps, None, ALU.add).then_inc(ve_ready, 1)
                        dve.wait_ge(rstd_ready, n + 1)
                        for t in range(QT):
                            ins = dve.tensor_scalar(dst[:, t, :], src[:, t, :], mv[:, t, 0:1], rstd[:, t:t + 1],
                                                    ALU.subtract, ALU.mult)
                        if gain is None:
                            if n == 4:
                                link(ins)
                            else:
                                ins.then_inc(hn_ready, 1)
                            return
                        link(ins)
                        link(dve.tensor_tensor(dst[:, :, :], dst[:, :, :], wide(GAIN + gain), ALU.mult))
                        ins = dve.tensor_tensor(dst[:, :, :], dst[:, :, :], wide(BETA + gain), ALU.add)
                        if n == 3:
                            link(ins)
                        else:
                            ins.then_inc(hn_ready, 1)

                    def cut(a, t):
                        for m in range(KD):
                            n = PART[(a, t, m)]
                            j = JOB[("qk"[t], a, m)]
                            dve.wait_ge(m_act, nth[j])
                            if n >= 2:
                                dve.wait_ge(part_out[n % 2], 16 * (n // 2))
                            s = parts[:, n % 2, :, :]
                            link(dve.tensor_copy(s[:, 0, :], qf[:, n % 2, :]))
                            link(dve.tensor_tensor(rest[:, :], qf[:, n % 2, :], s[:, 0, :], ALU.subtract))
                            link(dve.tensor_copy(s[:, 1, :], rest[:, :]))
                            dve.tensor_tensor(s[:, 2, :], rest[:, :], s[:, 1, :], ALU.subtract).then_inc(part_ready, 1)

                    def values(a):
                        for half in range(2):
                            m = bank_of(("v", a, half))
                            for i in range(2):
                                ins = dve.tensor_tensor(V[:, 2 * half + i, :, 0:DEPTH],
                                                        m[:, i * D:(i + 1) * D].rearrange("p (h d) -> p h d", h=H),
                                                        b_row[:, BV + a, :].rearrange("p (h d) -> p h d", h=H), ALU.add)
                            ins.then_inc(m_dve, 1)

                    def maximum(a, v, qt):
                        n = (a * UNITS + v) * QT + qt
                        g = a * NG + v // HG
                        dve.wait_ge(s_full, n + 1)
                        if v % HG == 0 and qt == 0 and g >= 2:
                            dve.wait_ge(m_full, JOB[("max", (g - 2) // NG, (g - 2) % NG)] + 1)
                        dst = Mx[:, g % 2, v % HG, qt:qt + 1]
                        if a == 0:
                            dve.tensor_tensor_reduce(bankS[n % 2][:, :], bankS[n % 2][:, :], mb_n[:, qt, :], 1.0, -3.0e38,
                                                     ALU.add, ALU.max, dst).then_inc(s_read, 1)
                        else:
                            dve.tensor_reduce(dst, bankS[n % 2][:, :], AX.X, ALU.max).then_inc(s_read, 1)

                    def masked(u, j):
                        e = u * HG + j
                        if u >= NP_ and j == 0:
                            dve.wait_ge(av_done, u - NP_ + 1)
                        dve.wait_ge(t_full, e + 1)
                        dve.tensor_tensor(prob[:, u % NP_, j, :], bankT[e % 3][:, :], mb_t[:, u % QT, :],
                                          ALU.add).then_inc(t_masked, 1)

                    def attention(a):
                        if a == 0:
                            dve.wait_ge(mask_ready, 2)
                        for u in range(-LEAD, UNITS + 2):
                            for j in range(HG):
                                if a == 0 and 0 <= u < UNITS:
                                    masked(u, j)
                                if u + LEAD < UNITS:
                                    maximum(a, u + LEAD, j)
                            g = max_group(u)
                            if g is not None:
                                n = a * NG + g
                                m = bank_of(("max", a, g))
                                dve.tensor_scalar(neg[:, :], m[0:HG * QT, 0:P], -1.0, None,
                                                  ALU.mult).then_inc(m_dve, 1)
                                dve.wait_ge(m_dve, nth[JOB[("max", a, g)]])
                                if n >= 2:
                                    dve.wait_ge(rows_in[n % 2], 48 * (n // 2))
                                link(dve.tensor_copy(MR[:, n % 2, 0, :], neg[:, :]))
                                link(dve.tensor_tensor(neg[:, :], neg[:, :], MR[:, n % 2, 0, :], ALU.subtract))
                                link(dve.tensor_copy(MR[:, n % 2, 1, :], neg[:, :]))
                                dve.tensor_tensor(MR[:, n % 2, 2, :], neg[:, :], MR[:, n % 2, 1, :],
                                                  ALU.subtract).then_inc(mr_ready, 1)
                            g = out_group(u)
                            if g is not None:
                                m = bank_of(("oT", a, g))[:, :].rearrange("p (t h c) -> p t h c", t=QT, h=HG)
                                link(dve.reciprocal(rsum[:, g % 2, :, :], m[:, :, :, DEPTH]))
                                o = T1[:, :, g * HG * DEPTH:(g + 1) * HG * DEPTH].rearrange("p t (h c) -> p t h c", h=HG)
                                dve.tensor_tensor(o, m[:, :, :, 0:DEPTH],
                                                  rsum[:, g % 2, :, :].unsqueeze(3).broadcast_to([P, QT, HG, DEPTH]),
                                                  ALU.mult).then_inc(m_dve, 1)

                    def add_out(name, dst, hb):
                        dve.wait_ge(hb_ready, hb)
                        for half in range(2):
                            m = bank_of((*name, half))
                            dve.tensor_tensor(dst[:, 2 * half:2 * half + 2, :],
                                              m[:, :].rearrange("p (t n) -> p t n", t=2),
                                              HB[:, 2 * half:2 * half + 2, :], ALU.add).then_inc(m_dve, 1)
                        dve.wait_ge(m_dve, nth[JOB[(*name, 1)]])

                    dve.wait_ge(row_in, 16)
                    norm(0, X, 1e-5)
                    cut(0, 0)
                    cut(0, 1)
                    values(0)
                    attention(0)
                    add_out(("out", 0), T1, 1)
                    norm(1, T1, 1e-6, 0)
                    cut(1, 1)
                    values(1)
                    cut(1, 0)
                    attention(1)
                    add_out(("out", 1), T1, 2)
                    norm(2, T1, 1e-6, 1)
                    add_out(("ff2",), T1, 3)
                    norm(3, T1, 1e-6, 2, T1)
                    dve.tensor_tensor(X[:, :, :], X[:, :, :], T1[:, :, :], ALU.add).then_inc(hn_ready, 1)
                    dve.wait_ge(hn_ready, 4)
                    norm(4, X, 1e-5)
                    link(dve.tensor_reduce(amax[:, :], Hn[:, :, :], AX.X, ALU.max, apply_absolute_value=True))
                    link(dve.tensor_scalar(xscale[:, :], amax[:, :], 1e-6, 1.0 / 127.0, ALU.max, ALU.mult))
                    link(dve.reciprocal(xrec[:, :], xscale[:, :]))
                    for t in range(QT):
                        ins = dve.tensor_scalar(T1[:, t, :], Hn[:, t, :], xrec[:, t:t + 1], MAGIC, ALU.mult, ALU.add)
                    link(ins)
                    link(dve.tensor_scalar(T1[:, :, :], T1[:, :, :], -MAGIC, 127.0, ALU.add, ALU.min))
                    dve.tensor_scalar(xq[:, :, :], T1[:, :, :], -128.0, None, ALU.max).then_inc(hn_ready, 1)
                    m = bank_of(("i8T",))
                    dve.tensor_copy(xqT[:, :, :].rearrange("p k s -> p (k s)"), m[:, :].bitcast(BF16)).then_inc(m_dve, 1)
                    for half in range(2):
                        m = bank_of(("i8", half))
                        for i in range(2):
                            t = 2 * half + i
                            ins = dve.scalar_tensor_tensor(out=T1[:, t, :], in0=m[:, i * D:(i + 1) * D],
                                                           scalar=xscale[:, t:t + 1], in1=b_row[:, I8S, :],
                                                           op0=ALU.mult, op1=ALU.mult)
                        ins.then_inc(m_dve, 1)
                    dve.wait_ge(m_dve, nth[JOB[("i8", 1)]])
                    dve.wait_ge(hb_ready, 4)
                    link(dve.tensor_tensor(X[:, :, :], T1[:, :, :], HB[:, :, :], ALU.add))
                    norm(5, X, 1e-5)
                    cut(2, 1)
                    values(2)
                    cut(2, 0)
                    attention(2)
                    add_out(("out", 2), X, 5)
                    norm(6, X, 1e-5)
                    m = bank_of(("logits",))
                    dve.tensor_copy(lg[:, :, :].rearrange("p t e -> p (t e)"), m[:, 0:QT * NE]).then_inc(m_dve, 1)
                    dve.wait_ge(m_dve, nth[JOB[("logits",)]])
                    for t in range(QT):
                        ins = dve.max(top[:, t, :], lg[:, t, :])
                    ins.then_inc(top_ready, 1)
                    dve.wait_ge(top_ready, 1)
                    for t in range(QT):
                        ins = dve.max_index(topi[:, t, :], top[:, t, :], lg[:, t, :])
                    link(ins)
                    link(dve.tensor_copy(route[:, :, 0:2], topi[:, :, 0:2]))
                    for t in range(QT):
                        for k in range(2):
                            ins = dve.tensor_scalar(sel[:, k, t, :], iota_e[:, :], route[:, t, k:k + 1], None,
                                                    ALU.is_equal)
                    link(ins)
                    dve.tensor_tensor(both[:, :, :], sel[:, 0, :, :], sel[:, 1, :, :], ALU.add).then_inc(both_ready, 1)
                    dve.wait_ge(gate_sem, 1)
                    link(dve.tensor_scalar(gate_e[:, :, :], gate_e[:, :, :], 1.0, None, ALU.add))
                    dve.reciprocal(route[:, :, 4:6], gate_e[:, :, :])
                    m = bank_of(("rank",))[:, 0:(QT + 1) * NE].rearrange("p (t e) -> p t e", e=NE)
                    link(dve.tensor_tensor(ranks[:, :, :], m[:, 0:QT, :],
                                           cnt[:, :].unsqueeze(1).broadcast_to([P, QT, NE]), ALU.add))
                    link(dve.tensor_tensor(cnt[:, :], m[:, QT, :], cnt[:, :], ALU.add))
                    link(dve.tensor_tensor(sel[:, :, :, :], sel[:, :, :, :],
                                           ranks[:, :, :].unsqueeze(1).broadcast_to([P, 2, QT, NE]), ALU.mult))
                    dve.tensor_reduce(route[:, :, 2:4].rearrange("p t k -> p k t"), sel[:, :, :, :], AX.X,
                                      ALU.add).then_inc(route_ready, 1)

            nc.all_engine_barrier()
            for s in every:
                nc.gpsimd.sem_clear(s)
            nc.all_engine_barrier()

    experts(nc, cnt, x_scr, t_scr, tT_scr, route_scr, disp, y_disp, zeroed, gate_up, down, sgT, suT, sdT, out)


def experts(nc, cnt, x_scr, t_scr, tT_scr, route_scr, disp, y_disp, zeroed, gate_up, down, sgT, suT, sdT, out):
    with ExitStack() as phase:
        def sb(name, shape, dt):
            return phase.enter_context(nc.sbuf_tensor(name, shape, dt))

        def sem(name):
            return phase.enter_context(nc.semaphore(name))

        acc = sb("acc", [P, TT, D], F32)
        w_gu = sb("w_gu", [P, NE, KD, 2 * EH], F32)
        w_dn = sb("w_dn", [P, NE, EH // P, D], F32)
        route = sb("route", [P, TT, 6], F32)
        slot = sb("slot", [P, TT, 2], U32)
        tile_expert = sb("tile_expert", [1, TILES], I32)
        bank = [phase.enter_context(nc.psum_tensor(f"ebank{i}", [P, 512], F32)) for i in range(8)]
        w_in = sem("w_in")

        with ExitStack() as step:
            def sb2(name, shape, dt):
                return step.enter_context(nc.sbuf_tensor(name, shape, dt))

            def sem2(name):
                return step.enter_context(nc.semaphore(name))

            t_all = sb2("t_all", [P, TT, D], F32)
            tT = sb2("tT", [P, KD, B * S], F32)
            s_gu = sb2("s_gu", [P, 2, KD, SH], F32)
            s_dn = sb2("s_dn", [P, SH // P, D], F32)
            sg = sb2("sg", [P, 2, S], F32)
            hid = sb2("hid", [P, 2, SH // P, S], F32)
            iota_e = sb2("iota_e2", [P, NE], F32)
            iota_t = sb2("iota_t", [P, TILES], F32)
            ones_e = sb2("ones_e", [P, NE], F32)
            ntile = sb2("ntile", [P, NE], F32)
            end = sb2("end", [P, NE], F32)
            start = sb2("start", [P, NE], F32)
            pick = sb2("pick", [P, TT, 2, NE], F32)
            slotf = sb2("slotf", [P, TT, 2], F32)
            past = sb2("past", [1, TILES, NE], F32)
            texp = sb2("texp", [1, TILES], F32)
            data_in = sem2("data_in")
            shared_in = sem2("shared_in")
            iota_ready = sem2("iota_ready")
            slot_ready = sem2("slot_ready")
            scattered = sem2("scattered")
            up_full = sem2("up_full")
            sg_done = sem2("sg_done")
            hid_done = sem2("hid_done")
            y_full = sem2("y_full")
            y_read = sem2("y_read")
            chain2 = sem2("chain2")
            with nc.Block() as block:
                @block.sync
                def _(sp):
                    for i, w in enumerate((sgT, suT)):
                        sp.dma_start(s_gu[:, i, :, :], w.rearrange("(k p) n -> p k n", p=P)).then_inc(shared_in, 16)
                    sp.dma_start(s_dn[:, :, :], sdT.rearrange("(k p) n -> p k n", p=P)).then_inc(shared_in, 16)
                    for b in range(B):
                        sp.dma_start(tT[:, :, b * S:(b + 1) * S],
                                     tT_scr[b].rearrange("(k p) n -> p k n", p=P)).then_inc(shared_in, 16)
                    sp.dma_start(route[:, :, :].rearrange("p (b t) c -> p b (t c)", b=B),
                                 route_scr.rearrange("b p n -> p b n")).then_inc(data_in, 16)
                    sp.dma_start(t_all[:, :, :], t_scr.rearrange("b (t p) n -> p (b t) n", p=P)).then_inc(data_in, 16)
                    sp.dma_start(acc[:, :, :], x_scr.rearrange("b (t p) n -> p (b t) n", p=P)).then_inc(data_in, 16)

                @block.gpsimd
                def _(pool):
                    pool.iota(iota_e[:, :], [[1, NE]], base=0, channel_multiplier=0,
                              allow_small_or_imprecise_dtypes=True).then_inc(iota_ready, 1)
                    pool.iota(iota_t[:, :], [[1, TILES]], base=0, channel_multiplier=0,
                              allow_small_or_imprecise_dtypes=True).then_inc(iota_ready, 1)
                    pool.wait_ge(slot_ready, 1)
                    pool.wait_ge(data_in, 48)
                    pool.wait_ge(zeroed, 16)
                    for t in range(TT):
                        for k in range(2):
                            pool.indirect_dma_start(disp, bass.IndirectOffsetOnAxis(slot[:, t, k:k + 1], 0),
                                                    t_all[:, t, :], None).then_inc(scattered, 16)
                    pool.wait_ge(scattered, 32 * TT)

                @block.scalar
                def _(act):
                    act.wait_ge(shared_in, 112)
                    for n in range(B * SH // P):
                        if n < NE:
                            act.dma_start(w_gu[:, n, :, :], gate_up[n].rearrange("(k p) n -> p k n", p=P)).then_inc(w_in, 16)
                            act.dma_start(w_dn[:, n, :, :], down[n].rearrange("(k p) n -> p k n", p=P)).then_inc(w_in, 16)
                        act.wait_ge(up_full, n + 1)
                        if n >= 2:
                            act.wait_ge(hid_done, n - 1)
                        act.activation(sg[:, n % 2, :], bank[(n % 2) * 2][:, :], ACT.Silu).then_inc(sg_done, 1)

                @block.tensor
                def _(pe):
                    def down_products(c):
                        pe.wait_ge(hid_done, HT * (c + 1))
                        for t in range(QT):
                            n = c * QT + t
                            if n >= 4:
                                pe.wait_ge(y_read, n - 3)
                            for k in range(HT):
                                ins = pe.matmul(bank[4 + n % 4][:, 0:D], hid[:, c % 2, k, t * P:(t + 1) * P],
                                                s_dn[:, k, :], start=(k == 0), stop=(k == HT - 1))
                            ins.then_inc(y_full, 1)

                    pe.wait_ge(shared_in, 112)
                    for c in range(B):
                        for m in range(HT):
                            n = c * HT + m
                            if n >= 2:
                                pe.wait_ge(hid_done, n - 1)
                            for i in range(2):
                                for k in range(KD):
                                    ins = pe.matmul(bank[(n % 2) * 2 + i][:, :], s_gu[:, i, k, m * P:(m + 1) * P],
                                                    tT[:, k, c * S:(c + 1) * S], start=(k == 0), stop=(k == KD - 1))
                            ins.then_inc(up_full, 1)
                            if c and m == 0:
                                down_products(c - 1)
                    down_products(B - 1)

                @block.vector
                def _(dve):
                    links = [0]

                    def link(ins):
                        links[0] += 1
                        ins.then_inc(chain2, 1)
                        dve.wait_ge(chain2, links[0])

                    link(dve.memset(ones_e[:, :], 1.0))
                    link(dve.tensor_scalar(ntile[:, :], cnt[:, :], 1.0 / P, (P - 1.0) / (2 * P), ALU.mult, ALU.add))
                    link(dve.tensor_scalar(ntile[:, :], ntile[:, :], MAGIC, None, ALU.add))
                    link(dve.tensor_scalar(ntile[:, :], ntile[:, :], -MAGIC, None, ALU.add))
                    link(dve.tensor_tensor_scan(end[:, :], ones_e[:, :], ntile[:, :], 0.0, ALU.mult, ALU.add))
                    link(dve.tensor_tensor(start[:, :], end[:, :], ntile[:, :], ALU.subtract))
                    dve.wait_ge(iota_ready, 2)
                    dve.wait_ge(data_in, 48)
                    wide = [P, TT * 2, NE]
                    flat = pick[:, :, :, :].rearrange("p t k e -> p (t k) e")
                    for k in range(2):
                        ins = dve.tensor_tensor(pick[:, :, k, :], iota_e[:, :].unsqueeze(1).broadcast_to([P, TT, NE]),
                                                route[:, :, k].unsqueeze(2).broadcast_to([P, TT, NE]), ALU.is_equal)
                    link(ins)
                    link(dve.tensor_tensor(flat, flat, start[:, :].unsqueeze(1).broadcast_to(wide), ALU.mult))
                    link(dve.tensor_reduce(slotf[:, :, :].rearrange("p t k -> p (t k)"), flat, AX.X, ALU.add))
                    link(dve.scalar_tensor_tensor(out=slotf[:, :, :], in0=slotf[:, :, :], scalar=float(P),
                                                  in1=route[:, :, 2:4], op0=ALU.mult, op1=ALU.add))
                    dve.tensor_copy(slot[:, :, :], slotf[:, :, :]).then_inc(slot_ready, 1)
                    link(dve.tensor_tensor(past[:, :, :], iota_t[0:1, :].unsqueeze(2).broadcast_to([1, TILES, NE]),
                                           end[0:1, :].unsqueeze(1).broadcast_to([1, TILES, NE]), ALU.is_ge))
                    link(dve.tensor_reduce(texp[:, :], past[:, :, :], AX.X, ALU.add))
                    link(dve.tensor_scalar(texp[:, :], texp[:, :], NE - 1.0, None, ALU.min))
                    link(dve.tensor_copy(tile_expert[:, :], texp[:, :]))
                    for c in range(B + 1):
                        for m in range(HT):
                            if c < B:
                                n = c * HT + m
                                dve.wait_ge(sg_done, n + 1)
                                dve.tensor_tensor(hid[:, c % 2, m, :], bank[(n % 2) * 2 + 1][:, :], sg[:, n % 2, :],
                                                  ALU.mult).then_inc(hid_done, 1)
                            if c and m == 0:
                                for t in range(QT):
                                    n = (c - 1) * QT + t
                                    dve.wait_ge(y_full, n + 1)
                                    dve.tensor_tensor(acc[:, n, :], bank[4 + n % 4][:, 0:D], acc[:, n, :],
                                                      ALU.add).then_inc(y_read, 1)

        with ExitStack() as step:
            def sb3(name, shape, dt):
                return step.enter_context(nc.sbuf_tensor(name, shape, dt))

            def sem3(name):
                s = step.enter_context(nc.semaphore(name))
                every.append(s)
                return s

            every = []
            NX = 8
            identf = sb3("identf2", [P, P], F32)
            ident_ready = step.enter_context(nc.semaphore("ident_ready"))
            xr = sb3("xr", [P, NX, D], F32)
            xT = sb3("xT", [P, 3, KD, P], F32)
            sgt = sb3("sgt", [P, 2, EH], F32)
            ht = sb3("ht", [P, 2, EH], F32)
            hTt = sb3("hTt", [P, 2, EH // P, P], F32)
            yt = sb3("yt", [P, 2, D], F32)
            rows_in = [sem3(f"rows_in_x{i}") for i in range(NX)]
            xT_full = sem3("xT_full")
            xT_read = sem3("xT_read")
            gu_full = sem3("gu_full")
            sg_ready = sem3("sg_ready")
            h_ready = sem3("h_ready")
            hT_full = sem3("hT_full")
            hT_read = sem3("hT_read")
            yt_full = sem3("yt_full")
            yt_read = sem3("yt_read")
            yt_out = [sem3(f"yt_out{i}") for i in range(2)]
            with nc.Block() as block:
                @block.gpsimd
                def _(pool):
                    pool.memset(identf[:, :], 0.0).then_inc(ident_ready, 1)
                    pool.wait_ge(ident_ready, 1)
                    pool.affine_select(out=identf[:, :], in_=identf[:, :], compare_op=ALU.not_equal, fill=1.0, base=0,
                                       pattern=[[-1, P]], channel_multiplier=1)

                @block.sync
                def _(sp):
                    sp.wait_ge(w_in, 32 * NE)

            x_t = disp.rearrange("(g t p) n -> g t p n", t=TSTEP, p=P)
            y_t = y_disp.rearrange("(g t p) n -> g t p n", t=TSTEP, p=P)
            with nc.Fori(0, TILES // TSTEP) as group:
                with nc.Block() as block:
                    @block.sync
                    def _(sp):
                        for s in range(TSTEP):
                            if s >= NX:
                                sp.wait_ge(xT_full, s - NX + 1)
                            sp.dma_start(xr[:, s % NX, :], x_t[group, s]).then_inc(rows_in[s % NX], 16)

                    @block.tensor
                    def _(pe):
                        def turn_rows(s):
                            pe.wait_ge(rows_in[s % NX], 16 * (s // NX + 1))
                            if s >= 2:
                                pe.wait_ge(xT_read, s - 1)
                            for k in range(KD):
                                ins = pe.transpose(bank[s % 2][:, k * P:(k + 1) * P], xr[:, s % NX, k * P:(k + 1) * P],
                                                   identf[:, :])
                            ins.then_inc(xT_full, 1)

                        def turn_hidden(s):
                            pe.wait_ge(h_ready, s + 1)
                            if s >= 2:
                                pe.wait_ge(hT_read, s - 1)
                            for k in range(EH // P):
                                ins = pe.transpose(bank[4 + s % 2][:, k * P:(k + 1) * P], ht[:, s % 2, k * P:(k + 1) * P],
                                                   identf[:, :])
                            ins.then_inc(hT_full, 1)

                        def down_product(s):
                            pe.wait_ge(hT_read, s + 1)
                            if s >= 2:
                                pe.wait_ge(yt_read, s - 1)
                            for k in range(EH // P):
                                ins = pe.matmul(bank[6 + s % 2][:, 0:D], hTt[:, s % 2, k, :],
                                                w_dn[:, bass.ds(expert[s], 1), k, :].rearrange("p a n -> p (a n)"),
                                                start=(k == 0), stop=(k == EH // P - 1))
                            ins.then_inc(yt_full, 1)

                        expert = []
                        turn_rows(0)
                        turn_rows(1)
                        for s in range(TSTEP + 2):
                            if s < TSTEP:
                                expert.append(pe.value_load(tile_expert[0:1, bass.ds(group * TSTEP + s, 1)],
                                                            min_val=0, max_val=NE - 1))
                                pe.wait_ge(xT_read, s + 1)
                                if s >= 2:
                                    pe.wait_ge(h_ready, s - 1)
                                for k in range(KD):
                                    ins = pe.matmul(bank[2 + s % 2][:, :], xT[:, s % 3, k, :],
                                                    w_gu[:, bass.ds(expert[s], 1), k, :].rearrange("p a n -> p (a n)"),
                                                    start=(k == 0), stop=(k == KD - 1))
                                ins.then_inc(gu_full, 1)
                            if s + 2 < TSTEP:
                                turn_rows(s + 2)
                            if 0 <= s - 1 < TSTEP:
                                turn_hidden(s - 1)
                            if s >= 2:
                                down_product(s - 2)

                    @block.scalar
                    def _(act):
                        for s in range(TSTEP + 2):
                            if s < TSTEP:
                                act.wait_ge(gu_full, s + 1)
                                if s >= 2:
                                    act.wait_ge(h_ready, s - 1)
                                act.activation(sgt[:, s % 2, :], bank[2 + s % 2][:, 0:EH], ACT.Silu).then_inc(sg_ready, 1)
                            if s >= 2:
                                n = s - 2
                                act.wait_ge(yt_full, n + 1)
                                if n >= 2:
                                    act.wait_ge(yt_out[n % 2], 16 * (n // 2))
                                act.activation(yt[:, n % 2, :], bank[6 + n % 2][:, 0:D], ACT.Copy).then_inc(yt_read, 1)
                                act.wait_ge(yt_read, n + 1)
                                act.dma_start(y_t[group, n], yt[:, n % 2, :]).then_inc(yt_out[n % 2], 16)
                        for i in range(2):
                            act.wait_ge(yt_out[i], 16 * (TSTEP // 2))

                    @block.vector
                    def _(dve):
                        def read_rows(s):
                            dve.wait_ge(xT_full, s + 1)
                            if s >= 3:
                                dve.wait_ge(gu_full, s - 2)
                            dve.tensor_copy(xT[:, s % 3, :, :].rearrange("p k n -> p (k n)"),
                                            bank[s % 2][:, 0:D]).then_inc(xT_read, 1)

                        read_rows(0)
                        read_rows(1)
                        for s in range(TSTEP):
                            dve.wait_ge(sg_ready, s + 1)
                            if s >= 2:
                                dve.wait_ge(hT_full, s - 1)
                            dve.tensor_tensor(ht[:, s % 2, :], bank[2 + s % 2][:, EH:2 * EH], sgt[:, s % 2, :],
                                              ALU.mult).then_inc(h_ready, 1)
                            if s + 2 < TSTEP:
                                read_rows(s + 2)
                            dve.wait_ge(hT_full, s + 1)
                            if s >= 2:
                                dve.wait_ge(yt_full, s - 1)
                            dve.tensor_copy(hTt[:, s % 2, :, :].rearrange("p k n -> p (k n)"),
                                            bank[4 + s % 2][:, 0:EH]).then_inc(hT_read, 1)
                nc.all_engine_barrier()
                for s in every:
                    nc.gpsimd.sem_clear(s)
                nc.all_engine_barrier()

        with ExitStack() as step:
            NR = 4
            got = step.enter_context(nc.sbuf_tensor("got", [P, NR, 2, D], F32))
            got_in = [step.enter_context(nc.semaphore(f"got_in{i}")) for i in range(NR)]
            first = step.enter_context(nc.semaphore("first"))
            added = step.enter_context(nc.semaphore("added"))
            stored = step.enter_context(nc.semaphore("stored"))
            with nc.Block() as block:
                @block.gpsimd
                def _(pool):
                    for t in range(TT):
                        if t >= NR:
                            pool.wait_ge(added, t - NR + 1)
                        for k in range(2):
                            pool.indirect_dma_start(got[:, t % NR, k, :], None, y_disp,
                                                    bass.IndirectOffsetOnAxis(slot[:, t, k:k + 1], 0))\
                                .then_inc(got_in[t % NR], 16)

                @block.vector
                def _(dve):
                    for t in range(TT):
                        dve.wait_ge(got_in[t % NR], 32 * (t // NR + 1))
                        for k, s in enumerate((first, added)):
                            dve.scalar_tensor_tensor(out=acc[:, t, :], in0=got[:, t % NR, k, :],
                                                     scalar=route[:, t, 4 + k:5 + k], in1=acc[:, t, :],
                                                     op0=ALU.mult, op1=ALU.add).then_inc(s, 1)
                            if k == 0:
                                dve.wait_ge(first, t + 1)

                @block.sync
                def _(sp):
                    o = out.rearrange("b (t p) n -> (b t) p n", p=P)
                    for t in range(0, TT, 2):
                        sp.wait_ge(added, t + 2)
                        sp.dma_start(o[t:t + 2].rearrange("t p n -> p t n"), acc[:, t:t + 2, :]).then_inc(stored, 16)
                    sp.wait_ge(stored, 8 * TT)


def kernel(**inputs):
    import numpy as np
    import concourse.bacc as bacc
    from concourse.bass_utils import run_bass_kernel_spmd as run

    t = {k: np.asarray(v) for k, v in inputs.items()}
    L0, L1 = "L0_xattn_", "L1_xattn_"

    def chunks(w):
        return w.reshape(-1, P, w.shape[1]).transpose(1, 0, 2)

    qkv = [[t[L0 + f"w{c}{n}"] for c in "qkv"] for n in (1, 2)] + [[t[L1 + f"w{c}_w"].T for c in "qkv"]]
    wqkv = np.concatenate([chunks(w) for ws in qkv for w in ws], axis=1)
    wo = np.concatenate([chunks(w) for w in (t[L0 + "wo1"], t[L0 + "wo2"], t[L1 + "dense_w"].T)], axis=1)
    bqk = np.concatenate([t[n].reshape(KD, P).T for n in (
        L0 + "bq1", L0 + "bk1", L0 + "bq2", L0 + "bk2", L1 + "wq_b", L1 + "wk_b")], axis=1)
    brow = np.stack([t[n] for n in (
        L0 + "bv1", L0 + "bv2", L1 + "wv_b", L0 + "bo1", L0 + "bo2", L1 + "dense_b", L0 + "b_ff2",
        L0 + "g1", L0 + "g2", L0 + "g3", L0 + "be1", L0 + "be2", L0 + "be3",
        "L0_ffn_weight_scale", "L0_ffn_bias")])
    pm = t["mask_Bx1x1xS_ff1"].reshape(B, S)
    arrays = {
        "x": t["x"], "ctxT": t["ctx_1024"].transpose(0, 2, 1),
        "am": t["mask_1x1xSxS_fk0"].reshape(S, S), "amT": t["mask_1x1xSxS_fk0"].reshape(S, S).T,
        "pmrow": pm, "pmcol": pm.reshape(B, QT, P).transpose(0, 2, 1),
        "wqkv": wqkv, "wo": wo, "bqk": bqk, "brow": brow, "bff1": t[L0 + "b_ff1"].reshape(FT, P).T,
        "wff1": t[L0 + "w_ff1"], "wff2": t[L0 + "w_ff2"], "wi8": np.ascontiguousarray(t["L0_ffn_weight_q"].T).view(np.int32),
        "routerT": t["L1_ffn_router_w"].T, "gate_up": t["L1_ffn_gate_up_w"], "down": t["L1_ffn_down_w"],
        "sgT": t["L1_ffn_shared_gate_w"].T, "suT": t["L1_ffn_shared_up_w"].T, "sdT": t["L1_ffn_shared_down_w"].T,
    }
    arrays = {f"in_{k}": np.ascontiguousarray(v) for k, v in arrays.items()}
    nc = bacc.Bacc("TRN2", target_bir_lowering=False, num_devices=1)
    args = [nc.dram_tensor(k, a.shape, mybir.dt.from_np(a.dtype), kind="ExternalInput").ap()
            for k, a in arrays.items()]
    args.append(nc.dram_tensor("out_0", (B, S, D), F32, kind="ExternalOutput").ap())
    build(nc, *args)
    return run(nc, [arrays], core_ids=[0]).results[0]["out_0"]
```

```python
from contextlib import ExitStack

import concourse.bass as bass
from concourse import mybir

ALU = mybir.AluOpType
ACT = mybir.ActivationFunctionType
AX = mybir.AxisListType
F32 = mybir.dt.float32
BF16 = mybir.dt.bfloat16
I8 = mybir.dt.int8
I32 = mybir.dt.int32
U32 = mybir.dt.uint32

B, S, D, H = 4, 512, 256, 16
DEPTH = D // H
P = 128
QT = S // P
KD = D // P
DFF = 1024
FT = DFF // P
NE, EH = 16, 256
SH = 512
HG = 4
NG = H // HG
PAIRS_Q = (0, 0, 1, 1, 0, 2)
PAIRS_K = (0, 1, 0, 1, 2, 0)
STACK = DEPTH * len(PAIRS_Q)
ROWS = STACK + 3
ATT = 3
LEAD = 7
AV_AT = 2
UNITS = NG * QT
LAST = UNITS + 2
MAGIC = 1.5 * 2.0 ** 23
NEG = -1.0e9
CAST = 1.0 / DEPTH ** 0.5
TT = B * QT
HT = SH // P
TOPK = 2
TILES = 48
TSTEP = 24


START = (8, 25, 42, 59, 88, 105)

LATER = 12


def pair_order():
    early, late = {}, {}

    def put(where, step, *ops):
        where.setdefault(step, []).extend(ops)

    def halves(*op):
        return (*op, 0), (*op, 1)

    put(late, START[0] + 3, ("weights", 0))
    put(late, START[2], ("zero", 0))
    for n, first in enumerate(START):
        p, a = n % 2, n // 2
        if a == 0:
            s = 1
            put(early, 0, ("in", p))
            put(early, s, ("stats", p, 0))
            put(early, s + 1, ("apply", p, 0))
            s = s + 1 if p == 0 else first - LATER
            put(late, s, ("turn", p, 0), ("res", p, 0))
            put(late, s + 1, ("col", n, "k", 0), ("col", n, "q", 0))
            put(early, s + 2, ("cut", n, "k", 0), ("cut", n, "q", 0))
            put(late, s + 2, ("col", n, "k", 1), ("col", n, "q", 1))
            if p == 0:
                put(late, s - 1, ("mask", p, 0))
                put(late, s, ("mask", p, 1))
                put(late, s + 2, ("load", n, 0), ("load", n, 1))
            else:
                put(late, s + 2, ("mask", p, 0))
                put(early, first + 1, ("mask", p, 1))
            put(early, s + 3, ("cut", n, "k", 1), ("cut", n, "q", 1))
            put(late, s + 3, *halves("v", n))
            put(early, s + 4, ("val", n))
        else:
            e = START[n - 2] + LEAD + LAST + 1
            put(late, e - 2, ("ctx", n))
            put(late, e, ("attT", n - 2), *halves("out", n - 2))
            put(early, e + 1, ("add", n - 2), ("stats", p, a))
            put(late, e + 1, ("col", n, "k", 0), ("col", n, "k", 1))
            put(early, e + 2, ("apply", p, a), ("affine", p, a), ("cut", n, "k", 0), ("cut", n, "k", 1))
            put(late, e + 3, ("turn", p, a), ("res", p, a))
            if a == 1:
                put(late, e + 4, ("col", n, "q", 0), ("col", n, "q", 1))
                put(early, e + 5, ("cut", n, "q", 0), ("cut", n, "q", 1))
                put(late, e + 5, *halves("v", n))
                put(early, e + 6, ("val", n))
            else:
                for f in range(FT):
                    put(late, e + 4 + f // 2, ("ff1", p, f))
                put(late, e + 8, ("ff2", p, 0, 0), ("ff2", p, 0, 1))
                put(late, e + 9, ("ff2", p, 1, 0), ("ff2", p, 1, 1))
                put(early, e + 9, ("ffadd", p, 0))
                put(early, e + 10, ("ffadd", p, 1), ("stats", p, 3))
                put(late, e + 10, *halves("v", n))
                put(early, e + 11, ("apply", p, 3), ("stats", p, 4), ("val", n))
                put(early, e + 12, ("apply", p, 4))
                put(late, e + 12, ("i8T", p))
                put(early, e + 13, ("i8turned", p))
                put(late, e + 13, ("i8", p), ("res", p, 4))
                put(early, e + 14, ("i8add", p), ("stats", p, 5))
                put(early, e + 15, ("apply", p, 5))
                put(late, e + 15, ("turn", p, 5), ("res", p, 5))
                put(late, e + 16, ("col", n, "q", 0), ("col", n, "q", 1))
                put(early, e + 17, ("cut", n, "q", 0), ("cut", n, "q", 1))
        for g in range(NG):
            if n or g >= 2:
                s = first - 1
                if n:
                    s = max(s, START[n - 1] + LEAD + QT * (g + 1) + 1)
                put(early, s, ("load", n, g))
        if a == 2:
            e = first + LEAD + LAST + 1
            put(late, e, ("attT", n), *halves("out", n))
            put(early, e + 1, ("add", n), ("stats", p, 6))
            put(early, e + 2, ("apply", p, 6))
            put(late, e + 2, ("turn", p, 6))
            put(late, e + 3, ("logits", p))
            put(early, e + 4, ("top", p))
            put(late, e + 4, ("rank", p))
            put(early, e + 5, ("route", p))

    order = []
    for step in range(max(early) + 1):
        under_way = [(n, step - first - LEAD) for n, first in enumerate(START) if first <= step <= first + LEAD + LAST]
        between = early.get(step, []) + late.get(step, [])
        for j in range(HG):
            order += [("tiles", n, u, j) for n, u in under_way]
            order += between[len(between) * j // HG:len(between) * (j + 1) // HG]
        order += [("jobs", n, u) for n, u in under_way]
    return order


def max_group(u):
    v = u + LEAD - 1
    return v // QT if v >= 0 and v % QT == QT - 1 and v < UNITS else None


def out_group(u):
    v = u - 2
    return v // QT if v >= 0 and v % QT == QT - 1 and v < UNITS else None


def jobs_made(kind, *at):
    if kind == "turn":
        return [("turn", *at, kd) for kd in range(KD)]
    if kind == "attT":
        return [("attT", *at, kd) for kd in range(KD)]
    if kind == "i8":
        return [(kind, *at, half) for half in range(2)]
    if kind in ("col", "v", "out", "ff1", "i8T", "logits", "rank"):
        return [(kind, *at)]
    if kind == "ff2":
        return [(kind, *at[0:2])] if at[2] == 0 else []
    if kind == "jobs":
        n, u = at
        return [(what, n, g) for what, g in (("max", max_group(u)), ("oT", out_group(u))) if g is not None]
    return []


def jobs_read(kind, *at):
    if kind in ("turn", "attT", "col", "ff1"):
        return "act", jobs_made(kind, *at)
    made = {"val": "v", "add": "out", "i8turned": "i8T", "i8add": "i8", "top": "logits", "route": "rank"}
    if kind in ("val", "add"):
        return "dve", [(made[kind], *at, half) for half in range(2)]
    if kind in made:
        return "dve", jobs_made(made[kind], *at)
    if kind == "ffadd":
        return "dve", [("ff2", *at)]
    if kind == "tiles":
        n, u, j = at
        return "dve", jobs_made("jobs", n, u - 1) if j == 1 else []
    return "dve", []


ORDER = pair_order()
JOB = {name: j for j, name in enumerate(job for op in ORDER for job in jobs_made(*op))}
READ = {}
for _engine in ("act", "dve"):
    for _op in ORDER:
        if jobs_read(*_op)[0] == _engine:
            for _job in jobs_read(*_op)[1]:
                READ[_job] = (_engine, 1 + sum(e == _engine for e, _ in READ.values()))
JOB_AT = list(JOB)
PART = {op[1:]: j for j, op in enumerate(op for op in ORDER if op[0] == "cut")}


def build(nc, x, ctxT, am, amT, pmrow, pmcol, wqkv, wo, bqk, brow, bff1, wff1, wff2, wi8,
          routerT, gate_up, down, sgT, suT, sdT, out):
    x_scr = nc.dram_tensor("x_scr", [B, S, D], F32, kind="Internal").ap()
    tT_scr = nc.dram_tensor("tT_scr", [B, D, S], F32, kind="Internal").ap()
    t_scr = nc.dram_tensor("t_scr", [B, S, D], F32, kind="Internal").ap()
    route_scr = nc.dram_tensor("route_scr", [B, P, QT * 6], F32, kind="Internal").ap()
    disp = nc.dram_tensor("disp", [TILES * P, D], F32, kind="Internal").ap()
    y_disp = nc.dram_tensor("y_disp", [TILES * P, D], F32, kind="Internal").ap()
    stack_scr = nc.dram_tensor("stack_scr", [2 * ATT, 2, STACK, H, S], BF16, kind="Internal").ap()

    lasting = ExitStack()
    cnt = lasting.enter_context(nc.sbuf_tensor("cnt", [P, NE], F32))
    zero = lasting.enter_context(nc.sbuf_tensor("zero", [P, D], F32))

    with ExitStack() as phase:
        def sb(name, shape, dt):
            return phase.enter_context(nc.sbuf_tensor(name, shape, dt))

        def sb2(name, shape, dt):
            return [sb(f"{name}{p}", shape, dt) for p in range(2)]

        def sem(name):
            s = phase.enter_context(nc.semaphore(name))
            every.append(s)
            return s

        def sem2(name):
            return [sem(f"{name}{p}") for p in range(2)]

        every = []
        identf = sb("identf", [P, P], F32)
        identb = sb("identb", [P, P], BF16)
        w_qkv = sb("w_qkv", [P, ATT, 3, KD, D], F32)
        w_o = sb("w_o", [P, ATT, KD, D], F32)
        w_ff1 = sb("w_ff1", [P, KD, DFF], F32)
        w_ff2 = sb("w_ff2", [P, FT, D], F32)
        w_i8b = sb("w_i8b", [P, KD, D], BF16)
        w_router = sb("w_router", [P, KD, NE], F32)
        b_qk = sb("b_qk", [P, ATT, 2, KD], F32)
        b_q4 = sb("b_q4", [P, ATT, KD], F32)
        b_ff1 = sb("b_ff1", [P, FT], F32)
        NROW = 15
        b_row = sb("b_row", [P, NROW, D], F32)
        BV, BO, BFF2, GAIN, BETA, I8S, I8B = 0, 3, 6, 7, 10, 13, 14
        minus_half = sb("minus_half", [P, QT], F32)
        iota_e = sb("iota_e", [P, NE], F32)
        ones_b = sb("ones_b", [P, P], BF16)
        before = sb("before", [P, P], BF16)
        X = sb2("X", [P, QT, D], F32)
        Hn = sb2("Hn", [P, QT, D], F32)
        T1 = sb2("T1", [P, QT, D], F32)
        hT = sb2("hT", [P, KD, S], F32)
        VW = DEPTH + 1
        V = sb2("V", [P, QT, H, VW], F32)
        pm_row = sb("pm_row", [P, S], F32)
        pm_col = sb2("pm_col", [P, QT], F32)
        cT = sb("cT", [P, KD, S], F32)
        ff_h = sb("ff_h", [P, FT, S], F32)
        mask0 = sb("mask0", [P, 2 * QT, S], F32)
        mb = [mask0[:, :, :], ff_h[:, :, :]]
        w_i8 = ff_h[:, 0, 0:KD * D // 4].bitcast(I32)
        QS = sb("QS", [P, H, S], BF16)
        KS = sb("KS", [P, H, S], BF16)
        NP_ = 2
        prob = sb("prob", [P, NP_, HG, S], F32)
        qf = sb("qf", [P, 2, S], F32)
        rest = sb("rest", [P, S], F32)
        parts = sb("parts", [P, 2, 3, S], BF16)
        Mx = sb("Mx", [P, 2, HG, QT], F32)
        neg = sb("neg", [HG * QT, P], F32)
        MR = sb("MR", [HG * QT, 2, 3, P], BF16)
        oT = sb("oT", [P, 2, S], F32)
        rsum = sb("rsum", [P, 2, QT, HG], F32)
        stats = sb("stats", [P, QT, 6], F32)
        mv = sb2("mv", [P, QT, 2], F32)
        ve = sb2("ve", [P, QT], F32)
        rstd = sb2("rstd", [P, QT], F32)
        amax = sb("amax", [P, QT], F32)
        xscale = sb2("xscale", [P, QT], F32)
        xrec = sb("xrec", [P, QT], F32)
        xq = [hT[p][:, 0, :].bitcast(BF16).rearrange("p (t n) -> p t n", t=QT) for p in range(2)]
        xqT = [hT[p][:, 1, :].bitcast(BF16).rearrange("p (k s) -> p k s", k=KD) for p in range(2)]
        lg = sb("lg", [P, QT, NE], F32)
        top = sb("top", [P, QT, 8], F32)
        topi = sb("topi", [P, QT, 8], U32)
        gate_e = sb2("gate_e", [P, QT, 2], F32)
        sel = sb2("sel", [P, 2, QT, NE], F32)
        both = sb2("both", [P, QT, NE], BF16)
        ranks = sb("ranks", [P, QT, NE], F32)
        route = sb2("route1", [P, QT, 6], F32)

        bank = [phase.enter_context(nc.psum_tensor(f"bank{i}", [P, 512], F32)) for i in range(8)]
        NS, NT, NM = 2, 2, 3
        bankS, bankT, bankO, bankM = bank[0:2], bank[2:4], bank[4], bank[5:8]
        made_at = {job: i for i, op in enumerate(ORDER) for job in jobs_made(*op)}
        read_at = {job: i for i, op in enumerate(ORDER) for job in jobs_read(*op)[1]}
        for j in range(len(JOB_AT) - NM):
            assert read_at[JOB_AT[j]] < made_at[JOB_AT[j + NM]], (JOB_AT[j], JOB_AT[j + NM])

        weights_in = sem("weights_in")
        consts_ready = sem("consts_ready")

        with nc.Block() as block:
            @block.sync
            def _(sp):
                n = 0
                for dst, src in ((b_qk[:, :, :, :].rearrange("p a w k -> p (a w k)"), bqk),
                                 (w_i8.rearrange("p (k n) -> p k n", k=KD), wi8.rearrange("(k p) n -> p k n", p=P)),
                                 (w_qkv[:, 0, :, :, :].rearrange("p w k n -> p (w k) n"), wqkv[:, 0:3 * KD, :]),
                                 (b_ff1[:, :], bff1),
                                 (b_row[:, 0:BFF2, :].rearrange("p r n -> p (r n)"),
                                  brow[0:BFF2].rearrange("r n -> (r n)").partition_broadcast(P))):
                    sp.dma_start(dst, src).then_inc(weights_in, 16)
                    n += 16
                sp.wait_ge(weights_in, n)

            @block.gpsimd
            def _(pool):
                pool.memset(identf[:, :], 0.0).then_inc(consts_ready, 1)
                pool.memset(identb[:, :], 0.0).then_inc(consts_ready, 1)
                pool.wait_ge(consts_ready, 2)
                for n, m in enumerate((identf, identb)):
                    pool.affine_select(out=m[:, :], in_=m[:, :], compare_op=ALU.not_equal, fill=1.0, base=0,
                                       pattern=[[-1, P]], channel_multiplier=1)
                pool.iota(iota_e[:, :], [[1, NE]], base=0, channel_multiplier=0,
                          allow_small_or_imprecise_dtypes=True)
                pool.memset(minus_half[:, :], -0.5)
                pool.memset(ones_b[:, :], 1.0).then_inc(consts_ready, 1)
                pool.wait_ge(consts_ready, 3)
                pool.affine_select(out=before[:, :], in_=ones_b[:, :], compare_op=ALU.is_gt, fill=0.0, base=0,
                                   pattern=[[1, P]], channel_multiplier=-1)

            @block.vector
            def _(dve):
                dve.memset(zero[:, :], 0.0)
                dve.memset(cnt[:, :], 0.0)
                for p in range(2):
                    dve.memset(V[p][:, :, :, :], 1.0)
                dve.memset(KS[STACK:ROWS, :, :], 1.0)
                dve.memset(bankO[:, :], 0.0)
                dve.wait_ge(weights_in, 80)
                dve.tensor_copy(w_i8b[:, :, :].rearrange("p k n -> p (k n)"), w_i8.bitcast(I8))
                dve.tensor_scalar(b_q4[:, :, :], b_qk[:, :, 0, :], CAST, None, ALU.mult)

        row_in = sem2("row_in")
        pm_in = sem2("pm_in")
        mask_in = [sem2("mask_in_n"), sem2("mask_in_t")]
        pm_neg = sem2("pm_neg")
        mask_ready = sem2("mask_ready")
        ctx_in = sem("ctx_in")
        m_full = sem("m_full")
        m_read = {"act": sem("m_act"), "dve": sem("m_dve")}
        s_full = sem("s_full")
        s_read = sem("s_read")
        t_full = sem("t_full")
        t_masked = sem("t_masked")
        exp_done = sem("exp_done")
        av_done = sem("av_done")
        o_read = sem("o_read")
        hn_ready = sem2("hn_ready")
        affine_ready = sem2("affine_ready")
        res_ready = sem2("res_ready")
        ve_ready = sem2("ve_ready")
        rstd_ready = sem2("rstd_ready")
        qf_ready = sem("qf_ready")
        part_ready = sem("part_ready")
        part_out = sem2("part_out")
        stack_in = [sem(f"stack_in{g}") for g in range(NG)]
        mr_ready = sem("mr_ready")
        rows_in = sem2("rows_in")
        top_ready = sem2("top_ready")
        both_ready = sem2("both_ready")
        route_ready = sem2("route_ready")
        gate_sem = sem2("gate_sem")
        chain = sem("chain")
        pchain = sem("pchain")
        row_out = sem("row_out")
        late_in = sem("late_in")
        zeroed = sem("zeroed")

        pairs = {name: ap.rearrange("(r p) a b -> r p a b", p=2)
                 for name, ap in dict(x=x, ctxT=ctxT, x_scr=x_scr, tT_scr=tT_scr, t_scr=t_scr).items()}
        pmrow2 = pmrow.rearrange("(r p) s -> r p s", p=2)
        pmcol2 = pmcol.rearrange("(r p) a b -> r p a b", p=2)
        route2 = route_scr.rearrange("(r p) a b -> r p a b", p=2)
        zero_half = disp.rearrange("(r q) n -> r q n", r=2)
        NORMS = 7
        RES = {0: 1, 1: 2, 2: 3, 4: 4, 5: 5}

        def read_done(eng, name):
            engine, count = READ[name]
            eng.wait_ge(m_read[engine], count)

        with nc.Fori(0, B // 2) as pair:
            with nc.Block() as block:
                @block.sync
                def _(sp):
                    def inputs(p):
                        sp.dma_start(X[p][:, :, :], pairs["x"][pair, p].rearrange("(t p) n -> p t n", p=P))\
                            .then_inc(row_in[p], 16)

                    def mask(p, i):
                        if i == 0:
                            if p:
                                sp.wait_ge(mask_ready[0], 1)
                            sp.dma_start(pm_row[:, :], pmrow2[pair, p].partition_broadcast(P)).then_inc(pm_in[p], 16)
                            sp.dma_start(pm_col[p][:, :], pmcol2[pair, p]).then_inc(pm_in[p], 16)
                        sp.dma_start(mb[p][:, QT * i:QT * (i + 1), :], (am, amT)[i].rearrange("(t p) k -> p t k", p=P))\
                            .then_inc(mask_in[i][p], 16)

                    def weights():
                        for dst, src in ((w_qkv[:, 1:, :, :, :].rearrange("p a w k n -> p (a w k) n"),
                                          wqkv[:, 3 * KD:, :]),
                                         (w_o[:, :, :, :].rearrange("p a k n -> p (a k) n"), wo),
                                         (w_ff1[:, :, :], wff1.rearrange("(k p) n -> p k n", p=P)),
                                         (w_ff2[:, :, :], wff2.rearrange("(k p) n -> p k n", p=P)),
                                         (w_router[:, :, :], routerT.rearrange("(k p) n -> p k n", p=P)),
                                         (b_row[:, BFF2:, :].rearrange("p r n -> p (r n)"),
                                          brow[BFF2:].rearrange("r n -> (r n)").partition_broadcast(P))):
                            sp.dma_start(dst, src).then_inc(late_in, 16)

                    def context(n):
                        p = n % 2
                        if n > 2:
                            sp.wait_ge(m_full, max(JOB[("v", n - 1, 1)], JOB[("col", n - 1, "k", 1)]) + 1)
                        sp.dma_start(cT[:, :, :], pairs["ctxT"][pair, p].rearrange("(k p) n -> p k n", p=P))\
                            .then_inc(ctx_in, 16)

                    def parts_out(n, what, m):
                        j = PART[(n, what, m)]
                        t = "qk".index(what)
                        sp.wait_ge(part_ready, j + 1)
                        for r, part in enumerate((PAIRS_Q, PAIRS_K)[t]):
                            sp.dma_start(stack_scr[n, t, DEPTH * r:DEPTH * (r + 1), 8 * m:8 * m + 8, :]
                                         .rearrange("d h s -> h d s"),
                                         parts[:, j % 2, part, :]).then_inc(part_out[j % 2], 16)

                    def load(n, g):
                        if n:
                            sp.wait_ge(av_done, (n - 1) * UNITS + QT * (g + 1))
                        for t, (what, dst) in enumerate((("q", QS), ("k", KS))):
                            j = PART[(n, what, g // 2)]
                            sp.wait_ge(part_out[j % 2], 96 * (j // 2 + 1))
                            sp.dma_start(dst[0:STACK, g * HG:(g + 1) * HG, :],
                                         stack_scr[n, t, :, g * HG:(g + 1) * HG, :]).then_inc(stack_in[g], 16)

                    def maxima(n, u):
                        g = max_group(u - 1)
                        if g is not None:
                            i = n * NG + g
                            sp.wait_ge(mr_ready, i + 1)
                            for j in range(3):
                                dst = QS[STACK + j:STACK + j + 1, g * HG:(g + 1) * HG, :]
                                sp.dma_start(dst.rearrange("o h (t q) -> o (h t) q", q=P),
                                             MR[:, i % 2, j, :]).then_inc(rows_in[i % 2], 16)

                    def turned(p):
                        sp.wait_ge(hn_ready[p], NORMS)
                        for name, src in (("x_scr", X), ("t_scr", Hn)):
                            sp.dma_start(pairs[name][pair, p].rearrange("(t p) n -> p t n", p=P),
                                         src[p][:, :, :]).then_inc(row_out, 16)
                        for kd in range(KD):
                            read_done(sp, ("turn", p, NORMS - 1, kd))
                        sp.dma_start(pairs["tT_scr"][pair, p].rearrange("(k p) n -> p k n", p=P),
                                     hT[p][:, :, :]).then_inc(row_out, 16)

                    for kind, *at in ORDER:
                        if kind == "in":
                            inputs(*at)
                        elif kind == "mask":
                            mask(*at)
                        elif kind == "weights":
                            weights()
                        elif kind == "zero":
                            sp.dma_start(zero_half[pair].rearrange("(t p) n -> p t n", p=P),
                                         zero[:, :].unsqueeze(1).broadcast_to([P, TILES // 2, D])).then_inc(zeroed, 16)
                        elif kind == "ctx":
                            context(*at)
                        elif kind == "cut":
                            parts_out(*at)
                        elif kind == "load":
                            load(*at)
                        elif kind == "tiles" and at[2] == 1:
                            maxima(*at[0:2])
                        elif kind == "logits":
                            turned(*at)
                        elif kind == "route":
                            p = at[0]
                            sp.wait_ge(route_ready[p], 1)
                            sp.dma_start(route2[pair, p], route[p][:, :, :].rearrange("p t c -> p (t c)"))\
                                .then_inc(row_out, 16)
                    sp.wait_ge(row_out, 128)
                    sp.wait_ge(zeroed, 16)

                @block.gpsimd
                def _(pool):
                    links = [0]

                    def link(ins):
                        links[0] += 1
                        ins.then_inc(pchain, 1)
                        pool.wait_ge(pchain, links[0])

                    def root(p, i):
                        pool.wait_ge(ve_ready[p], i + 1)
                        pool.tensor_tensor(rstd[p][:, :], ve[p][:, :], minus_half[:, :], ALU.pow)\
                            .then_inc(rstd_ready[p], 1)

                    def masks(p, i):
                        if i == 0:
                            pool.wait_ge(pm_in[p], 32)
                            link(pool.tensor_scalar(pm_row[:, :], pm_row[:, :], -1.0, None, ALU.mult))
                            link(pool.tensor_scalar(pm_col[p][:, :], pm_col[p][:, :], -1.0, None, ALU.mult))
                            pool.wait_ge(mask_in[0][p], 16)
                            m = mb[p][:, 0:QT, :]
                            link(pool.tensor_tensor(m, m, pm_row[:, :].unsqueeze(1).broadcast_to([P, QT, S]), ALU.mult))
                            pool.tensor_scalar(m, m, 1.0, NEG, ALU.add, ALU.mult).then_inc(mask_ready[p], 1)
                            return
                        pool.wait_ge(mask_in[1][p], 16)
                        for kt in range(QT):
                            m = mb[p][:, QT + kt, :]
                            link(pool.tensor_scalar(m, m, pm_col[p][:, kt:kt + 1], 1.0, ALU.mult, ALU.add))
                            pool.tensor_scalar(m, m, NEG, None, ALU.mult).then_inc(mask_ready[p], 1)

                    def affine(p, i):
                        if (p, i) == (0, 1):
                            pool.wait_ge(late_in, 96)
                        pool.wait_ge(hn_ready[p], i + 1)
                        for op, row_of in ((ALU.mult, GAIN), (ALU.add, BETA)):
                            ins = pool.tensor_tensor(Hn[p][:, :, :], Hn[p][:, :, :],
                                                     b_row[:, row_of + i - 1, :].unsqueeze(1).broadcast_to([P, QT, D]),
                                                     op)
                            if op is ALU.mult:
                                link(ins)
                        ins.then_inc(affine_ready[p], 1)

                    def residual(p, i):
                        if (p, i) == (0, 2):
                            pool.wait_ge(late_in, 96)
                        dst, row_of = {0: (Hn, BO), 1: (Hn, BO + 1), 2: (Hn, BFF2), 4: (X, I8B), 5: (X, BO + 2)}[i]
                        if dst is Hn:
                            pool.wait_ge(m_full, JOB[("turn", p, i, KD - 1)] + 1)
                        else:
                            pool.wait_ge(hn_ready[p], i + 1)
                        pool.tensor_tensor(dst[p][:, :, :], dst[p][:, :, :],
                                           b_row[:, row_of, :].unsqueeze(1).broadcast_to([P, QT, D]),
                                           ALU.add).then_inc(res_ready[p], 1)

                    for kind, *at in ORDER:
                        if kind == "stats":
                            root(*at)
                        elif kind == "mask":
                            masks(*at)
                        elif kind == "affine":
                            affine(*at)
                        elif kind == "res":
                            residual(*at)

                @block.scalar
                def _(act):
                    def read(name, dst, func=ACT.Identity, **kw):
                        j = JOB[name]
                        act.wait_ge(m_full, j + 1)
                        for d in dst:
                            ins = act.activation(d, bankM[j % NM][:, :], func, **kw)
                        return ins.then_inc(m_read["act"], 1)

                    def column(n, what, m):
                        a, name = n // 2, ("col", n, what, m)
                        j = PART[(n, what, m)]
                        if j >= 2:
                            act.wait_ge(part_ready, j - 1)
                            act.wait_ge(part_out[j % 2], 96 * (j // 2))
                        dst = (parts[:, j % 2, 0, :], qf[:, j % 2, :])
                        if what == "q":
                            read(name, dst, bias=b_q4[:, a, m:m + 1], scale=CAST)
                        else:
                            read(name, dst, bias=b_qk[:, a, 1, m:m + 1])

                    def tiles(n, u, j):
                        if 0 <= u < UNITS:
                            U = n * UNITS + u
                            if n >= 2 and U >= NP_ and j == 0:
                                act.wait_ge(av_done, U - NP_ + 1)
                            e = U * HG + j
                            if n < 2:
                                act.wait_ge(t_masked, e + 1)
                                src = prob[:, U % NP_, j, :]
                            else:
                                act.wait_ge(t_full, e + 1)
                                src = bankT[e % NT][:, :]
                            act.activation(prob[:, U % NP_, j, :], src, ACT.Exp).then_inc(exp_done, 1)
                        if j == HG - 1 and u > 0 and u % QT == 0 and u <= UNITS:
                            g = n * NG + u // QT - 1
                            act.wait_ge(av_done, n * UNITS + u)
                            if g >= 2:
                                act.wait_ge(m_full, JOB[("oT", (g - 2) // NG, (g - 2) % NG)] + 1)
                            act.activation(oT[:, g % 2, :], bankO[:, :], ACT.Copy).then_inc(o_read, 1)

                    for kind, *at in ORDER:
                        if kind == "tiles":
                            tiles(*at)
                        elif kind == "col":
                            column(*at)
                        elif kind in ("turn", "attT"):
                            for kd in range(KD):
                                read((kind, *at, kd), (hT[at[0] % 2][:, kd, :],))
                        elif kind == "ff1":
                            p, f = at
                            if p == 0 and f == 0:
                                act.wait_ge(t_masked, 2 * UNITS * HG)
                            read(("ff1", p, f), (ff_h[:, f, :],), ACT.Relu, bias=b_ff1[:, f:f + 1])
                        elif kind == "top":
                            p = at[0]
                            act.wait_ge(top_ready[p], 1)
                            act.activation(gate_e[p][:, :, :], top[:, :, 0:2], ACT.Exp, scale=-1.0)\
                                .then_inc(gate_sem[p], 1)

                @block.tensor
                def _(pe):
                    def bank_free(name):
                        j = JOB[name]
                        if j >= NM:
                            read_done(pe, JOB_AT[j - NM])
                        return bankM[j % NM]

                    def turn(kind, src, *at):
                        for kd in range(KD):
                            m = bank_free((kind, *at, kd))
                            for t in range(QT):
                                ins = pe.transpose(m[:, t * P:(t + 1) * P], src[:, t, kd * P:(kd + 1) * P],
                                                   identf[:, :])
                            ins.then_inc(m_full, 1)

                    def columns(name, w, src, m):
                        b = bank_free(name)
                        for kd in range(KD):
                            ins = pe.matmul(b[:, :], w[:, kd, m * P:(m + 1) * P], src[:, kd, :],
                                            start=(kd == 0), stop=(kd == KD - 1))
                        ins.then_inc(m_full, 1)

                    def tokens(name, half, src, w, nk, which=(0, 1)):
                        b = bank_free(name)
                        for i in which:
                            t = 2 * half + i
                            for k in range(nk):
                                ins = pe.matmul(b[:, i * D:(i + 1) * D], src[:, k, t * P:(t + 1) * P], w[:, k, :],
                                                start=(k == 0), stop=(k == nk - 1))
                        if which[-1] == 1:
                            ins.then_inc(m_full, 1)

                    def source(n, what):
                        p, a = n % 2, n // 2
                        if what != "q" and a:
                            pe.wait_ge(ctx_in, 16 * (n - 1))
                            return cT
                        read_done(pe, ("turn", p, (0, 1, 5)[a], KD - 1))
                        return hT[p]

                    def score(n, v, qt):
                        i = (n * UNITS + v) * QT + qt
                        if v % QT == 0 and qt == 0:
                            pe.wait_ge(stack_in[v // QT], 32 * (n + 1))
                        if i >= NS:
                            pe.wait_ge(s_read, i - NS + 1)
                        pe.matmul(bankS[i % NS][:, :], QS[0:STACK, v, qt * P:(qt + 1) * P], KS[0:STACK, v, :],
                                  start=True, stop=True).then_inc(s_full, 1)

                    def score_t(n, u, j):
                        g, kt = u // QT, u % QT
                        e = (n * UNITS + u) * HG + j
                        if kt == 0 and j == 0:
                            i = n * NG + g
                            pe.wait_ge(rows_in[i % 2], 48 * (i // 2 + 1))
                        if e >= NT:
                            b = e - NT
                            pe.wait_ge(t_masked if b < 2 * UNITS * HG else exp_done, b + 1)
                        h = g * HG + j
                        pe.matmul(bankT[e % NT][:, :], KS[0:ROWS, h, kt * P:(kt + 1) * P], QS[0:ROWS, h, :],
                                  start=True, stop=True).then_inc(t_full, 1)

                    def values(n, u):
                        U = n * UNITS + u
                        g, kt = u // QT, u % QT
                        if u == 0:
                            read_done(pe, ("v", n, 1))
                        pe.wait_ge(exp_done, (U + 1) * HG)
                        if kt == 0 and n * NG + g:
                            pe.wait_ge(o_read, n * NG + g)
                        for j in range(HG):
                            ins = pe.matmul(bankO[32 * j:32 * j + VW, :], V[n % 2][:, kt, g * HG + j, :],
                                            prob[:, U % NP_, j, :], start=(kt == 0), stop=(kt == QT - 1))
                        ins.then_inc(av_done, 1)

                    def tiles(n, u, j):
                        if 0 <= u < UNITS:
                            score_t(n, u, j)
                        if u + LEAD < UNITS:
                            score(n, u + LEAD, j)
                        if 0 <= u - 1 < UNITS and j == AV_AT:
                            values(n, u - 1)

                    def jobs(n, u):
                        g = max_group(u)
                        if g is not None:
                            m = bank_free(("max", n, g))
                            pe.wait_ge(s_read, (n * UNITS + (g + 1) * HG) * QT)
                            pe.transpose(m[0:HG * QT, 0:P],
                                         Mx[:, (n * NG + g) % 2, :, :].rearrange("p h t -> p (h t)"),
                                         identf[:, :]).then_inc(m_full, 1)
                        g = out_group(u)
                        if g is not None:
                            m = bank_free(("oT", n, g))
                            pe.wait_ge(o_read, n * NG + g + 1)
                            for t in range(QT):
                                ins = pe.transpose(m[:, t * P:(t + 1) * P],
                                                   oT[:, (n * NG + g) % 2, t * P:(t + 1) * P], identf[:, :])
                            ins.then_inc(m_full, 1)

                    for kind, *at in ORDER:
                        p = at[0] % 2
                        if kind == "tiles":
                            tiles(*at)
                        elif kind == "jobs":
                            jobs(*at)
                        elif kind == "turn":
                            i = at[1]
                            if i in (1, 2):
                                pe.wait_ge(affine_ready[p], i)
                            else:
                                pe.wait_ge(hn_ready[p], i + 1)
                            turn("turn", Hn[p], *at)
                        elif kind == "attT":
                            read_done(pe, ("oT", at[0], NG - 1))
                            turn("attT", T1[p], *at)
                        elif kind == "col":
                            n, what, m = at
                            columns((kind, *at), w_qkv[:, n // 2, "qkv".index(what), :, :], source(n, what), m)
                        elif kind == "v":
                            n, half = at
                            tokens(("v", n, half), half, source(n, "v"), w_qkv[:, n // 2, 2, :, :], KD)
                        elif kind == "out":
                            n, half = at
                            if n == 0 and half == 0:
                                pe.wait_ge(late_in, 96)
                            read_done(pe, ("attT", n, KD - 1))
                            tokens(("out", n, half), half, hT[p], w_o[:, n // 2, :, :], KD)
                        elif kind == "ff1":
                            read_done(pe, ("turn", p, 2, KD - 1))
                            columns(("ff1", *at), w_ff1, hT[p], at[1])
                        elif kind == "ff2":
                            read_done(pe, ("ff1", p, FT - 1))
                            tokens(("ff2", *at[0:2]), at[1], ff_h, w_ff2, FT, (at[2],))
                        elif kind == "i8T":
                            pe.wait_ge(hn_ready[p], 5)
                            m = bank_free(("i8T", p))[:, :].bitcast(BF16).rearrange("p (k s) -> p k s", k=KD)
                            for kd in range(KD):
                                for t in range(QT):
                                    ins = pe.transpose(m[:, kd, t * P:(t + 1) * P], xq[p][:, t, kd * P:(kd + 1) * P],
                                                       identb[:, :])
                            ins.then_inc(m_full, 1)
                        elif kind == "i8":
                            read_done(pe, ("i8T", p))
                            for half in range(2):
                                tokens(("i8", p, half), half, xqT[p], w_i8b, KD)
                        elif kind == "logits":
                            read_done(pe, ("turn", p, NORMS - 1, KD - 1))
                            m = bank_free(("logits", p))
                            for t in range(QT):
                                for kd in range(KD):
                                    ins = pe.matmul(m[:, t * NE:(t + 1) * NE], hT[p][:, kd, t * P:(t + 1) * P],
                                                    w_router[:, kd, :], start=(kd == 0), stop=(kd == KD - 1))
                            ins.then_inc(m_full, 1)
                        elif kind == "rank":
                            m = bank_free(("rank", p))
                            pe.wait_ge(both_ready[p], 1)
                            for t in range(QT + 1):
                                for e in range(min(t + 1, QT)):
                                    ins = pe.matmul(m[:, t * NE:(t + 1) * NE], (before if e == t else ones_b)[:, :],
                                                    both[p][:, e, :], start=(e == 0), stop=(e == min(t, QT - 1)))
                            ins.then_inc(m_full, 1)

                @block.vector
                def _(dve):
                    links = [0]

                    def link(ins):
                        links[0] += 1
                        ins.then_inc(chain, 1)
                        dve.wait_ge(chain, links[0])

                    def bank_of(name):
                        j = JOB[name]
                        dve.wait_ge(m_full, j + 1)
                        return bankM[j % NM]

                    def left(ins, name):
                        ins.then_inc(m_read["dve"], 1)

                    def wide(r):
                        return b_row[:, r, :].unsqueeze(1).broadcast_to([P, QT, D])

                    def statistics(p, i):
                        src = (X, T1, T1, T1, X, X, X)[i][p]
                        if i == 0:
                            dve.wait_ge(row_in[p], 16)
                        for t in range(QT):
                            ins = dve.bn_stats(stats[:, t, :], src[:, t, :])
                        link(ins)
                        for t in range(QT):
                            ins = dve.bn_aggr(mv[p][:, t, :], stats[:, t, :])
                        link(ins)
                        dve.tensor_scalar(ve[p][:, :], mv[p][:, :, 1], 1e-6 if i in (1, 2, 3) else 1e-5, None,
                                          ALU.add).then_inc(ve_ready[p], 1)

                    def normalise(p, i):
                        src = (X, T1, T1, T1, X, X, X)[i][p]
                        dst = (T1 if i == 3 else Hn)[p]
                        dve.wait_ge(rstd_ready[p], i + 1)
                        for t in range(QT):
                            ins = dve.tensor_scalar(dst[:, t, :], src[:, t, :], mv[p][:, t, 0:1],
                                                    rstd[p][:, t:t + 1], ALU.subtract, ALU.mult)
                        if i == 3:
                            link(ins)
                            link(dve.tensor_tensor(dst[:, :, :], dst[:, :, :], wide(GAIN + i - 1), ALU.mult))
                            ins = dve.tensor_tensor(dst[:, :, :], dst[:, :, :], wide(BETA + i - 1), ALU.add)
                        if i == 3:
                            link(ins)
                            ins = dve.tensor_tensor(X[p][:, :, :], X[p][:, :, :], T1[p][:, :, :], ALU.add)
                        if i == 4:
                            link(ins)
                            ins = quantise(p)
                        ins.then_inc(hn_ready[p], 1)
                        if i == 3:
                            dve.wait_ge(hn_ready[p], 4)

                    def quantise(p):
                        link(dve.tensor_reduce(amax[:, :], Hn[p][:, :, :], AX.X, ALU.max, apply_absolute_value=True))
                        link(dve.tensor_scalar(xscale[p][:, :], amax[:, :], 1e-6, 1.0 / 127.0, ALU.max, ALU.mult))
                        link(dve.reciprocal(xrec[:, :], xscale[p][:, :]))
                        for t in range(QT):
                            ins = dve.tensor_scalar(T1[p][:, t, :], Hn[p][:, t, :], xrec[:, t:t + 1], MAGIC,
                                                    ALU.mult, ALU.add)
                        link(ins)
                        link(dve.tensor_scalar(T1[p][:, :, :], T1[p][:, :, :], -MAGIC, 127.0, ALU.add, ALU.min))
                        return dve.tensor_scalar(xq[p], T1[p][:, :, :], -128.0, None, ALU.max)

                    def cut(n, what, m):
                        j = PART[(n, what, m)]
                        read_done(dve, ("col", n, what, m))
                        if j:
                            dve.wait_ge(part_ready, j)
                        s = parts[:, j % 2, :, :]
                        link(dve.tensor_tensor(rest[:, :], qf[:, j % 2, :], s[:, 0, :], ALU.subtract))
                        link(dve.tensor_copy(s[:, 1, :], rest[:, :]))
                        dve.tensor_tensor(s[:, 2, :], rest[:, :], s[:, 1, :], ALU.subtract).then_inc(part_ready, 1)

                    def take_values(n):
                        if n >= 2:
                            dve.wait_ge(av_done, (n - 1) * UNITS)
                        for half in range(2):
                            m = bank_of(("v", n, half))
                            for i in range(2):
                                ins = dve.tensor_tensor(V[n % 2][:, 2 * half + i, :, 0:DEPTH],
                                                        m[:, i * D:(i + 1) * D].rearrange("p (h d) -> p h d", h=H),
                                                        b_row[:, BV + n // 2, :].rearrange("p (h d) -> p h d", h=H),
                                                        ALU.add)
                            left(ins, ("v", n, half))

                    def maximum(n, v, qt):
                        i = (n * UNITS + v) * QT + qt
                        g = n * NG + v // HG
                        if n < 2 and v == 0 and qt == 0:
                            dve.wait_ge(mask_ready[n], 1)
                        dve.wait_ge(s_full, i + 1)
                        if v % HG == 0 and qt == 0 and g >= 2:
                            dve.wait_ge(m_full, JOB[("max", (g - 2) // NG, (g - 2) % NG)] + 1)
                        dst = Mx[:, g % 2, v % HG, qt:qt + 1]
                        b = bankS[i % NS][:, :]
                        if n < 2:
                            dve.tensor_tensor_reduce(b, b, mb[n][:, qt, :], 1.0, -3.0e38, ALU.add, ALU.max,
                                                     dst).then_inc(s_read, 1)
                        else:
                            dve.tensor_reduce(dst, b, AX.X, ALU.max).then_inc(s_read, 1)

                    def masked(n, u, j):
                        U = n * UNITS + u
                        e = U * HG + j
                        if u < QT and j == 0:
                            dve.wait_ge(mask_ready[n], 1 + u + 1)
                        if U >= NP_ and j == 0:
                            dve.wait_ge(av_done, U - NP_ + 1)
                        dve.wait_ge(t_full, e + 1)
                        dve.tensor_tensor(prob[:, U % NP_, j, :], bankT[e % NT][:, :], mb[n][:, QT + u % QT, :],
                                          ALU.add).then_inc(t_masked, 1)

                    def tiles(n, u, j):
                        if n < 2 and 0 <= u < UNITS:
                            masked(n, u, j)
                        if u + LEAD < UNITS:
                            maximum(n, u + LEAD, j)
                        if j == 1:
                            turned_jobs(n, u)

                    def turned_jobs(n, u):
                        g = max_group(u - 1)
                        if g is not None:
                            i = n * NG + g
                            m = bank_of(("max", n, g))
                            dve.tensor_scalar(neg[:, :], m[0:HG * QT, 0:P], -1.0, None,
                                              ALU.mult).then_inc(m_read["dve"], 1)
                            read_done(dve, ("max", n, g))
                            if i >= 2:
                                dve.wait_ge(rows_in[i % 2], 48 * (i // 2))
                            link(dve.tensor_copy(MR[:, i % 2, 0, :], neg[:, :]))
                            link(dve.tensor_tensor(neg[:, :], neg[:, :], MR[:, i % 2, 0, :], ALU.subtract))
                            link(dve.tensor_copy(MR[:, i % 2, 1, :], neg[:, :]))
                            dve.tensor_tensor(MR[:, i % 2, 2, :], neg[:, :], MR[:, i % 2, 1, :],
                                              ALU.subtract).then_inc(mr_ready, 1)
                        g = out_group(u - 1)
                        if g is not None:
                            m = bank_of(("oT", n, g))[:, :].rearrange("p (t h c) -> p t h c", t=QT, h=HG)
                            link(dve.reciprocal(rsum[:, g % 2, :, :], m[:, :, :, DEPTH]))
                            o = T1[n % 2][:, :, g * HG * DEPTH:(g + 1) * HG * DEPTH]
                            ins = dve.tensor_tensor(o.rearrange("p t (h c) -> p t h c", h=HG), m[:, :, :, 0:DEPTH],
                                                    rsum[:, g % 2, :, :].unsqueeze(3).broadcast_to([P, QT, HG, DEPTH]),
                                                    ALU.mult)
                            left(ins, ("oT", n, g))

                    def add(kind, at, src, dst, halves=(0, 1)):
                        for half in halves:
                            m = bank_of((kind, at, half))
                            left(dve.tensor_tensor(dst[:, 2 * half:2 * half + 2, :],
                                                   m[:, :].rearrange("p (t n) -> p t n", t=2),
                                                   src[:, 2 * half:2 * half + 2, :], ALU.add), (kind, at, half))
                        read_done(dve, (kind, at, half))

                    for kind, *at in ORDER:
                        p = at[0] % 2
                        if kind == "tiles":
                            tiles(*at)
                        elif kind == "stats":
                            statistics(*at)
                        elif kind == "apply":
                            if at == [0, 1]:
                                dve.wait_ge(late_in, 96)
                            normalise(*at)
                        elif kind == "cut":
                            cut(*at)
                        elif kind == "val":
                            take_values(*at)
                        elif kind == "add":
                            n, a = at[0], at[0] // 2
                            dve.wait_ge(res_ready[p], RES[(0, 1, 5)[a]])
                            if a == 2:
                                add("out", n, X[p], X[p])
                            else:
                                add("out", n, Hn[p], T1[p])
                        elif kind == "ffadd":
                            dve.wait_ge(res_ready[p], RES[2])
                            add("ff2", p, Hn[p], T1[p], (at[1],))
                        elif kind == "i8turned":
                            m = bank_of(("i8T", p))
                            left(dve.tensor_copy(xqT[p].rearrange("p k s -> p (k s)"), m[:, :].bitcast(BF16)),
                                 ("i8T", p))
                        elif kind == "i8add":
                            for half in range(2):
                                m = bank_of(("i8", p, half))
                                for i in range(2):
                                    t = 2 * half + i
                                    ins = dve.scalar_tensor_tensor(out=T1[p][:, t, :], in0=m[:, i * D:(i + 1) * D],
                                                                   scalar=xscale[p][:, t:t + 1], in1=b_row[:, I8S, :],
                                                                   op0=ALU.mult, op1=ALU.mult)
                                left(ins, ("i8", p, half))
                            read_done(dve, ("i8", p, 1))
                            dve.wait_ge(res_ready[p], RES[4])
                            link(dve.tensor_tensor(X[p][:, :, :], T1[p][:, :, :], X[p][:, :, :], ALU.add))
                        elif kind == "top":
                            m = bank_of(("logits", p))
                            left(dve.tensor_copy(lg[:, :, :].rearrange("p t e -> p (t e)"), m[:, 0:QT * NE]),
                                 ("logits", p))
                            read_done(dve, ("logits", p))
                            if p:
                                dve.wait_ge(gate_sem[0], 1)
                            for t in range(QT):
                                ins = dve.max(top[:, t, :], lg[:, t, :])
                            ins.then_inc(top_ready[p], 1)
                            dve.wait_ge(top_ready[p], 1)
                            for t in range(QT):
                                ins = dve.max_index(topi[:, t, :], top[:, t, :], lg[:, t, :])
                            link(ins)
                            link(dve.tensor_copy(route[p][:, :, 0:2], topi[:, :, 0:2]))
                            for t in range(QT):
                                for k in range(2):
                                    ins = dve.tensor_scalar(sel[p][:, k, t, :], iota_e[:, :], route[p][:, t, k:k + 1],
                                                            None, ALU.is_equal)
                            link(ins)
                            dve.tensor_tensor(both[p][:, :, :], sel[p][:, 0, :, :], sel[p][:, 1, :, :],
                                              ALU.add).then_inc(both_ready[p], 1)
                        elif kind == "route":
                            dve.wait_ge(gate_sem[p], 1)
                            link(dve.tensor_scalar(gate_e[p][:, :, :], gate_e[p][:, :, :], 1.0, None, ALU.add))
                            dve.reciprocal(route[p][:, :, 4:6], gate_e[p][:, :, :])
                            m = bank_of(("rank", p))[:, 0:(QT + 1) * NE].rearrange("p (t e) -> p t e", e=NE)
                            link(dve.tensor_tensor(ranks[:, :, :], m[:, 0:QT, :],
                                                   cnt[:, :].unsqueeze(1).broadcast_to([P, QT, NE]), ALU.add))
                            ins = dve.tensor_tensor(cnt[:, :], m[:, QT, :], cnt[:, :], ALU.add)
                            left(ins, ("rank", p))
                            read_done(dve, ("rank", p))
                            link(dve.tensor_tensor(sel[p][:, :, :, :], sel[p][:, :, :, :],
                                                   ranks[:, :, :].unsqueeze(1).broadcast_to([P, 2, QT, NE]), ALU.mult))
                            dve.tensor_reduce(route[p][:, :, 2:4].rearrange("p t k -> p k t"), sel[p][:, :, :, :], AX.X,
                                              ALU.add).then_inc(route_ready[p], 1)

            nc.all_engine_barrier()
            for s in every:
                nc.gpsimd.sem_clear(s)
            nc.all_engine_barrier()

    experts(nc, cnt, x_scr, t_scr, tT_scr, route_scr, disp, y_disp, gate_up, down, sgT, suT, sdT, out)


def experts(nc, cnt, x_scr, t_scr, tT_scr, route_scr, disp, y_disp, gate_up, down, sgT, suT, sdT, out):
    with ExitStack() as phase:
        def sb(name, shape, dt):
            return phase.enter_context(nc.sbuf_tensor(name, shape, dt))

        def sem(name):
            return phase.enter_context(nc.semaphore(name))

        acc = sb("acc", [P, TT, D], F32)
        w_gu = sb("w_gu", [P, NE, KD, 2 * EH], F32)
        w_dn = sb("w_dn", [P, NE, EH // P, D], F32)
        route = sb("route", [P, TT, 6], F32)
        slot = sb("slot", [P, TT, 2], U32)
        tile_expert = sb("tile_expert", [1, TILES], I32)
        bank = [phase.enter_context(nc.psum_tensor(f"ebank{i}", [P, 512], F32)) for i in range(8)]
        w_in = sem("w_in")

        with ExitStack() as step:
            def sb2(name, shape, dt):
                return step.enter_context(nc.sbuf_tensor(name, shape, dt))

            def sem2(name):
                return step.enter_context(nc.semaphore(name))

            t_all = sb2("t_all", [P, TT, D], F32)
            tT = sb2("tT", [P, KD, B * S], F32)
            s_gu = sb2("s_gu", [P, 2, KD, SH], F32)
            s_dn = sb2("s_dn", [P, SH // P, D], F32)
            sg = sb2("sg", [P, 2, S], F32)
            hid = sb2("hid", [P, 2, SH // P, S], F32)
            iota_e = sb2("iota_e2", [P, NE], F32)
            iota_t = sb2("iota_t", [P, TILES], F32)
            ones_e = sb2("ones_e", [P, NE], F32)
            ntile = sb2("ntile", [P, NE], F32)
            end = sb2("end", [P, NE], F32)
            start = sb2("start", [P, NE], F32)
            pick = sb2("pick", [P, TT, 2, NE], F32)
            slotf = sb2("slotf", [P, TT, 2], F32)
            past = sb2("past", [1, TILES, NE], F32)
            texp = sb2("texp", [1, TILES], F32)
            data_in = sem2("data_in")
            shared_in = sem2("shared_in")
            route_in = sem2("route_in")
            tokens_in = [sem2(f"tokens_in{b}") for b in range(B)]
            iota_ready = sem2("iota_ready")
            slot_ready = sem2("slot_ready")
            scattered = sem2("scattered")
            up_full = sem2("up_full")
            sg_done = sem2("sg_done")
            hid_done = sem2("hid_done")
            y_full = sem2("y_full")
            y_read = sem2("y_read")
            chain2 = sem2("chain2")
            with nc.Block() as block:
                @block.sync
                def _(sp):
                    def tokens_of(b):
                        sp.dma_start(tT[:, :, b * S:(b + 1) * S],
                                     tT_scr[b].rearrange("(k p) n -> p k n", p=P)).then_inc(tokens_in[b], 16)

                    tokens_of(0)
                    for i, w in enumerate((sgT, suT)):
                        sp.dma_start(s_gu[:, i, :, :], w.rearrange("(k p) n -> p k n", p=P)).then_inc(shared_in, 16)
                    sp.dma_start(s_dn[:, :, :], sdT.rearrange("(k p) n -> p k n", p=P)).then_inc(shared_in, 16)
                    sp.dma_start(route[:, :, :].rearrange("p (b t) c -> p b (t c)", b=B),
                                 route_scr.rearrange("b p n -> p b n")).then_inc(route_in, 16)
                    for b in range(1, B):
                        tokens_of(b)
                    sp.dma_start(t_all[:, :, :], t_scr.rearrange("b (t p) n -> p (b t) n", p=P)).then_inc(data_in, 16)
                    sp.dma_start(acc[:, :, :], x_scr.rearrange("b (t p) n -> p (b t) n", p=P)).then_inc(data_in, 16)

                @block.gpsimd
                def _(pool):
                    pool.iota(iota_e[:, :], [[1, NE]], base=0, channel_multiplier=0,
                              allow_small_or_imprecise_dtypes=True).then_inc(iota_ready, 1)
                    pool.iota(iota_t[:, :], [[1, TILES]], base=0, channel_multiplier=0,
                              allow_small_or_imprecise_dtypes=True).then_inc(iota_ready, 1)
                    pool.wait_ge(slot_ready, 1)
                    pool.wait_ge(data_in, 32)
                    for t in range(TT):
                        for k in range(2):
                            pool.indirect_dma_start(disp, bass.IndirectOffsetOnAxis(slot[:, t, k:k + 1], 0),
                                                    t_all[:, t, :], None).then_inc(scattered, 16)
                    pool.wait_ge(scattered, 32 * TT)

                @block.scalar
                def _(act):
                    act.wait_ge(tokens_in[B - 1], 16)
                    for n in range(B * SH // P):
                        if n < NE:
                            act.dma_start(w_gu[:, n, :, :], gate_up[n].rearrange("(k p) n -> p k n", p=P)).then_inc(w_in, 16)
                            act.dma_start(w_dn[:, n, :, :], down[n].rearrange("(k p) n -> p k n", p=P)).then_inc(w_in, 16)
                        act.wait_ge(up_full, n + 1)
                        if n >= 2:
                            act.wait_ge(hid_done, n - 1)
                        act.activation(sg[:, n % 2, :], bank[(n % 2) * 2][:, :], ACT.Silu).then_inc(sg_done, 1)

                @block.tensor
                def _(pe):
                    def down_products(c):
                        pe.wait_ge(hid_done, HT * (c + 1))
                        for t in range(QT):
                            n = c * QT + t
                            if n >= 4:
                                pe.wait_ge(y_read, n - 3)
                            for k in range(HT):
                                ins = pe.matmul(bank[4 + n % 4][:, 0:D], hid[:, c % 2, k, t * P:(t + 1) * P],
                                                s_dn[:, k, :], start=(k == 0), stop=(k == HT - 1))
                            ins.then_inc(y_full, 1)

                    pe.wait_ge(shared_in, 48)
                    for c in range(B):
                        pe.wait_ge(tokens_in[c], 16)
                        for m in range(HT):
                            n = c * HT + m
                            if n >= 2:
                                pe.wait_ge(hid_done, n - 1)
                            for i in range(2):
                                for k in range(KD):
                                    ins = pe.matmul(bank[(n % 2) * 2 + i][:, :], s_gu[:, i, k, m * P:(m + 1) * P],
                                                    tT[:, k, c * S:(c + 1) * S], start=(k == 0), stop=(k == KD - 1))
                            ins.then_inc(up_full, 1)
                            if c and m == 0:
                                down_products(c - 1)
                    down_products(B - 1)

                @block.vector
                def _(dve):
                    links = [0]

                    def link(ins):
                        links[0] += 1
                        ins.then_inc(chain2, 1)
                        dve.wait_ge(chain2, links[0])

                    link(dve.memset(ones_e[:, :], 1.0))
                    link(dve.tensor_scalar(ntile[:, :], cnt[:, :], 1.0 / P, (P - 1.0) / (2 * P), ALU.mult, ALU.add))
                    link(dve.tensor_scalar(ntile[:, :], ntile[:, :], MAGIC, None, ALU.add))
                    link(dve.tensor_scalar(ntile[:, :], ntile[:, :], -MAGIC, None, ALU.add))
                    link(dve.tensor_tensor_scan(end[:, :], ones_e[:, :], ntile[:, :], 0.0, ALU.mult, ALU.add))
                    link(dve.tensor_tensor(start[:, :], end[:, :], ntile[:, :], ALU.subtract))
                    dve.wait_ge(iota_ready, 2)
                    dve.wait_ge(route_in, 16)
                    wide = [P, TT * 2, NE]
                    flat = pick[:, :, :, :].rearrange("p t k e -> p (t k) e")
                    for k in range(2):
                        ins = dve.tensor_tensor(pick[:, :, k, :], iota_e[:, :].unsqueeze(1).broadcast_to([P, TT, NE]),
                                                route[:, :, k].unsqueeze(2).broadcast_to([P, TT, NE]), ALU.is_equal)
                    link(ins)
                    link(dve.tensor_tensor(flat, flat, start[:, :].unsqueeze(1).broadcast_to(wide), ALU.mult))
                    link(dve.tensor_reduce(slotf[:, :, :].rearrange("p t k -> p (t k)"), flat, AX.X, ALU.add))
                    link(dve.scalar_tensor_tensor(out=slotf[:, :, :], in0=slotf[:, :, :], scalar=float(P),
                                                  in1=route[:, :, 2:4], op0=ALU.mult, op1=ALU.add))
                    dve.tensor_copy(slot[:, :, :], slotf[:, :, :]).then_inc(slot_ready, 1)
                    link(dve.tensor_tensor(past[:, :, :], iota_t[0:1, :].unsqueeze(2).broadcast_to([1, TILES, NE]),
                                           end[0:1, :].unsqueeze(1).broadcast_to([1, TILES, NE]), ALU.is_ge))
                    link(dve.tensor_reduce(texp[:, :], past[:, :, :], AX.X, ALU.add))
                    link(dve.tensor_scalar(texp[:, :], texp[:, :], NE - 1.0, None, ALU.min))
                    link(dve.tensor_copy(tile_expert[:, :], texp[:, :]))
                    for c in range(B + 1):
                        for m in range(HT):
                            if c < B:
                                n = c * HT + m
                                dve.wait_ge(sg_done, n + 1)
                                dve.tensor_tensor(hid[:, c % 2, m, :], bank[(n % 2) * 2 + 1][:, :], sg[:, n % 2, :],
                                                  ALU.mult).then_inc(hid_done, 1)
                            if c and m == 0:
                                for t in range(QT):
                                    n = (c - 1) * QT + t
                                    dve.wait_ge(y_full, n + 1)
                                    if n == 0:
                                        dve.wait_ge(data_in, 32)
                                    dve.tensor_tensor(acc[:, n, :], bank[4 + n % 4][:, 0:D], acc[:, n, :],
                                                      ALU.add).then_inc(y_read, 1)

        with ExitStack() as step:
            def sb3(name, shape, dt):
                return step.enter_context(nc.sbuf_tensor(name, shape, dt))

            def sem3(name):
                s = step.enter_context(nc.semaphore(name))
                every.append(s)
                return s

            every = []
            NX = 8
            identf = sb3("identf2", [P, P], F32)
            ident_ready = step.enter_context(nc.semaphore("ident_ready"))
            xr = sb3("xr", [P, NX, D], F32)
            xT = sb3("xT", [P, 3, KD, P], F32)
            sgt = sb3("sgt", [P, 2, EH], F32)
            ht = sb3("ht", [P, 2, EH], F32)
            hTt = sb3("hTt", [P, 2, EH // P, P], F32)
            yt = sb3("yt", [P, 2, D], F32)
            rows_in = [sem3(f"rows_in_x{i}") for i in range(NX)]
            xT_full = sem3("xT_full")
            xT_read = sem3("xT_read")
            gu_full = sem3("gu_full")
            sg_ready = sem3("sg_ready")
            h_ready = sem3("h_ready")
            hT_full = sem3("hT_full")
            hT_read = sem3("hT_read")
            yt_full = sem3("yt_full")
            yt_read = sem3("yt_read")
            yt_out = [sem3(f"yt_out{i}") for i in range(2)]
            with nc.Block() as block:
                @block.gpsimd
                def _(pool):
                    pool.memset(identf[:, :], 0.0).then_inc(ident_ready, 1)
                    pool.wait_ge(ident_ready, 1)
                    pool.affine_select(out=identf[:, :], in_=identf[:, :], compare_op=ALU.not_equal, fill=1.0, base=0,
                                       pattern=[[-1, P]], channel_multiplier=1)

                @block.sync
                def _(sp):
                    sp.wait_ge(w_in, 32 * NE)

            x_t = disp.rearrange("(g t p) n -> g t p n", t=TSTEP, p=P)
            y_t = y_disp.rearrange("(g t p) n -> g t p n", t=TSTEP, p=P)
            with nc.Fori(0, TILES // TSTEP) as group:
                with nc.Block() as block:
                    @block.sync
                    def _(sp):
                        for s in range(TSTEP):
                            if s >= NX:
                                sp.wait_ge(xT_full, s - NX + 1)
                            sp.dma_start(xr[:, s % NX, :], x_t[group, s]).then_inc(rows_in[s % NX], 16)

                    @block.tensor
                    def _(pe):
                        def turn_rows(s):
                            pe.wait_ge(rows_in[s % NX], 16 * (s // NX + 1))
                            if s >= 2:
                                pe.wait_ge(xT_read, s - 1)
                            for k in range(KD):
                                ins = pe.transpose(bank[s % 2][:, k * P:(k + 1) * P], xr[:, s % NX, k * P:(k + 1) * P],
                                                   identf[:, :])
                            ins.then_inc(xT_full, 1)

                        def turn_hidden(s):
                            pe.wait_ge(h_ready, s + 1)
                            if s >= 2:
                                pe.wait_ge(hT_read, s - 1)
                            for k in range(EH // P):
                                ins = pe.transpose(bank[4 + s % 2][:, k * P:(k + 1) * P], ht[:, s % 2, k * P:(k + 1) * P],
                                                   identf[:, :])
                            ins.then_inc(hT_full, 1)

                        def down_product(s):
                            pe.wait_ge(hT_read, s + 1)
                            if s >= 2:
                                pe.wait_ge(yt_read, s - 1)
                            for k in range(EH // P):
                                ins = pe.matmul(bank[6 + s % 2][:, 0:D], hTt[:, s % 2, k, :],
                                                w_dn[:, bass.ds(expert[s], 1), k, :].rearrange("p a n -> p (a n)"),
                                                start=(k == 0), stop=(k == EH // P - 1))
                            ins.then_inc(yt_full, 1)

                        expert = []
                        turn_rows(0)
                        turn_rows(1)
                        for s in range(TSTEP + 2):
                            if s < TSTEP:
                                expert.append(pe.value_load(tile_expert[0:1, bass.ds(group * TSTEP + s, 1)],
                                                            min_val=0, max_val=NE - 1))
                                pe.wait_ge(xT_read, s + 1)
                                if s >= 2:
                                    pe.wait_ge(h_ready, s - 1)
                                for k in range(KD):
                                    ins = pe.matmul(bank[2 + s % 2][:, :], xT[:, s % 3, k, :],
                                                    w_gu[:, bass.ds(expert[s], 1), k, :].rearrange("p a n -> p (a n)"),
                                                    start=(k == 0), stop=(k == KD - 1))
                                ins.then_inc(gu_full, 1)
                            if s + 2 < TSTEP:
                                turn_rows(s + 2)
                            if 0 <= s - 1 < TSTEP:
                                turn_hidden(s - 1)
                            if s >= 2:
                                down_product(s - 2)

                    @block.scalar
                    def _(act):
                        for s in range(TSTEP + 2):
                            if s < TSTEP:
                                act.wait_ge(gu_full, s + 1)
                                if s >= 2:
                                    act.wait_ge(h_ready, s - 1)
                                act.activation(sgt[:, s % 2, :], bank[2 + s % 2][:, 0:EH], ACT.Silu).then_inc(sg_ready, 1)
                            if s >= 2:
                                n = s - 2
                                act.wait_ge(yt_full, n + 1)
                                if n >= 2:
                                    act.wait_ge(yt_out[n % 2], 16 * (n // 2))
                                act.activation(yt[:, n % 2, :], bank[6 + n % 2][:, 0:D], ACT.Copy).then_inc(yt_read, 1)
                                act.wait_ge(yt_read, n + 1)
                                act.dma_start(y_t[group, n], yt[:, n % 2, :]).then_inc(yt_out[n % 2], 16)
                        for i in range(2):
                            act.wait_ge(yt_out[i], 16 * (TSTEP // 2))

                    @block.vector
                    def _(dve):
                        def read_rows(s):
                            dve.wait_ge(xT_full, s + 1)
                            if s >= 3:
                                dve.wait_ge(gu_full, s - 2)
                            dve.tensor_copy(xT[:, s % 3, :, :].rearrange("p k n -> p (k n)"),
                                            bank[s % 2][:, 0:D]).then_inc(xT_read, 1)

                        read_rows(0)
                        read_rows(1)
                        for s in range(TSTEP):
                            dve.wait_ge(sg_ready, s + 1)
                            if s >= 2:
                                dve.wait_ge(hT_full, s - 1)
                            dve.tensor_tensor(ht[:, s % 2, :], bank[2 + s % 2][:, EH:2 * EH], sgt[:, s % 2, :],
                                              ALU.mult).then_inc(h_ready, 1)
                            if s + 2 < TSTEP:
                                read_rows(s + 2)
                            dve.wait_ge(hT_full, s + 1)
                            if s >= 2:
                                dve.wait_ge(yt_full, s - 1)
                            dve.tensor_copy(hTt[:, s % 2, :, :].rearrange("p k n -> p (k n)"),
                                            bank[4 + s % 2][:, 0:EH]).then_inc(hT_read, 1)
                nc.all_engine_barrier()
                for s in every:
                    nc.gpsimd.sem_clear(s)
                nc.all_engine_barrier()

        with ExitStack() as step:
            NR = 4
            got = step.enter_context(nc.sbuf_tensor("got", [P, NR, 2, D], F32))
            got_in = [step.enter_context(nc.semaphore(f"got_in{i}")) for i in range(NR)]
            first = step.enter_context(nc.semaphore("first"))
            added = step.enter_context(nc.semaphore("added"))
            stored = step.enter_context(nc.semaphore("stored"))
            with nc.Block() as block:
                @block.gpsimd
                def _(pool):
                    for t in range(TT):
                        if t >= NR:
                            pool.wait_ge(added, t - NR + 1)
                        for k in range(2):
                            pool.indirect_dma_start(got[:, t % NR, k, :], None, y_disp,
                                                    bass.IndirectOffsetOnAxis(slot[:, t, k:k + 1], 0))\
                                .then_inc(got_in[t % NR], 16)

                @block.vector
                def _(dve):
                    for t in range(TT):
                        dve.wait_ge(got_in[t % NR], 32 * (t // NR + 1))
                        for k, s in enumerate((first, added)):
                            dve.scalar_tensor_tensor(out=acc[:, t, :], in0=got[:, t % NR, k, :],
                                                     scalar=route[:, t, 4 + k:5 + k], in1=acc[:, t, :],
                                                     op0=ALU.mult, op1=ALU.add).then_inc(s, 1)
                            if k == 0:
                                dve.wait_ge(first, t + 1)

                @block.sync
                def _(sp):
                    o = out.rearrange("b (t p) n -> (b t) p n", p=P)
                    for t in range(0, TT, 2):
                        sp.wait_ge(added, t + 2)
                        sp.dma_start(o[t:t + 2].rearrange("t p n -> p t n"), acc[:, t:t + 2, :]).then_inc(stored, 16)
                    sp.wait_ge(stored, 8 * TT)


def kernel(**inputs):
    import numpy as np
    import concourse.bacc as bacc
    from concourse.bass_utils import run_bass_kernel_spmd as run

    t = {k: np.asarray(v) for k, v in inputs.items()}
    L0, L1 = "L0_xattn_", "L1_xattn_"

    def chunks(w):
        return w.reshape(-1, P, w.shape[1]).transpose(1, 0, 2)

    qkv = [[t[L0 + f"w{c}{n}"] for c in "qkv"] for n in (1, 2)] + [[t[L1 + f"w{c}_w"].T for c in "qkv"]]
    wqkv = np.concatenate([chunks(w) for ws in qkv for w in ws], axis=1)
    wo = np.concatenate([chunks(w) for w in (t[L0 + "wo1"], t[L0 + "wo2"], t[L1 + "dense_w"].T)], axis=1)
    bqk = np.concatenate([t[n].reshape(KD, P).T for n in (
        L0 + "bq1", L0 + "bk1", L0 + "bq2", L0 + "bk2", L1 + "wq_b", L1 + "wk_b")], axis=1)
    brow = np.stack([t[n] for n in (
        L0 + "bv1", L0 + "bv2", L1 + "wv_b", L0 + "bo1", L0 + "bo2", L1 + "dense_b", L0 + "b_ff2",
        L0 + "g1", L0 + "g2", L0 + "g3", L0 + "be1", L0 + "be2", L0 + "be3",
        "L0_ffn_weight_scale", "L0_ffn_bias")])
    pm = t["mask_Bx1x1xS_ff1"].reshape(B, S)
    arrays = {
        "x": t["x"], "ctxT": t["ctx_1024"].transpose(0, 2, 1),
        "am": t["mask_1x1xSxS_fk0"].reshape(S, S), "amT": t["mask_1x1xSxS_fk0"].reshape(S, S).T,
        "pmrow": pm, "pmcol": pm.reshape(B, QT, P).transpose(0, 2, 1),
        "wqkv": wqkv, "wo": wo, "bqk": bqk, "brow": brow, "bff1": t[L0 + "b_ff1"].reshape(FT, P).T,
        "wff1": t[L0 + "w_ff1"], "wff2": t[L0 + "w_ff2"], "wi8": np.ascontiguousarray(t["L0_ffn_weight_q"].T).view(np.int32),
        "routerT": t["L1_ffn_router_w"].T, "gate_up": t["L1_ffn_gate_up_w"], "down": t["L1_ffn_down_w"],
        "sgT": t["L1_ffn_shared_gate_w"].T, "suT": t["L1_ffn_shared_up_w"].T, "sdT": t["L1_ffn_shared_down_w"].T,
    }
    arrays = {f"in_{k}": np.ascontiguousarray(v) for k, v in arrays.items()}
    nc = bacc.Bacc("TRN2", target_bir_lowering=False, num_devices=1)
    args = [nc.dram_tensor(k, a.shape, mybir.dt.from_np(a.dtype), kind="ExternalInput").ap()
            for k, a in arrays.items()]
    args.append(nc.dram_tensor("out_0", (B, S, D), F32, kind="ExternalOutput").ap())
    build(nc, *args)
    return run(nc, [arrays], core_ids=[0]).results[0]["out_0"]
```
